# Optimizing a Trainium2 kernel written in Bass

```python
import numpy as np
import jax
import jax.numpy as jnp

def _softmax(x, axis=-1):
    return jax.nn.softmax(x, axis=axis)

def _gelu(x):
    return jax.nn.gelu(x, approximate=True)

def _silu(x):
    return jax.nn.silu(x)

def _sigmoid(x):
    return jax.nn.sigmoid(x)

def _layernorm(x, axis=-1, eps=1e-05):
    m = jnp.mean(x, axis=axis, keepdims=True)
    v = jnp.var(x, axis=axis, keepdims=True)
    return (x - m) / jnp.sqrt(v + eps)

def _scatter_add(tgt, idx, src, axis=0):
    return tgt.at[idx].add(src)

def _segment_sum(src, seg, n):
    return jax.ops.segment_sum(src, seg, n)
kernel_name = 'mk_flamingo_gated_d2_seqx_r4_4e3759'

def setup_inputs(seed: int=0):
    np.random.seed(seed)
    _w = jnp.asarray

    def _rec_inputs():
        import jax
        import jax.numpy as jnp
        _rk = jax.random.key(seed)
        x = -7.109e-05 + 0.9999 * jax.random.normal(jax.random.fold_in(_rk, 1), (4, 512, 512), jnp.float32)
        _lenS = 512 - jax.random.randint(jax.random.fold_in(_rk, 7), (4,), 0, max(1, 512 // 4) + 1, jnp.int32)
        _lenS2 = 512 - jax.random.randint(jax.random.fold_in(_rk, 8), (4,), 0, max(1, 512 // 4) + 1, jnp.int32)
        _ctx_2048P = jax.random.normal(jax.random.fold_in(_rk, 11), (4, 16, 512), jnp.float32)
        _ctx_2048c = jax.random.dirichlet(jax.random.fold_in(_rk, 511), 0.3 * jnp.ones((16,), jnp.float32), (4, 512))
        _ctx_2048t = jnp.einsum('bsk,bkd->bsd', _ctx_2048c, _ctx_2048P)
        _ctx_2048t = _ctx_2048t * jax.lax.rsqrt(jnp.mean(jnp.square(_ctx_2048t)) + 1e-12) * 0.953939
        ctx_2048 = -3.05549e-07 + 0.0199987 * (_ctx_2048t + 0.3 * jax.random.normal(jax.random.fold_in(_rk, 611), (4, 512, 512), jnp.float32))
        _g = jax.random.normal(jax.random.fold_in(_rk, 9001), (2, 2), jnp.float32)
        _g = jnp.sign(_g) * jnp.maximum(jnp.abs(_g), 1.0) + (_g == 0) * 1.0
        g_xattn = _g[0]
        g_ffn = _g[1]
        return (x, ctx_2048, g_xattn, g_ffn)
    x, ctx_2048, g_xattn, g_ffn = _rec_inputs()

    def _L0_xattn_setup():
        import jax, jax.numpy as jnp
        import numpy as np
        FP8_MAX = 448.0
        ACT_EPS = 0.0001
        W_EPS = 1e-06
        BLK = 128

        def quant_dequant_act_1x128(x):
            E, M, K = x.shape
            xb = x.reshape(E, M, K // BLK, BLK)
            amax = jnp.max(jnp.abs(xb), axis=-1, keepdims=True)
            safe = jnp.maximum(amax, ACT_EPS)
            q = (xb * (FP8_MAX / safe)).astype(jnp.float8_e4m3fn)
            return (q.astype(jnp.float32) * (safe / FP8_MAX)).reshape(E, M, K)

        def quant_dequant_weight_128x128(w):
            E, N, K = w.shape
            wb = w.reshape(E, N // BLK, BLK, K // BLK, BLK)
            amax = jnp.max(jnp.abs(wb), axis=(2, 4), keepdims=True)
            safe = jnp.maximum(amax, W_EPS)
            q = (wb * (FP8_MAX / safe)).astype(jnp.float8_e4m3fn)
            return (q.astype(jnp.float32) * (safe / FP8_MAX)).reshape(E, N, K)
        key = jax.random.key(seed)
        kx, kw = jax.random.split(key)
        E, M, K, N = (8, 1024, 512, 512)
        x = jax.random.normal(kx, (E, M, K), dtype=jnp.float32)
        weight = jax.random.normal(kw, (E, N, K), dtype=jnp.float32) * 0.02
        return {'x': x, 'weight': weight}
    _L0_xattn_all = _L0_xattn_setup()
    _L0_xattn_in = {k: v for k, v in _L0_xattn_all.items() if k in ()}
    del _L0_xattn_all

    def _L0_ffn_setup():
        import jax, jax.numpy as jnp
        import numpy as np
        D_MODEL = 512
        D_FF = 2048

        def absmean_quant(w):
            scale = jnp.mean(jnp.abs(w))
            mask = (jnp.abs(w) >= scale * 0.7).astype(w.dtype)
            return jnp.sign(w) * mask
        key = jax.random.key(seed)
        k_x, k_w1, k_w2 = jax.random.split(key, 3)
        x = jax.random.normal(k_x, (4, 1024, D_MODEL), dtype=jnp.float32)
        w1 = jax.random.normal(k_w1, (D_FF, D_MODEL), dtype=jnp.float32)
        b1 = jnp.zeros((D_FF,), dtype=jnp.float32)
        w2 = jax.random.normal(k_w2, (D_MODEL, D_FF), dtype=jnp.float32)
        b2 = jnp.zeros((D_MODEL,), dtype=jnp.float32)
        return {'x': x, 'w1': w1, 'b1': b1, 'w2': w2, 'b2': b2}
    _L0_ffn_all = _L0_ffn_setup()
    _L0_ffn_in = {k: v for k, v in _L0_ffn_all.items() if k in ('w1', 'b1', 'w2', 'b2')}
    del _L0_ffn_all

    def _L1_xattn_setup():
        import jax, jax.numpy as jnp
        import numpy as np
        HIDDEN = 512
        N_HEADS = 16
        N_KV_HEADS = 4
        HEAD_DIM = 128
        EPS = 1e-06

        def rms_norm(x, w, eps=EPS):
            xf = x.astype(jnp.float32)
            var = jnp.mean(xf * xf, axis=-1, keepdims=True)
            return w * (xf * jax.lax.rsqrt(var + eps)).astype(x.dtype)
        key = jax.random.key(seed)
        ks = jax.random.split(key, 8)
        B, S, S_ENC = (4, 512, 256)
        inner = N_HEADS * HEAD_DIM
        kv_dim = N_KV_HEADS * HEAD_DIM
        s = 0.02
        return {'hidden_states': jax.random.normal(ks[0], (B, S, HIDDEN), jnp.float32), 'encoder_hidden_states': jax.random.normal(ks[1], (B, S_ENC, HIDDEN), jnp.float32), 'Wq': jax.random.normal(ks[2], (HIDDEN, inner), jnp.float32) * s, 'Wk': jax.random.normal(ks[3], (HIDDEN, kv_dim), jnp.float32) * s, 'Wv': jax.random.normal(ks[4], (HIDDEN, kv_dim), jnp.float32) * s, 'Wo': jax.random.normal(ks[5], (inner, HIDDEN), jnp.float32) * s, 'q_norm_w': jnp.ones((HEAD_DIM,), jnp.float32), 'k_norm_w': jnp.ones((HEAD_DIM,), jnp.float32)}
    _L1_xattn_all = _L1_xattn_setup()
    _L1_xattn_in = {k: v for k, v in _L1_xattn_all.items() if k in ('Wq', 'Wk', 'Wv', 'Wo', 'q_norm_w', 'k_norm_w')}
    del _L1_xattn_all

    def _L1_ffn_setup():
        import jax, jax.numpy as jnp
        import numpy as np
        TOP_K = 2
        SCALING = 2.0
        key = jax.random.key(seed)
        ks = jax.random.split(key, 10)
        B, S, H, I, E, R = (1, 128, 512, 256, 8, 16)
        w = 1.0 / np.sqrt(H)
        inp = {'x': jax.random.normal(ks[0], (B, S, H), jnp.float32), 'gate_weight': jax.random.normal(ks[1], (E, H), jnp.float32) * w, 'gate_lora_A': jax.random.normal(ks[2], (R, H), jnp.float32) * 0.02, 'gate_lora_B': jax.random.normal(ks[3], (E, R), jnp.float32) * 0.02, 'gate_up_proj': jax.random.normal(ks[4], (E, H, 2 * I), jnp.float32) * w, 'down_proj': jax.random.normal(ks[5], (E, I, H), jnp.float32) * (1.0 / np.sqrt(I)), 'gup_lora_A': jax.random.normal(ks[6], (E, R, H), jnp.float32) * 0.02, 'gup_lora_B': jax.random.normal(ks[7], (E, 2 * I, R), jnp.float32) * 0.02, 'down_lora_A': jax.random.normal(ks[8], (E, R, I), jnp.float32) * 0.02, 'down_lora_B': jax.random.normal(ks[9], (E, H, R), jnp.float32) * 0.02}
        return inp
    _L1_ffn_all = _L1_ffn_setup()
    _L1_ffn_in = {k: v for k, v in _L1_ffn_all.items() if k in ('gate_weight', 'gate_lora_A', 'gate_lora_B', 'gate_up_proj', 'down_proj', 'gup_lora_A', 'gup_lora_B', 'down_lora_A', 'down_lora_B')}
    del _L1_ffn_all
    return {'x': x, 'ctx_2048': ctx_2048, 'g_xattn': g_xattn, 'g_ffn': g_ffn, 'L0_ffn_w1': _L0_ffn_in['w1'], 'L0_ffn_b1': _L0_ffn_in['b1'], 'L0_ffn_w2': _L0_ffn_in['w2'], 'L0_ffn_b2': _L0_ffn_in['b2'], 'L1_xattn_Wq': _L1_xattn_in['Wq'], 'L1_xattn_Wk': _L1_xattn_in['Wk'], 'L1_xattn_Wv': _L1_xattn_in['Wv'], 'L1_xattn_Wo': _L1_xattn_in['Wo'], 'L1_xattn_q_norm_w': _L1_xattn_in['q_norm_w'], 'L1_xattn_k_norm_w': _L1_xattn_in['k_norm_w'], 'L1_ffn_gate_weight': _L1_ffn_in['gate_weight'], 'L1_ffn_gate_lora_A': _L1_ffn_in['gate_lora_A'], 'L1_ffn_gate_lora_B': _L1_ffn_in['gate_lora_B'], 'L1_ffn_gate_up_proj': _L1_ffn_in['gate_up_proj'], 'L1_ffn_down_proj': _L1_ffn_in['down_proj'], 'L1_ffn_gup_lora_A': _L1_ffn_in['gup_lora_A'], 'L1_ffn_gup_lora_B': _L1_ffn_in['gup_lora_B'], 'L1_ffn_down_lora_A': _L1_ffn_in['down_lora_A'], 'L1_ffn_down_lora_B': _L1_ffn_in['down_lora_B']}

def reference(x, ctx_2048, g_xattn, g_ffn, L0_ffn_w1, L0_ffn_b1, L0_ffn_w2, L0_ffn_b2, L1_xattn_Wq, L1_xattn_Wk, L1_xattn_Wv, L1_xattn_Wo, L1_xattn_q_norm_w, L1_xattn_k_norm_w, L1_ffn_gate_weight, L1_ffn_gate_lora_A, L1_ffn_gate_lora_B, L1_ffn_gate_up_proj, L1_ffn_down_proj, L1_ffn_gup_lora_A, L1_ffn_gup_lora_B, L1_ffn_down_lora_A, L1_ffn_down_lora_B):
    import jax
    import jax.numpy as jnp

    def _L0_xattn_ref(x, weight):
        import jax, jax.numpy as jnp
        import numpy as np
        FP8_MAX = 448.0
        ACT_EPS = 0.0001
        W_EPS = 1e-06
        BLK = 128

        def quant_dequant_act_1x128(x):
            E, M, K = x.shape
            xb = x.reshape(E, M, K // BLK, BLK)
            amax = jnp.max(jnp.abs(xb), axis=-1, keepdims=True)
            safe = jnp.maximum(amax, ACT_EPS)
            q = (xb * (FP8_MAX / safe)).astype(jnp.float8_e4m3fn)
            return (q.astype(jnp.float32) * (safe / FP8_MAX)).reshape(E, M, K)

        def quant_dequant_weight_128x128(w):
            E, N, K = w.shape
            wb = w.reshape(E, N // BLK, BLK, K // BLK, BLK)
            amax = jnp.max(jnp.abs(wb), axis=(2, 4), keepdims=True)
            safe = jnp.maximum(amax, W_EPS)
            q = (wb * (FP8_MAX / safe)).astype(jnp.float8_e4m3fn)
            return (q.astype(jnp.float32) * (safe / FP8_MAX)).reshape(E, N, K)
        xq = quant_dequant_act_1x128(x)
        wq = quant_dequant_weight_128x128(weight)
        return jnp.einsum('emk,enk->emn', xq, wq)

    def _L0_ffn_ref(x, w1, b1, w2, b2):
        import jax, jax.numpy as jnp
        import numpy as np
        D_MODEL = 512
        D_FF = 2048

        def absmean_quant(w):
            scale = jnp.mean(jnp.abs(w))
            mask = (jnp.abs(w) >= scale * 0.7).astype(w.dtype)
            return jnp.sign(w) * mask
        w1_q = absmean_quant(w1)
        w2_q = absmean_quant(w2)
        h = jnp.einsum('bsd,fd->bsf', x, w1_q) + b1
        h = jax.nn.gelu(h, approximate=False)
        out = jnp.einsum('bsf,df->bsd', h, w2_q) + b2
        return out

    def _L1_xattn_ref(hidden_states, encoder_hidden_states, Wq, Wk, Wv, Wo, q_norm_w, k_norm_w):
        import jax, jax.numpy as jnp
        import numpy as np
        HIDDEN = 512
        N_HEADS = 16
        N_KV_HEADS = 4
        HEAD_DIM = 128
        EPS = 1e-06

        def rms_norm(x, w, eps=EPS):
            xf = x.astype(jnp.float32)
            var = jnp.mean(xf * xf, axis=-1, keepdims=True)
            return w * (xf * jax.lax.rsqrt(var + eps)).astype(x.dtype)
        B, S, _ = hidden_states.shape
        S_enc = encoder_hidden_states.shape[1]
        groups = N_HEADS // N_KV_HEADS
        scale = 1.0 / HEAD_DIM ** 0.5
        q = (hidden_states @ Wq).reshape(B, S, N_HEADS, HEAD_DIM)
        k = (encoder_hidden_states @ Wk).reshape(B, S_enc, N_KV_HEADS, HEAD_DIM)
        v = (encoder_hidden_states @ Wv).reshape(B, S_enc, N_KV_HEADS, HEAD_DIM)
        q = rms_norm(q, q_norm_w)
        k = rms_norm(k, k_norm_w)
        k = jnp.repeat(k, groups, axis=2)
        v = jnp.repeat(v, groups, axis=2)
        scores = jnp.einsum('bqhd,bkhd->bhqk', q, k) * scale
        probs = jax.nn.softmax(scores, axis=-1)
        out = jnp.einsum('bhqk,bkhd->bqhd', probs, v)
        out = out.reshape(B, S, N_HEADS * HEAD_DIM)
        return out @ Wo

    def _L1_ffn_ref(x, gate_weight, gate_lora_A, gate_lora_B, gate_up_proj, down_proj, gup_lora_A, gup_lora_B, down_lora_A, down_lora_B):
        import jax, jax.numpy as jnp
        import numpy as np
        TOP_K = 2
        SCALING = 2.0
        B, S, H = x.shape
        xf = x.reshape(-1, H)
        gate_delta = SCALING * (gate_lora_B @ gate_lora_A)
        router_logits = xf @ gate_weight.T + xf @ gate_delta.T
        probs = jax.nn.softmax(router_logits.astype(jnp.float32), axis=-1)
        routing_weights, selected = jax.lax.top_k(probs, TOP_K)
        routing_weights = routing_weights / routing_weights.sum(-1, keepdims=True)
        routing_weights = routing_weights.astype(xf.dtype)
        gup = jnp.einsum('th,eho->teo', xf, gate_up_proj)
        gup = gup + SCALING * jnp.einsum('ter,eor->teo', jnp.einsum('th,erh->ter', xf, gup_lora_A), gup_lora_B)
        gates, h = jnp.split(gup, 2, axis=-1)
        h = jax.nn.silu(gates) * h
        out = jnp.einsum('tei,eih->teh', h, down_proj)
        out = out + SCALING * jnp.einsum('ter,ehr->teh', jnp.einsum('tei,eri->ter', h, down_lora_A), down_lora_B)
        out_sel = jnp.take_along_axis(out, selected[:, :, None], axis=1)
        y = jnp.einsum('tkh,tk->th', out_sel, routing_weights)
        return y.reshape(B, S, H)
    x = x + jnp.tanh(g_xattn[0]) * _L0_xattn_ref(_layernorm(x, axis=-1), ctx_2048)
    x = x + jnp.tanh(g_ffn[0]) * _L0_ffn_ref(_layernorm(x, axis=-1), L0_ffn_w1, L0_ffn_b1, L0_ffn_w2, L0_ffn_b2)
    x = x + jnp.tanh(g_xattn[1]) * _L1_xattn_ref(_layernorm(x, axis=-1), ctx_2048, L1_xattn_Wq, L1_xattn_Wk, L1_xattn_Wv, L1_xattn_Wo, L1_xattn_q_norm_w, L1_xattn_k_norm_w)
    x = x + jnp.tanh(g_ffn[1]) * _L1_ffn_ref(_layernorm(x, axis=-1), L1_ffn_gate_weight, L1_ffn_gate_lora_A, L1_ffn_gate_lora_B, L1_ffn_gate_up_proj, L1_ffn_down_proj, L1_ffn_gup_lora_A, L1_ffn_gup_lora_B, L1_ffn_down_lora_A, L1_ffn_down_lora_B)
    return x

_drawn_inputs = setup_inputs


def setup_inputs(seed=0):
    import zlib

    import numpy as np

    out = dict(_drawn_inputs(seed))
    spreads = {'g_ffn': (-1.0, 0.6),
     'L0_ffn_b1': (0.0, 0.8),
     'L0_ffn_b2': (0.0, 2.0),
     'L1_xattn_q_norm_w': (1.0, 0.6),
     'L1_xattn_k_norm_w': (1.0, 0.6)}
    factors = {'L1_xattn_Wq': 64.0,
     'L1_xattn_Wk': 64.0,
     'L1_xattn_Wv': 64.0,
     'L1_xattn_Wo': 64.0,
     'L1_ffn_gate_weight': 8.0,
     'L1_ffn_gate_lora_A': 8.0,
     'L1_ffn_gate_lora_B': 8.0,
     'L1_ffn_gate_up_proj': 8.0,
     'L1_ffn_down_proj': 8.0,
     'L1_ffn_gup_lora_A': 8.0,
     'L1_ffn_gup_lora_B': 8.0,
     'L1_ffn_down_lora_A': 8.0,
     'L1_ffn_down_lora_B': 8.0}
    for name, (base, spread) in spreads.items():
        noise = np.random.default_rng([zlib.crc32(name.encode()), seed]).standard_normal(out[name].shape)
        drawn = base * np.exp(spread * noise) if base else spread * noise
        out[name] = jnp.asarray(drawn.astype(out[name].dtype))
    for name, factor in factors.items():
        out[name] = (out[name] * factor).astype(out[name].dtype)
    return out
```

```python
from contextlib import ExitStack

import concourse.bass as bass
from concourse import mybir

F32 = mybir.dt.float32
F32R = mybir.dt.float32r
U32 = mybir.dt.uint32
ALU = mybir.AluOpType
ACT = mybir.ActivationFunctionType
AX = mybir.AxisListType

P = 128
B, S, D = 4, 512, 512
KT = D // P
TT = S // P
T = B * TT
F = 2048
FT = F // P
NH, G, DH = 16, 4, 128
HG = NH // G
E, I, R = 8, 256, 16
LN_EPS, RMS_EPS = 1e-5, 1e-6
FP8_MAX = 448.0
ACT_EPS, W_EPS = 1e-4, 1e-6
EXPONENT = 0x7F800000
FP8_LEAST = 2.0 ** -6
FP8_SHIFT = 1.5 * 2.0 ** 20


class Signal:

    def __init__(self, K, name, per=1, credit=0, unit=1):
        self.sem = K.ctx.enter_context(K.nc.semaphore(name))
        self.per, self.credit, self.unit = per, credit, unit
        self.opening = credit * unit

    def at(self, n, i=0):
        assert self.credit + n >= 0
        return i * (self.per * self.unit) + (self.credit + n + 1) * self.unit


class Count:

    def __init__(self, signal, i=0):
        self.sem, self.signals, self.i, self.n = signal.sem, signal, i, 0

    def next(self):
        self.n += 1
        return self.signals.at(self.n - 1, self.i)


class Kernel:

    def __init__(self, nc, ctx):
        self.nc, self.ctx = nc, ctx

    def scope(self, ctx):
        nc = self.nc

        def sb(name, shape, dt=F32):
            return ctx.enter_context(nc.sbuf_tensor(name, shape, dt))

        def ps(name, shape=(P, 512)):
            return ctx.enter_context(nc.psum_tensor(name, list(shape), F32))

        return sb, ps


def three_pass(pe, out, lhs_hi, lhs_lo, rhs_hi, rhs_lo, start, stop):
    pe.matmul(out, lhs_hi, rhs_hi, start=start, stop=False)
    pe.matmul(out, lhs_hi, rhs_lo, start=False, stop=False)
    return pe.matmul(out, lhs_lo, rhs_hi, start=False, stop=stop)


def f32(ap):
    return ap.bitcast(F32)


def layer_norm_stats(dve, x, stats, mv, step, apart):
    for t in range(TT):
        ins = dve.bn_stats(stats[:, t, :], x[:, t, :])
    ins.then_inc(step.sem, 1)
    dve.wait_ge(step.sem, step.next())
    dve.sem_inc(apart, 1)
    for t in range(TT):
        ins = dve.bn_aggr(mv[:, t, :], stats[:, t, :])
    return ins


def quantise(dve, step, v, scale, least, grid, out_scale, safe, amax):
    dve.tensor_scalar(safe, amax, least, None, ALU.max).then_inc(step.sem, 1)
    dve.wait_ge(step.sem, step.next())
    dve.reciprocal(scale, safe).then_inc(step.sem, 1)
    dve.wait_ge(step.sem, step.next())
    dve.tensor_scalar(scale, scale, FP8_MAX, None, ALU.mult).then_inc(step.sem, 1)
    dve.wait_ge(step.sem, step.next())
    dve.tensor_scalar(out_scale, safe, 1.0 / FP8_MAX, None, ALU.mult)
    n = v.shape[1]
    dve.tensor_tensor(v, v, scale.unsqueeze(2).to_broadcast([P, n, P]), ALU.mult).then_inc(step.sem, 1)
    dve.wait_ge(step.sem, step.next())
    dve.tensor_scalar(grid.bitcast(U32), v.bitcast(U32), EXPONENT, None, ALU.bitwise_and).then_inc(step.sem, 1)
    dve.wait_ge(step.sem, step.next())
    dve.tensor_scalar(grid, grid, FP8_LEAST, FP8_SHIFT, ALU.max, ALU.mult).then_inc(step.sem, 1)
    dve.wait_ge(step.sem, step.next())
    dve.tensor_tensor(v, v, grid, ALU.add).then_inc(step.sem, 1)
    dve.wait_ge(step.sem, step.next())
    dve.tensor_tensor(v, v, grid, ALU.subtract).then_inc(step.sem, 1)
    dve.wait_ge(step.sem, step.next())
    return dve.tensor_tensor(v, v, out_scale.unsqueeze(2).to_broadcast([P, n, P]), ALU.mult)


def stage_context(K, x, ctx_t, wk, wv, k_norm_w, g_xattn, g_ffn, keys, values):
    nc = K.nc
    with ExitStack() as ctx:
        sb, ps = K.scope(ctx)
        w_raw = sb("c_w_raw", [P, KT, D])
        wk_hi, wk_lo = sb("wk_hi", [P, KT, D], F32R), sb("wk_lo", [P, KT, D], F32R)
        wv_hi, wv_lo = sb("wv_hi", [P, KT, D], F32R), sb("wv_lo", [P, KT, D], F32R)
        c_raw = sb("c_raw", [P, KT, S])
        c_hi, c_lo = sb("c_hi", [P, KT, S], F32R), sb("c_lo", [P, KT, S], F32R)
        cq_hi, cq_lo = sb("cq_hi", [P, KT, S], F32R), sb("cq_lo", [P, KT, S], F32R)
        grid = sb("grid", [P, KT * 4, P])
        xn = sb("c_xn", [P, TT, D])
        xq_hi, xq_lo = sb("xq_hi", [P, KT, S], F32R), sb("xq_lo", [P, KT, S], F32R)
        k_out = sb("k_out", [P, 2, G, S], F32R)
        v_out = sb("v_out", [P, 2, TT, G * DH], F32R)
        v_full = sb("v_full", [P, 2, G * DH])
        k_sq = sb("k_sq", [P, 2, G * DH])
        k_ms = sb("k_ms", [P, 2, G])
        k_eps = sb("k_eps", [P, 2, G])
        k_rstd = sb("k_rstd", [P, 2, G])
        k_nrm = sb("k_nrm", [P, 2, G * DH])
        k_full = sb("k_full", [P, 2, G * P])
        kw = sb("kw", [P, 1])
        blocks = [sb(f"q_{n}", [P, KT * 4]) for n in ("amax", "amax_all", "safe", "scale", "back", "x_amax",
                                                       "x_safe", "x_scale", "x_back")]
        amax, amax_all, safe, scale, back, x_amax, x_safe, x_scale, x_back = (t[:, :] for t in blocks)
        stats = sb("c_stats", [P, TT, 6])
        mv = sb("c_mv", [P, TT, 2])
        veps = sb("c_veps", [P, TT])
        rstd = sb("c_rstd", [P, TT])

        p_key = [ps(f"p_key{n}") for n in range(2)]
        p_val = [ps(f"p_val{n}") for n in range(2)]
        p_kt = ps("p_kt")
        p_xt = [ps(f"p_xt{n}") for n in range(2)]
        p_y = ps("p_y")

        w_in = [Signal(K, f"c_weight{n}_in", unit=16) for n in range(2)]
        gates_in = Signal(K, "c_gates_in", unit=16)
        kw_in = Signal(K, "c_key_norm_in", unit=16)
        ctx_in = Signal(K, "c_context_in", unit=16)
        x_in = Signal(K, "c_x_in", unit=16)
        w_hi = Signal(K, "c_weight_hi")
        w_lo = Signal(K, "c_weight_lo")
        ident_made = Signal(K, "c_ident_made")
        ctx_hi = Signal(K, "c_context_hi")
        ctx_lo = Signal(K, "c_context_lo")
        ctx_amax = Signal(K, "c_context_amax")
        ctx_amax_all = Signal(K, "c_context_amax_all")
        ctx_quant = Signal(K, "c_context_quantised")
        cq_hi_made = Signal(K, "c_cq_hi", credit=1)
        cq_lo_made = Signal(K, "c_cq_lo", credit=1)
        x_var = Signal(K, "c_x_variance")
        x_rstd = Signal(K, "c_x_rstd")
        x_quant = Signal(K, "c_x_quantised")
        key_made = Signal(K, "c_key_product", per=TT, credit=1)
        val_made = Signal(K, "c_value_product", per=TT, credit=1)
        val_copied = Signal(K, "c_value_copied", per=TT, credit=2)
        val_lo = Signal(K, "c_value_lo", per=TT, credit=2)
        key_sq = Signal(K, "c_key_squares", per=TT)
        key_rstd = Signal(K, "c_key_rstd", per=TT, credit=2)
        key_nrm = Signal(K, "c_key_normalised", per=TT, credit=2)
        key_turned = Signal(K, "c_key_transposed", per=TT, credit=2)
        key_full = Signal(K, "c_key_full", per=TT, credit=1)
        key_hi = Signal(K, "c_key_hi", per=TT)
        key_lo = Signal(K, "c_key_lo", per=TT, credit=2)
        kv_out = Signal(K, "c_kv_stored", per=2, credit=2, unit=16)
        x_turned = Signal(K, "c_x_transposed", per=KT, credit=1)
        xq_hi_made = Signal(K, "c_xq_hi", per=KT)
        xq_lo_made = Signal(K, "c_xq_lo", per=KT, credit=2)
        y_made = Signal(K, "c_product", per=TT, credit=1)
        y_added = Signal(K, "c_added", per=TT, credit=1)
        v_steps = Signal(K, "c_vector_steps", per=19)
        p_steps = Signal(K, "c_pool_steps", per=1 + TT)
        block = ctx.enter_context(nc.Block())

        @block.sync
        def _(sp):
            sp.sem_inc(kv_out.sem, kv_out.opening)
            sp.dma_start(w_raw[:, :, :], wk.rearrange("(k p) n -> p k n", p=P)).then_inc(w_in[0].sem, 16)
            sp.dma_start(K.gates_raw[:, 0:2], g_xattn.partition_broadcast(P)).then_inc(gates_in.sem, 16)
            sp.dma_start(K.gates_raw[:, 2:4], g_ffn.partition_broadcast(P)).then_inc(gates_in.sem, 16)
            sp.dma_start(kw[:, :], k_norm_w.rearrange("(p a) -> p a", a=1)).then_inc(kw_in.sem, 16)
            sp.wait_ge(w_lo.sem, w_lo.at(0))
            sp.dma_start(w_raw[:, :, :], wv.rearrange("(k p) n -> p k n", p=P)).then_inc(w_in[1].sem, 16)
            with sp.Fori(0, B) as b:
                sp.wait_ge(cq_lo_made.sem, cq_lo_made.at(-1, b))
                sp.sem_inc(K.apart, 1)
                sp.wait_ge(cq_hi_made.sem, cq_hi_made.at(-1, b))
                sp.sem_inc(K.apart, 1)
                sp.dma_start(c_raw[:, :, :],
                             ctx_t[bass.ds(b, 1)].rearrange("a (k p) n -> p (a k) n",
                                                            p=P)).then_inc(ctx_in.sem, 16)
                sp.dma_start(K.x[:, bass.ds(b * TT, TT), :],
                             x[bass.ds(b * S, S), :].rearrange("(t p) d -> p t d", p=P)).then_inc(x_in.sem, 16)
                sp.wait_ge(key_lo.sem, key_lo.at(TT - 1, b))
                sp.sem_inc(K.apart, 1)
                sp.wait_ge(val_lo.sem, val_lo.at(TT - 1, b))
                sp.sem_inc(K.apart, 1)
                sp.dma_start(keys[bass.ds(b, 1)].rearrange("a p h g n -> p (a h) g n"),
                             f32(k_out[:, :, :, :])).then_inc(kv_out.sem, 16)
                sp.dma_start(values[bass.ds(b, 1)].rearrange("a p h t n -> p (a h) t n"),
                             f32(v_out[:, :, :, :])).then_inc(kv_out.sem, 16)
            sp.wait_ge(kv_out.sem, kv_out.at(1, B - 1))

        @block.scalar
        def _(act):
            for s in (cq_hi_made, val_copied, key_nrm, key_full):
                act.sem_inc(s.sem, s.opening)
            for n, hi in enumerate((wk_hi, wv_hi)):
                act.wait_ge(w_in[n].sem, w_in[n].at(0))
                act.activation(hi[:, :, :], w_raw[:, :, :], ACT.Copy).then_inc(w_hi.sem, 1)
            act.wait_ge(gates_in.sem, gates_in.at(1))
            act.activation(K.gates[:, :], K.gates_raw[:, :], ACT.Tanh).then_inc(K.gates_made.sem, 1)
            act.wait_ge(kw_in.sem, kw_in.at(0))
            with act.Fori(0, B) as b:
                act.wait_ge(ctx_in.sem, ctx_in.at(0, b))
                act.wait_ge(val_made.sem, val_made.at(-1, b))
                act.activation(c_hi[:, :, :], c_raw[:, :, :], ACT.Copy).then_inc(ctx_hi.sem, 1)

                def values_and_squares(j):
                    act.wait_ge(val_made.sem, val_made.at(j, b))
                    if j == 0:
                        act.wait_ge(kv_out.sem, kv_out.at(-1, b))
                    act.wait_ge(val_lo.sem, val_lo.at(j - 2, b))
                    act.activation(v_out[:, 0, j, :], p_val[j % 2][:, :], ACT.Copy)
                    act.activation(v_full[:, j % 2, :], p_val[j % 2][:, :], ACT.Copy).then_inc(val_copied.sem, 1)
                    act.wait_ge(key_made.sem, key_made.at(j, b))
                    act.wait_ge(key_rstd.sem, key_rstd.at(j - 2, b))
                    for g in range(G):
                        cols = slice(g * DH, (g + 1) * DH)
                        ins = act.activation(k_sq[:, j % 2, cols], p_key[j % 2][:, cols], ACT.Square,
                                             accum_out=k_ms[:, j % 2, g:g + 1])
                    ins.then_inc(key_sq.sem, 1)

                def normalise_keys(j):
                    act.wait_ge(key_rstd.sem, key_rstd.at(j, b))
                    act.wait_ge(key_turned.sem, key_turned.at(j - 2, b))
                    for g in range(G):
                        cols = slice(g * DH, (g + 1) * DH)
                        ins = act.activation(k_nrm[:, j % 2, cols], p_key[j % 2][:, cols], ACT.Copy,
                                             scale=k_rstd[:, j % 2, g:g + 1])
                    ins.then_inc(key_nrm.sem, 1)
                    act.wait_ge(key_turned.sem, key_turned.at(j, b))
                    act.wait_ge(key_lo.sem, key_lo.at(j - 2, b))
                    act.activation(k_full[:, j % 2, :], p_kt[:, :], ACT.Copy,
                                   scale=kw[:, 0:1]).then_inc(key_full.sem, 1)

                for j in range(TT):
                    values_and_squares(j)
                    if j >= 1:
                        normalise_keys(j - 1)
                normalise_keys(TT - 1)
                act.wait_ge(ctx_quant.sem, ctx_quant.at(0, b))
                act.wait_ge(y_made.sem, y_made.at(-1, b))
                act.activation(cq_hi[:, :, :], c_raw[:, :, :], ACT.Copy).then_inc(cq_hi_made.sem, 1)
                for k in range(KT):
                    act.wait_ge(x_turned.sem, x_turned.at(k, b))
                    act.activation(xq_hi[:, k, :], p_xt[k % 2][:, :], ACT.Copy).then_inc(xq_hi_made.sem, 1)

        @block.gpsimd
        def _(pool):
            for s in (val_lo, key_rstd, key_lo):
                pool.sem_inc(s.sem, s.opening)
            pool.memset(K.power[:, :], -0.5)
            pool.memset(K.ln_eps[:, :], LN_EPS)
            step = Count(ident_made)
            pool.memset(K.ident[:, :], 0.0).then_inc(step.sem, 1)
            pool.wait_ge(step.sem, step.next())
            pool.affine_select(out=K.ident[:, :], in_=K.ident[:, :], compare_op=ALU.not_equal, fill=1.0,
                               base=0, pattern=[[-1, P]], channel_multiplier=1).then_inc(step.sem, 1)
            pool.wait_ge(step.sem, step.next())
            with pool.Fori(0, B) as b:
                step = Count(p_steps, b)
                pool.wait_ge(ctx_hi.sem, ctx_hi.at(0, b))
                pool.tensor_tensor(c_lo[:, :, :], c_raw[:, :, :], f32(c_hi[:, :, :]),
                                   ALU.subtract).then_inc(ctx_lo.sem, 1)
                pool.wait_ge(ctx_amax.sem, ctx_amax.at(0, b))
                pool.sem_inc(K.apart, 1)
                pool.partition_all_reduce(amax_all, amax, P,
                                          bass.bass_isa.ReduceOp.max).then_inc(ctx_amax_all.sem, 1)
                pool.wait_ge(x_var.sem, x_var.at(0, b))
                pool.sem_inc(K.apart, 1)
                pool.tensor_scalar(veps[:, :], mv[:, :, 1], LN_EPS, None, ALU.add).then_inc(step.sem, 1)
                pool.wait_ge(step.sem, step.next())
                pool.tensor_tensor(rstd[:, :], veps[:, :], K.power[:, 0:TT], ALU.pow).then_inc(x_rstd.sem, 1)

                def rstd_and_values_lo(j):
                    pool.wait_ge(key_sq.sem, key_sq.at(j, b))
                    pool.wait_ge(key_nrm.sem, key_nrm.at(j - 2, b))
                    pool.sem_inc(K.apart, 1)
                    pool.tensor_scalar(k_eps[:, j % 2, :], k_ms[:, j % 2, :], 1.0 / DH, RMS_EPS,
                                       ALU.mult, ALU.add).then_inc(step.sem, 1)
                    pool.wait_ge(step.sem, step.next())
                    pool.tensor_tensor(k_rstd[:, j % 2, :], k_eps[:, j % 2, :],
                                       K.power[:, 0:G], ALU.pow).then_inc(key_rstd.sem, 1)
                    pool.wait_ge(val_copied.sem, val_copied.at(j, b))
                    pool.tensor_tensor(v_out[:, 1, j, :], v_full[:, j % 2, :],
                                       f32(v_out[:, 0, j, :]), ALU.subtract).then_inc(val_lo.sem, 1)

                def split_keys(j):
                    cols = slice(j * P, (j + 1) * P)
                    whole = k_full[:, j % 2, :].rearrange("p (g n) -> p g n", g=G)
                    pool.wait_ge(key_full.sem, key_full.at(j, b))
                    pool.sem_inc(K.apart, 1)
                    pool.tensor_copy(k_out[:, 0, :, cols], whole).then_inc(key_hi.sem, 1)
                    pool.wait_ge(key_hi.sem, key_hi.at(j, b))
                    pool.tensor_tensor(k_out[:, 1, :, cols], whole, f32(k_out[:, 0, :, cols]),
                                       ALU.subtract).then_inc(key_lo.sem, 1)

                for j in range(TT):
                    if j == 0:
                        pool.wait_ge(kv_out.sem, kv_out.at(-1, b))
                    rstd_and_values_lo(j)
                    if j >= 1:
                        split_keys(j - 1)
                split_keys(TT - 1)
                assert step.n == p_steps.per

        @block.vector
        def _(dve):
            for s in (cq_lo_made, xq_lo_made, y_added):
                dve.sem_inc(s.sem, s.opening)
            for n, (hi, lo) in enumerate(((wk_hi, wk_lo), (wv_hi, wv_lo))):
                dve.wait_ge(w_hi.sem, w_hi.at(n))
                dve.tensor_tensor(lo[:, :, :], w_raw[:, :, :], f32(hi[:, :, :]),
                                  ALU.subtract).then_inc(w_lo.sem, 1)
            dve.wait_ge(K.gates_made.sem, K.gates_made.at(0))
            with dve.Fori(0, B) as b:
                step = Count(v_steps, b)
                c_blocks = c_raw[:, :, :].rearrange("p k (c n) -> p (k c) n", n=P)
                dve.wait_ge(ctx_in.sem, ctx_in.at(0, b))
                dve.tensor_reduce(amax, c_blocks, AX.X, ALU.max,
                                  apply_absolute_value=True).then_inc(ctx_amax.sem, 1)
                dve.wait_ge(x_in.sem, x_in.at(0, b))
                xs = K.x[:, bass.ds(b * TT, TT), :]
                layer_norm_stats(dve, xs, stats, mv, step, K.apart).then_inc(x_var.sem, 1)
                dve.wait_ge(ctx_amax_all.sem, ctx_amax_all.at(0, b))
                dve.wait_ge(ctx_hi.sem, ctx_hi.at(0, b))
                dve.wait_ge(ctx_lo.sem, ctx_lo.at(0, b))
                quantise(dve, step, c_blocks, scale, W_EPS, grid[:, :, :], back, safe,
                         amax_all).then_inc(ctx_quant.sem, 1)
                dve.wait_ge(cq_hi_made.sem, cq_hi_made.at(0, b))
                dve.tensor_tensor(cq_lo[:, :, :], c_raw[:, :, :], f32(cq_hi[:, :, :]),
                                  ALU.subtract).then_inc(cq_lo_made.sem, 1)
                dve.wait_ge(x_rstd.sem, x_rstd.at(0, b))
                dve.wait_ge(x_turned.sem, x_turned.at(-1, b))
                for t in range(TT):
                    ins = dve.tensor_scalar(xn[:, t, :], xs[:, t, :], mv[:, t, 0:1], rstd[:, t:t + 1],
                                            ALU.subtract, ALU.mult)
                ins.then_inc(step.sem, 1)
                dve.wait_ge(step.sem, step.next())
                x_blocks = xn[:, :, :].rearrange("p t (c n) -> p (t c) n", n=P)
                dve.tensor_reduce(x_amax, x_blocks, AX.X, ALU.max,
                                  apply_absolute_value=True).then_inc(step.sem, 1)
                dve.wait_ge(step.sem, step.next())
                quantise(dve, step, x_blocks, x_scale, ACT_EPS, grid[:, :, :], x_back, x_safe,
                         x_amax).then_inc(x_quant.sem, 1)
                for k in range(KT):
                    dve.wait_ge(xq_hi_made.sem, xq_hi_made.at(k, b))
                    if k == 0:
                        dve.wait_ge(y_made.sem, y_made.at(-1, b))
                    dve.tensor_tensor(xq_lo[:, k, :], p_xt[k % 2][:, :], f32(xq_hi[:, k, :]),
                                      ALU.subtract).then_inc(xq_lo_made.sem, 1)
                for t in range(TT):
                    dve.wait_ge(y_made.sem, y_made.at(t, b))
                    dve.scalar_tensor_tensor(xs[:, t, :], p_y[:, :], K.gates[:, 0:1], xs[:, t, :],
                                             ALU.mult, ALU.add).then_inc(y_added.sem, 1)
                assert step.n == v_steps.per

        @block.tensor
        def _(pe):
            for s in (key_made, val_made, key_turned, x_turned, y_made):
                pe.sem_inc(s.sem, s.opening)
            pe.wait_ge(w_lo.sem, w_lo.at(1))
            pe.wait_ge(ident_made.sem, ident_made.at(1))
            with pe.Fori(0, B) as b:
                pe.wait_ge(ctx_lo.sem, ctx_lo.at(0, b))
                pe.wait_ge(ctx_hi.sem, ctx_hi.at(0, b))

                def keys_and_values(j):
                    rows = slice(j * P, (j + 1) * P)
                    pe.wait_ge(key_nrm.sem, key_nrm.at(j - 2, b))
                    for k in range(KT):
                        ins = three_pass(pe, p_key[j % 2][:, :], c_hi[:, k, rows], c_lo[:, k, rows],
                                         wk_hi[:, k, :], wk_lo[:, k, :], k == 0, k == KT - 1)
                    ins.then_inc(key_made.sem, 1)
                    pe.wait_ge(val_copied.sem, val_copied.at(j - 2, b))
                    for k in range(KT):
                        ins = three_pass(pe, p_val[j % 2][:, :], c_hi[:, k, rows], c_lo[:, k, rows],
                                         wv_hi[:, k, :], wv_lo[:, k, :], k == 0, k == KT - 1)
                    ins.then_inc(val_made.sem, 1)

                def turn_keys(j):
                    pe.wait_ge(key_nrm.sem, key_nrm.at(j, b))
                    pe.wait_ge(key_full.sem, key_full.at(j - 1, b))
                    for g in range(G):
                        ins = pe.transpose(p_kt[:, g * P:(g + 1) * P], k_nrm[:, j % 2, g * DH:(g + 1) * DH],
                                           K.ident[:, :])
                    ins.then_inc(key_turned.sem, 1)

                for j in range(TT):
                    keys_and_values(j)
                    if j >= 1:
                        turn_keys(j - 1)
                turn_keys(TT - 1)
                pe.wait_ge(x_quant.sem, x_quant.at(0, b))
                for k in range(KT):
                    pe.wait_ge(xq_lo_made.sem, xq_lo_made.at(k - 2, b))
                    for t in range(TT):
                        ins = pe.transpose(p_xt[k % 2][:, t * P:(t + 1) * P], xn[:, t, k * P:(k + 1) * P],
                                           K.ident[:, :])
                    ins.then_inc(x_turned.sem, 1)
                pe.wait_ge(xq_lo_made.sem, xq_lo_made.at(KT - 1, b))
                pe.wait_ge(cq_lo_made.sem, cq_lo_made.at(0, b))
                for t in range(TT):
                    rows = slice(t * P, (t + 1) * P)
                    pe.wait_ge(y_added.sem, y_added.at(t - 1, b))
                    for k in range(KT):
                        ins = three_pass(pe, p_y[:, :], xq_hi[:, k, rows], xq_lo[:, k, rows],
                                         cq_hi[:, k, :], cq_lo[:, k, :], k == 0, k == KT - 1)
                    ins.then_inc(y_made.sem, 1)


def stage_norm(K, tag):
    with ExitStack() as ctx:
        sb, ps = K.scope(ctx)
        xn = sb(f"{tag}_xn", [P, 2, TT, D])
        stats = sb(f"{tag}_stats", [P, TT, 6])
        mv = sb(f"{tag}_mv", [P, TT, 2])
        veps = sb(f"{tag}_veps", [P, TT])
        rstd = sb(f"{tag}_rstd", [P, TT])
        p_t = [ps(f"{tag}_p{k}") for k in range(2 * KT)]

        var = Signal(K, f"{tag}_variance", per=2)
        rstd_made = Signal(K, f"{tag}_rstd", per=2)
        normed = Signal(K, f"{tag}_normalised", per=2)
        turned = Signal(K, f"{tag}_transposed", per=2 * KT, credit=2 * KT)
        hi_made = Signal(K, f"{tag}_hi", per=2 * KT)
        lo_made = Signal(K, f"{tag}_lo", per=2 * KT, credit=2 * KT)
        steps = Signal(K, f"{tag}_vector_steps", per=2)
        p_steps = Signal(K, f"{tag}_pool_steps", per=2)
        block = ctx.enter_context(K.nc.Block())

        @block.vector
        def _(dve):
            dve.sem_inc(lo_made.sem, lo_made.opening)
            with dve.Fori(0, B // 2) as i:
                step = Count(steps, i)
                for u in range(2):
                    xs = K.x[:, bass.ds(i * (2 * TT) + u * TT, TT), :]
                    if u == 1:
                        dve.wait_ge(normed.sem, normed.at(0, i))
                    layer_norm_stats(dve, xs, stats, mv, step, K.apart).then_inc(var.sem, 1)
                    dve.wait_ge(rstd_made.sem, rstd_made.at(u, i))
                    dve.wait_ge(turned.sem, turned.at((u - 2) * KT + KT - 1, i))
                    for t in range(TT):
                        ins = dve.tensor_scalar(xn[:, u, t, :], xs[:, t, :], mv[:, t, 0:1], rstd[:, t:t + 1],
                                                ALU.subtract, ALU.mult)
                    ins.then_inc(normed.sem, 1)
                for u in range(2):
                    for k in range(KT):
                        dve.wait_ge(hi_made.sem, hi_made.at(u * KT + k, i))
                        cols = bass.ds(i * (2 * S) + u * S, S)
                        dve.tensor_tensor(K.xt_lo[:, k, cols], p_t[u * KT + k][:, :],
                                          f32(K.xt_hi[:, k, cols]), ALU.subtract).then_inc(lo_made.sem, 1)

        @block.gpsimd
        def _(pool):
            with pool.Fori(0, B // 2) as i:
                step = Count(p_steps, i)
                for u in range(2):
                    pool.wait_ge(var.sem, var.at(u, i))
                    pool.tensor_tensor(veps[:, :], mv[:, :, 1], K.ln_eps[:, :], ALU.add).then_inc(step.sem, 1)
                    pool.wait_ge(step.sem, step.next())
                    pool.tensor_tensor(rstd[:, :], veps[:, :], K.power[:, 0:TT],
                                       ALU.pow).then_inc(rstd_made.sem, 1)

        @block.tensor
        def _(pe):
            pe.sem_inc(turned.sem, turned.opening)
            with pe.Fori(0, B // 2) as i:
                for u in range(2):
                    pe.wait_ge(normed.sem, normed.at(u, i))
                    for k in range(KT):
                        pe.wait_ge(lo_made.sem, lo_made.at((u - 2) * KT + k, i))
                        for t in range(TT):
                            ins = pe.transpose(p_t[u * KT + k][:, t * P:(t + 1) * P],
                                               xn[:, u, t, k * P:(k + 1) * P], K.ident[:, :])
                        ins.then_inc(turned.sem, 1)

        @block.scalar
        def _(act):
            with act.Fori(0, B // 2) as i:
                for u in range(2):
                    for k in range(KT):
                        act.wait_ge(turned.sem, turned.at(u * KT + k, i))
                        act.activation(K.xt_hi[:, k, bass.ds(i * (2 * S) + u * S, S)],
                                       p_t[u * KT + k][:, :], ACT.Copy).then_inc(hi_made.sem, 1)


def stage_ffn(K, w1_t, w2_t, b1_t, b2):
    with ExitStack() as ctx:
        sb, ps = K.scope(ctx)
        CH = 4
        w1q, w2q = sb("w1q", [P, KT, F], F32R), sb("w2q", [P, FT, D], F32R)
        raw = sb("f_raw", [P, 2, F])
        least = sb("f_least", [P, F])
        sums = sb("f_sums", [P, CH, 32])
        total = sb("f_total", [P, 2])
        total_all = sb("f_total_all", [P, 2])
        thr, neg_thr = sb("f_thr", [P, 2]), sb("f_neg_thr", [P, 2])
        b1_c = sb("b1_c", [P, FT])
        b2_r, b2_g = sb("b2_r", [P, D]), sb("b2_g", [P, D])
        act_out = sb("f_act", [P, 2, S])
        h_hi, h_lo = sb("h_hi", [P, 2, S], F32R), sb("h_lo", [P, 2, S], F32R)
        p_h = [ps(f"p_h{n}") for n in range(2)]
        p_y = [ps(f"f_y{t}") for t in range(TT)]

        bias_in = Signal(K, "f_bias_in", unit=16)
        w_in = [Signal(K, f"f_weights_in{n}", unit=16) for n in range(2)]
        w_used = Signal(K, "f_weights_used")
        totals = Signal(K, "f_totals")
        total_made = Signal(K, "f_total_all_made")
        w_made = Signal(K, "f_ternary_made")
        b2_made = Signal(K, "f_b2_scaled")
        b2_added = Signal(K, "f_b2_added", per=TT)
        h_made = Signal(K, "f_h_product", per=FT)
        gelu_made = Signal(K, "f_gelu", per=FT, credit=2)
        hi_made = Signal(K, "f_h_hi", per=FT, credit=2)
        lo_made = Signal(K, "f_h_lo", per=FT, credit=2)
        h_used = Signal(K, "f_h_used", per=FT, credit=2)
        y_added = Signal(K, "f_added", per=TT, credit=TT)
        steps = Signal(K, "f_vector_steps")
        block = ctx.enter_context(K.nc.Block())
        chunks = [w1_t.rearrange("(k p) f -> k p f", p=P)[c] for c in range(CH)]
        chunks2 = [w2_t.rearrange("(c k p) n -> c p k n", p=P, k=CH)[c] for c in range(CH)]
        loads = [(w, c) for w in range(2) for _ in range(2) for c in range(CH)]

        @block.sync
        def _(sp):
            sp.dma_start(b1_c[:, :], b1_t).then_inc(bias_in.sem, 16)
            sp.dma_start(b2_r[:, :], b2.partition_broadcast(P)).then_inc(bias_in.sem, 16)
            for n, (w, c) in enumerate(loads):
                if n >= 2:
                    sp.wait_ge(w_used.sem, w_used.at(n - 2))
                dst = raw[:, n % 2, :]
                if w == 0:
                    sp.dma_start(dst, chunks[c]).then_inc(w_in[n % 2].sem, 16)
                else:
                    sp.dma_start(dst.rearrange("p (k n) -> p k n", k=CH), chunks2[c]).then_inc(w_in[n % 2].sem,
                                                                                               16)

        @block.gpsimd
        def _(pool):
            for w in range(2):
                pool.wait_ge(totals.sem, totals.at(w))
                pool.partition_all_reduce(total_all[:, w:w + 1], total[:, w:w + 1], P,
                                          bass.bass_isa.ReduceOp.add).then_inc(total_made.sem, 1)
            pool.wait_ge(b2_made.sem, b2_made.at(0))
            for t in range(T):
                pool.tensor_tensor(K.x[:, t, :], K.x[:, t, :], b2_g[:, :], ALU.add).then_inc(b2_added.sem, 1)

        @block.vector
        def _(dve):
            dve.sem_inc(lo_made.sem, lo_made.opening)
            dve.sem_inc(y_added.sem, y_added.opening)
            step = Count(steps)
            dve.wait_ge(bias_in.sem, bias_in.at(1))
            dve.tensor_scalar(b2_g[:, :], b2_r[:, :], K.gates[:, 2:3], None, ALU.mult).then_inc(b2_made.sem, 1)
            n = 0
            for w, wq in enumerate((w1q[:, :, :], w2q[:, :, :])):
                for c in range(CH):
                    dve.wait_ge(w_in[n % 2].sem, w_in[n % 2].at(n // 2))
                    dve.tensor_reduce(sums[:, c, :],
                                      raw[:, n % 2, :].rearrange("p (a n) -> p a n", a=32),
                                      AX.X, ALU.add, apply_absolute_value=True).then_inc(w_used.sem, 1)
                    n += 1
                dve.wait_ge(w_used.sem, w_used.at(n - 1))
                dve.tensor_reduce(total[:, w:w + 1], sums[:, :, :], AX.XY, ALU.add).then_inc(totals.sem, 1)
                dve.wait_ge(total_made.sem, total_made.at(w))
                dve.tensor_scalar(thr[:, w:w + 1], total_all[:, w:w + 1], 1.0 / (D * F), 0.7,
                                  ALU.mult, ALU.mult)
                dve.tensor_scalar(neg_thr[:, w:w + 1], total_all[:, w:w + 1], -1.0 / (D * F), 0.7,
                                  ALU.mult, ALU.mult).then_inc(step.sem, 1)
                dve.wait_ge(step.sem, step.next())
                for c in range(CH):
                    dve.wait_ge(w_in[n % 2].sem, w_in[n % 2].at(n // 2))
                    dve.wait_ge(w_used.sem, w_used.at(n - 1))
                    part = wq.rearrange("p k n -> p (k n)")[:, c * F:(c + 1) * F]
                    dve.tensor_scalar(least[:, :], raw[:, n % 2, :], neg_thr[:, w:w + 1], None,
                                      ALU.is_le).then_inc(step.sem, 1)
                    dve.wait_ge(step.sem, step.next())
                    dve.scalar_tensor_tensor(part, raw[:, n % 2, :], thr[:, w:w + 1],
                                             least[:, :], ALU.is_ge, ALU.subtract).then_inc(w_used.sem, 1)
                    n += 1
            with dve.Fori(0, B) as b:
                for f in range(FT):
                    dve.wait_ge(hi_made.sem, hi_made.at(f, b))
                    dve.wait_ge(h_used.sem, h_used.at(f - 2, b))
                    dve.tensor_tensor(h_lo[:, f % 2, :], act_out[:, f % 2, :],
                                      f32(h_hi[:, f % 2, :]), ALU.subtract).then_inc(lo_made.sem, 1)
                dve.wait_ge(h_used.sem, h_used.at(FT - 1, b))
                dve.wait_ge(b2_added.sem, b2_added.at(TT - 1, b))
                for t in range(TT):
                    xt = K.x[:, bass.ds(b * TT + t, 1), :].rearrange("p a n -> p (a n)")
                    dve.scalar_tensor_tensor(xt, p_y[t][:, :], K.gates[:, 2:3], xt,
                                             ALU.mult, ALU.add).then_inc(y_added.sem, 1)

        @block.scalar
        def _(act):
            act.sem_inc(gelu_made.sem, gelu_made.opening)
            act.sem_inc(hi_made.sem, hi_made.opening)
            act.wait_ge(bias_in.sem, bias_in.at(1))
            with act.Fori(0, B) as b:
                for f in range(FT):
                    act.wait_ge(h_made.sem, h_made.at(f, b))
                    act.wait_ge(lo_made.sem, lo_made.at(f - 2, b))
                    act.activation(act_out[:, f % 2, :], p_h[f % 2][:, :], ACT.Gelu,
                                   bias=b1_c[:, f:f + 1]).then_inc(gelu_made.sem, 1)
                    act.wait_ge(gelu_made.sem, gelu_made.at(f, b))
                    act.wait_ge(h_used.sem, h_used.at(f - 2, b))
                    act.activation(h_hi[:, f % 2, :], act_out[:, f % 2, :], ACT.Copy).then_inc(hi_made.sem, 1)

        @block.tensor
        def _(pe):
            pe.sem_inc(h_used.sem, h_used.opening)
            pe.wait_ge(w_used.sem, w_used.at(2 * CH - 1))

            def hidden(b, f):
                pe.wait_ge(gelu_made.sem, gelu_made.at(f - 2, b))
                for k in range(KT):
                    w = w1q[:, k, f * P:(f + 1) * P]
                    cols = bass.ds(b * S, S)
                    pe.matmul(p_h[f % 2][:, :], w, K.xt_hi[:, k, cols], start=k == 0, stop=False)
                    ins = pe.matmul(p_h[f % 2][:, :], w, K.xt_lo[:, k, cols], start=False, stop=k == KT - 1)
                ins.then_inc(h_made.sem, 1)

            def output(b, f):
                pe.wait_ge(lo_made.sem, lo_made.at(f, b))
                for t in range(TT):
                    rows = slice(t * P, (t + 1) * P)
                    if f == 0:
                        pe.wait_ge(y_added.sem, y_added.at(t - TT, b))
                    pe.matmul(p_y[t][:, :], h_hi[:, f % 2, rows], w2q[:, f, :], start=f == 0, stop=False)
                    ins = pe.matmul(p_y[t][:, :], h_lo[:, f % 2, rows], w2q[:, f, :], start=False,
                                    stop=f == FT - 1)
                ins.then_inc(h_used.sem, 1)

            with pe.Fori(0, B) as b:
                for f in range(FT):
                    hidden(b, f)
                    if f == 1:
                        pe.wait_ge(w_used.sem, w_used.at(4 * CH - 1))
                    if f >= 1:
                        output(b, f - 1)
                output(b, FT - 1)


def stage_attention(K, wq, wo, q_norm_w, keys, values):
    with ExitStack() as ctx:
        sb, ps = K.scope(ctx)
        U = HG * TT
        HALF = S // 2
        w_raw = sb("a_w_raw", [P, KT, HG * DH])
        wq_hi, wq_lo = sb("wq_hi", [P, KT, HG * DH], F32R), sb("wq_lo", [P, KT, HG * DH], F32R)
        wo_hi, wo_lo = sb("wo_hi", [P, HG, D], F32R), sb("wo_lo", [P, HG, D], F32R)
        k_in = sb("k_in", [P, 2, 2, S], F32R)
        v_in = sb("v_in", [P, 2, TT, DH], F32R)
        q_hi, q_lo = sb("q_hi", [P, 2, S], F32R), sb("q_lo", [P, 2, S], F32R)
        q_sq = sb("q_sq", [P, S])
        q_ms = sb("q_ms", [P, 2, TT])
        q_rs = sb("q_rs", [P, 2, TT])
        neg_max = sb("neg_max", [P, U])
        bias = sb("a_bias", [P, U])
        total = sb("a_total", [P, U])
        inv = sb("a_inv", [P, U])
        prob = sb("prob", [P, 3, S])
        pt_hi, pt_lo = sb("pt_hi", [P, 2, TT, HALF], F32R), sb("pt_lo", [P, 2, TT, HALF], F32R)
        o_hi, o_lo = sb("o_hi", [P, HG, S], F32R), sb("o_lo", [P, HG, S], F32R)
        ones = sb("a_ones", [P, 1])
        qw = sb("qw", [P, 1])
        p_s = [ps(f"p_s{n}") for n in range(3)]
        p_t = [ps(f"p_t{n}") for n in range(2)]
        p_q = ps("p_q")
        p_o = [ps(f"p_o{n}") for n in range(2)]
        QUERY_AT = {4 * j - 5 if j > 1 else 0: j for j in range(1, HG)}
        SUMS_AT = {4 * j - 4 if j > 1 else 1: j for j in range(1, HG)}

        qw_in = Signal(K, "a_query_norm_in", unit=16)
        w_in = Signal(K, "a_weights_in", per=2, unit=16)
        w_hi = Signal(K, "a_weights_hi", per=2)
        w_lo = Signal(K, "a_weights_lo", per=2, credit=1)
        keys_in = Signal(K, "a_keys_in", unit=16)
        values_in = Signal(K, "a_values_in", unit=16)
        ones_made = Signal(K, "a_ones_made")
        q_made = Signal(K, "a_q_product", per=HG, credit=1)
        q_squared = Signal(K, "a_q_squared", per=HG)
        q_hi_made = Signal(K, "a_q_hi", per=HG)
        q_lo_made = Signal(K, "a_q_lo", per=HG)
        ms_made = Signal(K, "a_q_square_sums", per=HG, credit=1)
        ms_read = Signal(K, "a_q_square_sums_read", per=HG, credit=1)
        rs_made = Signal(K, "a_q_scale", per=HG)
        s_made = Signal(K, "a_scores", per=U, credit=U + 1)
        max_made = Signal(K, "a_max", per=U)
        bias_made = Signal(K, "a_bias_made", per=U)
        exp_made = Signal(K, "a_exp", per=U, credit=3)
        inv_made = Signal(K, "a_inverse", per=U)
        p_made = Signal(K, "a_probabilities", per=U)
        t_made = Signal(K, "a_transposed", per=U, credit=3)
        pt_hi_made = Signal(K, "a_pt_hi", per=U)
        pt_lo_made = Signal(K, "a_pt_lo", per=U, credit=2)
        o_made = Signal(K, "a_heads_out", per=2 * HG, credit=2)
        o_hi_made = Signal(K, "a_o_hi", per=HG)
        o_lo_made = Signal(K, "a_o_lo", per=HG, credit=2)
        y_made = Signal(K, "a_product", per=TT, credit=TT)
        y_added = Signal(K, "a_added", per=TT, credit=2)
        block = ctx.enter_context(K.nc.Block())
        wq_v = wq.rearrange("(k p) n -> p k n", p=P)
        wo_v = wo.rearrange("(h p) n -> p h n", p=P)

        def batches(eng, g, first, body):
            first(g * B)
            with eng.Fori(0, B - 1) as b:
                body(g * B + b, b, False)
            body(g * B + (B - 1), B - 1, True)

        @block.sync
        def _(sp):
            sp.dma_start(qw[:, :], q_norm_w.rearrange("(p a) -> p a", a=1)).then_inc(qw_in.sem, 16)
            with sp.Fori(0, G) as g:
                sp.wait_ge(w_lo.sem, w_lo.at(-1, g))
                sp.sem_inc(K.apart, 1)
                sp.dma_start(w_raw[:, :, :], wq_v[:, :, bass.ds(g * (HG * DH), HG * DH)]).then_inc(w_in.sem, 16)

                def load(it, b):
                    if isinstance(b, int):
                        at, slot = slice(b, b + 1), slice(b % 2, b % 2 + 1)
                    else:
                        at, slot = bass.ds(b, 1), bass.ds(b % 2, 1)
                    sp.wait_ge(s_made.sem, s_made.at(-U - 1, it))
                    sp.sem_inc(K.apart, 1)
                    sp.dma_start(
             f32(k_in[:, slot, :, :]).rearrange("p s h n -> p (s h) n"),
             keys[at, :, :, bass.ds(g, 1), :].rearrange("a p h c n -> p (a h c) n")).then_inc(keys_in.sem, 16)
                    sp.wait_ge(o_made.sem, o_made.at(-1, it))
                    sp.sem_inc(K.apart, 1)
                    sp.dma_start(
           f32(v_in[:, :, :, :]),
           values[at, :, :, :, bass.ds(g * DH,
                                       DH)].rearrange("a p h t n -> p (a h) t n")).then_inc(values_in.sem, 16)
                    sp.wait_ge(keys_in.sem, keys_in.at(0, it))
                    sp.sem_inc(K.apart, 1)
                    sp.wait_ge(values_in.sem, values_in.at(0, it))
                    sp.sem_inc(K.apart, 1)

                load(g * B, 0)
                sp.wait_ge(w_lo.sem, w_lo.at(0, g))
                sp.sem_inc(K.apart, 1)
                sp.dma_start(w_raw[:, :, :], wo_v[:, bass.ds(g * HG, HG), :]).then_inc(w_in.sem, 16)
                with sp.Fori(1, B) as b:
                    load(g * B + b, b)

        @block.gpsimd
        def _(pool):
            pool.memset(ones[:, :], 1.0).then_inc(ones_made.sem, 1)
            with pool.Fori(0, G * B) as it:
                for h in range(HG):
                    pool.wait_ge(ms_read.sem, ms_read.at(h, it))
                    pool.tensor_tensor(q_rs[:, h % 2, :], q_ms[:, h % 2, :], K.power[:, 0:TT],
                                       ALU.pow).then_inc(rs_made.sem, 1)

        @block.scalar
        def _(act):
            act.sem_inc(exp_made.sem, exp_made.opening)
            act.wait_ge(qw_in.sem, qw_in.at(0))

            def split_query(it, h):
                act.wait_ge(q_made.sem, q_made.at(h, it))
                act.wait_ge(s_made.sem, s_made.at((h - 1) * TT - 1, it))
                act.activation(q_hi[:, h % 2, :], p_q[:, :], ACT.Copy,
                               scale=qw[:, 0:1]).then_inc(q_hi_made.sem, 1)
                act.wait_ge(ms_made.sem, ms_made.at(h - 1, it))
                act.activation(q_sq[:, :], p_q[:, :], ACT.Square).then_inc(q_squared.sem, 1)

            def exp(it, u):
                act.wait_ge(bias_made.sem, bias_made.at(u, it))
                act.wait_ge(t_made.sem, t_made.at(u - 3, it))
                act.activation(prob[:, u % 3, :], p_s[u % 3][:, :], ACT.Exp, bias=bias[:, u:u + 1],
                               scale=q_rs[:, u // TT % 2, u % TT:u % TT + 1],
                               accum_out=total[:, u:u + 1]).then_inc(exp_made.sem, 1)

            def head_out(it, h):
                act.wait_ge(o_made.sem, o_made.at(2 * h + 1, it))
                if h == 0:
                    act.wait_ge(y_made.sem, y_made.at(-1, it))
                act.activation(o_hi[:, h, :], p_o[h % 2][:, :], ACT.Copy).then_inc(o_hi_made.sem, 1)

            def first(it):
                split_query(it, 0)
                exp(it, 0)
                exp(it, 1)

            def body(it, b, last):
                for u in range(U):
                    if u in QUERY_AT:
                        split_query(it, QUERY_AT[u])
                    act.wait_ge(t_made.sem, t_made.at(u, it))
                    if u % 2 == 0:
                        act.wait_ge(o_made.sem, o_made.at(u // 2 - 2, it))
                    act.activation(
          pt_hi[:, u // 2 % 2, :, (u % 2) * P:(u % 2 + 1) * P],
          p_t[u % 2][:, :].rearrange("p (t n) -> p t n", t=TT), ACT.Copy).then_inc(pt_hi_made.sem, 1)
                    if u + 2 < U:
                        exp(it, u + 2)
                    if u % TT == 2 and u > TT:
                        head_out(it, u // TT - 1)
                if last:
                    head_out(it, HG - 1)
                else:
                    split_query(it + 1, 0)
                    head_out(it, HG - 1)
                    exp(it + 1, 0)
                    exp(it + 1, 1)

            with act.Fori(0, G) as g:
                for w, (hi, n) in enumerate(((wq_hi, "wq"), (wo_hi, "wo"))):
                    act.wait_ge(w_in.sem, w_in.at(w, g))
                    act.activation(hi[:, :, :], w_raw[:, :, :], ACT.Copy).then_inc(w_hi.sem, 1)
                batches(act, g, first, body)

        @block.vector
        def _(dve):
            for s in (w_lo, ms_read, pt_lo_made, o_lo_made, y_added):
                dve.sem_inc(s.sem, s.opening)
            dve.wait_ge(qw_in.sem, qw_in.at(0))

            def split_query(it, h):
                dve.wait_ge(q_hi_made.sem, q_hi_made.at(h, it))
                dve.wait_ge(q_squared.sem, q_squared.at(h, it))
                dve.scalar_tensor_tensor(q_lo[:, h % 2, :], p_q[:, :], qw[:, 0:1],
                                         f32(q_hi[:, h % 2, :]), ALU.mult, ALU.subtract).then_inc(q_lo_made.sem, 1)

            def query_scale(it, h):
                dve.wait_ge(ms_made.sem, ms_made.at(h, it))
                dve.tensor_scalar(q_ms[:, h % 2, :], p_q[:, 0:TT], DH * RMS_EPS, None,
                                  ALU.add).then_inc(ms_read.sem, 1)

            def maximum(it, u):
                dve.wait_ge(s_made.sem, s_made.at(u, it))
                dve.tensor_reduce(neg_max[:, u:u + 1], p_s[u % 3][:, :], AX.X, ALU.max,
                                  negate=True).then_inc(max_made.sem, 1)

            def shift(it, u):
                dve.wait_ge(max_made.sem, max_made.at(u, it))
                if u % TT == 0:
                    dve.wait_ge(rs_made.sem, rs_made.at(u // TT, it))
                dve.tensor_tensor(bias[:, u:u + 1], neg_max[:, u:u + 1],
                                  q_rs[:, u // TT % 2, u % TT:u % TT + 1], ALU.mult).then_inc(bias_made.sem, 1)

            def invert(it, u):
                dve.wait_ge(exp_made.sem, exp_made.at(u, it))
                dve.reciprocal(inv[:, u:u + 1], total[:, u:u + 1]).then_inc(inv_made.sem, 1)

            def normalise(it, u):
                dve.wait_ge(inv_made.sem, inv_made.at(u, it))
                dve.tensor_scalar(prob[:, u % 3, :], prob[:, u % 3, :], inv[:, u:u + 1], None,
                                  ALU.mult).then_inc(p_made.sem, 1)

            def head_out(it, h):
                dve.wait_ge(o_hi_made.sem, o_hi_made.at(h, it))
                dve.tensor_tensor(o_lo[:, h, :], p_o[h % 2][:, :], f32(o_hi[:, h, :]),
                                  ALU.subtract).then_inc(o_lo_made.sem, 1)

            def add(it, b, t):
                dve.wait_ge(y_made.sem, y_made.at(t, it))
                xt = K.x[:, bass.ds(b * TT + t, 1), :].rearrange("p a n -> p (a n)")
                dve.scalar_tensor_tensor(xt, p_t[t % 2][:, :], K.gates[:, 1:2], xt,
                                         ALU.mult, ALU.add).then_inc(y_added.sem, 1)

            def first(it):
                split_query(it, 0)
                query_scale(it, 0)
                for u in range(2):
                    maximum(it, u)
                    shift(it, u)
                invert(it, 0)
                normalise(it, 0)

            def body(it, b, last):
                for u in range(U):
                    if u in QUERY_AT:
                        split_query(it, QUERY_AT[u])
                    if u + 2 < U:
                        maximum(it, u + 2)
                    if u + 1 < U:
                        invert(it, u + 1)
                    if u + 2 < U:
                        shift(it, u + 2)
                    if u + 1 < U:
                        normalise(it, u + 1)
                    if u in SUMS_AT:
                        query_scale(it, SUMS_AT[u])
                    dve.wait_ge(pt_hi_made.sem, pt_hi_made.at(u, it))
                    dve.tensor_tensor(
          pt_lo[:, u // 2 % 2, :, (u % 2) * P:(u % 2 + 1) * P],
          p_t[u % 2][:, :].rearrange("p (t n) -> p t n", t=TT),
          f32(pt_hi[:, u // 2 % 2, :, (u % 2) * P:(u % 2 + 1) * P]), ALU.subtract).then_inc(pt_lo_made.sem, 1)
                    if u % TT == 2 and u > TT:
                        head_out(it, u // TT - 1)
                if last:
                    head_out(it, HG - 1)
                    add(it, b, 0)
                else:
                    split_query(it + 1, 0)
                    head_out(it, HG - 1)
                    query_scale(it + 1, 0)
                    for u in range(2):
                        maximum(it + 1, u)
                        shift(it + 1, u)
                    add(it, b, 0)
                    invert(it + 1, 0)
                    normalise(it + 1, 0)
                for t in range(1, TT):
                    add(it, b, t)

            with dve.Fori(0, G) as g:
                for w, (hi, lo) in enumerate(((wq_hi, wq_lo), (wo_hi, wo_lo))):
                    dve.wait_ge(w_hi.sem, w_hi.at(w, g))
                    dve.tensor_tensor(lo[:, :, :], w_raw[:, :, :], f32(hi[:, :, :]),
                                      ALU.subtract).then_inc(w_lo.sem, 1)
                batches(dve, g, first, body)

        @block.tensor
        def _(pe):
            for s in (q_made, ms_made, s_made, t_made, o_made, y_made):
                pe.sem_inc(s.sem, s.opening)
            pe.wait_ge(ones_made.sem, ones_made.at(0))

            def query(it, b, h):
                pe.wait_ge(ms_read.sem, ms_read.at(h - 1, it))
                heads = slice(h * DH, (h + 1) * DH)
                cols = bass.ds(b * S, S)
                for k in range(KT):
                    ins = three_pass(pe, p_q[:, :], wq_hi[:, k, heads], wq_lo[:, k, heads],
                                     K.xt_hi[:, k, cols], K.xt_lo[:, k, cols], k == 0, k == KT - 1)
                ins.then_inc(q_made.sem, 1)

            def square_sums(it, h):
                pe.wait_ge(q_squared.sem, q_squared.at(h, it))
                pe.wait_ge(q_lo_made.sem, q_lo_made.at(h, it))
                for t in range(TT):
                    ins = pe.matmul(p_q[:, t:t + 1], q_sq[:, t * P:(t + 1) * P], ones[:, :],
                                    start=True, stop=True)
                ins.then_inc(ms_made.sem, 1)

            def scores(it, b, u):
                h, qt = divmod(u, TT)
                if u == 0:
                    pe.wait_ge(keys_in.sem, keys_in.at(0, it))
                pe.wait_ge(exp_made.sem, exp_made.at(u - 3, it))
                if qt == 0:
                    pe.wait_ge(q_lo_made.sem, q_lo_made.at(h, it))
                rows = slice(qt * P, (qt + 1) * P)
                slot = bass.ds(b % 2, 1)
                k_hi = k_in[:, slot, 0, :].rearrange("p s n -> p (s n)")
                k_lo = k_in[:, slot, 1, :].rearrange("p s n -> p (s n)")
                three_pass(pe, p_s[u % 3][:, :], q_hi[:, h % 2, rows], q_lo[:, h % 2, rows],
                           k_hi, k_lo, True, True).then_inc(s_made.sem, 1)

            def turn(it, u):
                pe.wait_ge(p_made.sem, p_made.at(u, it))
                if u < 2:
                    pe.wait_ge(y_added.sem, y_added.at(u - 2, it))
                else:
                    pe.wait_ge(pt_lo_made.sem, pt_lo_made.at(u - 2, it))
                for t in range(TT):
                    ins = pe.transpose(p_t[u % 2][:, t * P:(t + 1) * P], prob[:, u % 3, t * P:(t + 1) * P],
                                       K.ident[:, :])
                ins.then_inc(t_made.sem, 1)

            def weigh_values(it, m):
                pe.wait_ge(pt_lo_made.sem, pt_lo_made.at(2 * m + 1, it))
                if m == 0:
                    pe.wait_ge(values_in.sem, values_in.at(0, it))
                if m % 2 == 0:
                    pe.wait_ge(o_lo_made.sem, o_lo_made.at(m // 2 - 2, it))
                for t in range(TT):
                    ins = three_pass(pe, p_o[m // 2 % 2][:, (m % 2) * HALF:(m % 2 + 1) * HALF],
                                     v_in[:, 0, t, :], v_in[:, 1, t, :],
                                     pt_hi[:, m % 2, t, :], pt_lo[:, m % 2, t, :], t == 0, t == TT - 1)
                ins.then_inc(o_made.sem, 1)

            def project(it, t):
                if t < 2:
                    pe.wait_ge(pt_lo_made.sem, pt_lo_made.at(U - 2 + t, it))
                else:
                    pe.wait_ge(y_added.sem, y_added.at(t - 2, it))
                pe.wait_ge(o_lo_made.sem, o_lo_made.at(HG - 1, it))
                rows = slice(t * P, (t + 1) * P)
                for h in range(HG):
                    ins = three_pass(pe, p_t[t % 2][:, :], o_hi[:, h, rows], o_lo[:, h, rows],
                                     wo_hi[:, h, :], wo_lo[:, h, :], h == 0, h == HG - 1)
                ins.then_inc(y_made.sem, 1)

            def start(it, b):
                query(it, b, 0)
                square_sums(it, 0)
                for u in range(3):
                    scores(it, b, u)

            def body(it, b, last):
                for u in range(U):
                    if u in QUERY_AT:
                        query(it, b, QUERY_AT[u])
                    turn(it, u)
                    if u in SUMS_AT:
                        square_sums(it, SUMS_AT[u])
                    if u + 3 < U:
                        scores(it, b, u + 3)
                    if u % 2 == 1 and u >= 3:
                        weigh_values(it, (u - 3) // 2)
                if last:
                    weigh_values(it, 2 * HG - 1)
                else:
                    query(it + 1, b + 1, 0)
                    weigh_values(it, 2 * HG - 1)
                    square_sums(it + 1, 0)
                    for u in range(3):
                        scores(it + 1, b + 1, u)
                for t in range(TT):
                    project(it, t)

            with pe.Fori(0, G) as g:
                pe.wait_ge(w_lo.sem, w_lo.at(0, g))
                pe.wait_ge(w_lo.sem, w_lo.at(1, g))
                batches(pe, g, lambda it: start(it, 0), body)


def stage_router(K, gate_t, lora_a, lora_b_t):
    with ExitStack() as ctx:
        sb, ps = K.scope(ctx)
        g_raw, g_full = sb("g_raw", [P, KT, E]), sb("g_full", [P, KT, E])
        a_raw, b_raw = sb("ga_raw", [R, D]), sb("gb_raw", [R, E])
        g_hi, g_lo = sb("g_hi", [P, KT, P], F32R), sb("g_lo", [P, KT, P], F32R)
        flat = sb("r_logits_t", [E, B * S])
        logit = sb("r_logits", [P, T, E])
        prob = sb("r_prob", [P, T, E])
        most, total, inv = sb("r_max", [P, T]), sb("r_total", [P, T]), sb("r_inv", [P, T])
        top = sb("r_top", [P, T, 8])
        index = sb("r_index", [P, T, 8], U32)
        place = sb("r_place", [P, T, 2])
        number_i, number = sb("r_number_i", [P, E], mybir.dt.int32), sb("r_number", [P, E])
        mask, other = sb("r_mask", [P, T, E]), sb("r_other", [P, T, E])
        p_g = ps("p_g")
        p_l = [ps(f"p_l{b}") for b in range(B)]
        p_t = ps("r_pt")

        loaded = Signal(K, "r_loaded", unit=16)
        zeroed = Signal(K, "r_zeroed")
        numbered = Signal(K, "r_numbered")
        delta_made = Signal(K, "r_delta")
        gate_made = Signal(K, "r_gate_split")
        logits_made = Signal(K, "r_logits_made")
        logits_read = Signal(K, "r_logits_read")
        turned = Signal(K, "r_transposed")
        shifted = Signal(K, "r_shifted")
        exp_made = Signal(K, "r_exp")
        steps = Signal(K, "r_vector_steps")
        block = ctx.enter_context(K.nc.Block())

        @block.sync
        def _(sp):
            sp.dma_start(g_raw[:, :, :], gate_t.rearrange("(k p) e -> p k e", p=P)).then_inc(loaded.sem, 16)
            sp.dma_start(a_raw[:, :], lora_a).then_inc(loaded.sem, 16)
            sp.dma_start(b_raw[:, :], lora_b_t).then_inc(loaded.sem, 16)

        @block.gpsimd
        def _(pool):
            pool.memset(f32(g_hi[:, :, :]), 0.0).then_inc(zeroed.sem, 1)
            pool.memset(f32(g_lo[:, :, :]), 0.0).then_inc(zeroed.sem, 1)
            pool.iota(number_i[:, :], pattern=[[1, E]], base=0, channel_multiplier=0).then_inc(numbered.sem, 1)

        @block.tensor
        def _(pe):
            pe.wait_ge(loaded.sem, loaded.at(2))
            for k in range(KT):
                ins = pe.matmul(p_g[:, k * E:(k + 1) * E], a_raw[:, k * P:(k + 1) * P], b_raw[:, :],
                                start=True, stop=True)
            ins.then_inc(delta_made.sem, 1)
            pe.wait_ge(gate_made.sem, gate_made.at(1))
            for b in range(B):
                cols = slice(b * S, (b + 1) * S)
                for k in range(KT):
                    ins = three_pass(pe, p_l[b][:, :], g_hi[:, k, :], g_lo[:, k, :],
                                     K.xt_hi[:, k, cols], K.xt_lo[:, k, cols], k == 0, k == KT - 1)
                ins.then_inc(logits_made.sem, 1)
            for t in range(T):
                if t % TT == 0:
                    pe.wait_ge(logits_read.sem, logits_read.at(t // TT))
                ins = pe.transpose(p_t[:, t * E:(t + 1) * E], flat[:, t * P:(t + 1) * P], K.ident[0:E, 0:E])
            ins.then_inc(turned.sem, 1)

        @block.scalar
        def _(act):
            for b in range(B):
                act.wait_ge(logits_made.sem, logits_made.at(b))
                act.activation(flat[:, b * S:(b + 1) * S], p_l[b][0:E, :], ACT.Copy).then_inc(logits_read.sem, 1)
            act.wait_ge(shifted.sem, shifted.at(0))
            act.activation(prob[:, :, :], logit[:, :, :], ACT.Exp).then_inc(exp_made.sem, 1)

        @block.vector
        def _(dve):
            step = Count(steps)

            def over(ap, shape=(P, T, E)):
                return ap.to_broadcast(list(shape))

            dve.wait_ge(loaded.sem, loaded.at(2))
            dve.wait_ge(delta_made.sem, delta_made.at(0))
            dve.scalar_tensor_tensor(g_full[:, :, :], p_g[:, 0:KT * E].rearrange("p (k e) -> p k e", k=KT),
                                     2.0, g_raw[:, :, :], ALU.mult, ALU.add).then_inc(step.sem, 1)
            dve.wait_ge(step.sem, step.next())
            dve.wait_ge(zeroed.sem, zeroed.at(1))
            dve.tensor_copy(g_hi[:, :, 0:E], g_full[:, :, :]).then_inc(gate_made.sem, 1)
            dve.wait_ge(gate_made.sem, gate_made.at(0))
            dve.tensor_tensor(g_lo[:, :, 0:E], g_full[:, :, :], f32(g_hi[:, :, 0:E]),
                              ALU.subtract).then_inc(gate_made.sem, 1)
            dve.wait_ge(numbered.sem, numbered.at(0))
            dve.tensor_copy(number[:, :], number_i[:, :]).then_inc(step.sem, 1)
            dve.wait_ge(step.sem, step.next())
            dve.wait_ge(turned.sem, turned.at(0))
            dve.tensor_copy(logit[:, :, :],
                            p_t[:, 0:T * E].rearrange("p (t e) -> p t e", t=T)).then_inc(step.sem, 1)
            dve.wait_ge(step.sem, step.next())
            dve.tensor_reduce(most[:, :], logit[:, :, :], AX.X, ALU.max).then_inc(step.sem, 1)
            dve.wait_ge(step.sem, step.next())
            dve.tensor_tensor(logit[:, :, :], logit[:, :, :], over(most[:, :].unsqueeze(2)),
                              ALU.subtract).then_inc(shifted.sem, 1)
            dve.wait_ge(exp_made.sem, exp_made.at(0))
            dve.tensor_reduce(total[:, :], prob[:, :, :], AX.X, ALU.add).then_inc(step.sem, 1)
            dve.wait_ge(step.sem, step.next())
            dve.reciprocal(inv[:, :], total[:, :]).then_inc(step.sem, 1)
            dve.wait_ge(step.sem, step.next())
            dve.tensor_tensor(prob[:, :, :], prob[:, :, :], over(inv[:, :].unsqueeze(2)),
                              ALU.mult).then_inc(step.sem, 1)
            dve.wait_ge(step.sem, step.next())
            for t in range(T):
                ins = dve.max(top[:, t, :], prob[:, t, :])
            ins.then_inc(step.sem, 1)
            dve.wait_ge(step.sem, step.next())
            for t in range(T):
                ins = dve.max_index(index[:, t, :], top[:, t, :], prob[:, t, :])
            ins.then_inc(step.sem, 1)
            dve.wait_ge(step.sem, step.next())
            dve.tensor_copy(place[:, :, :], index[:, :, 0:2]).then_inc(step.sem, 1)
            dve.wait_ge(step.sem, step.next())
            every = number[:, :].unsqueeze(1).to_broadcast([P, T, E])
            dve.tensor_tensor(mask[:, :, :], every, over(place[:, :, 0:1]), ALU.is_equal)
            dve.tensor_tensor(other[:, :, :], every, over(place[:, :, 1:2]), ALU.is_equal).then_inc(step.sem, 1)
            dve.wait_ge(step.sem, step.next())
            dve.tensor_tensor(mask[:, :, :], mask[:, :, :], other[:, :, :], ALU.add).then_inc(step.sem, 1)
            dve.wait_ge(step.sem, step.next())
            dve.tensor_tensor(total[:, :], top[:, :, 0], top[:, :, 1], ALU.add).then_inc(step.sem, 1)
            dve.wait_ge(step.sem, step.next())
            dve.reciprocal(inv[:, :], total[:, :]).then_inc(step.sem, 1)
            dve.wait_ge(step.sem, step.next())
            dve.tensor_scalar(inv[:, :], inv[:, :], K.gates[:, 3:4], None, ALU.mult).then_inc(step.sem, 1)
            dve.wait_ge(step.sem, step.next())
            dve.tensor_tensor(mask[:, :, :], mask[:, :, :], prob[:, :, :], ALU.mult).then_inc(step.sem, 1)
            dve.wait_ge(step.sem, step.next())
            dve.tensor_tensor(K.route[:, :, :], mask[:, :, :], over(inv[:, :].unsqueeze(2)),
                              ALU.mult).then_inc(step.sem, 1)
            dve.wait_ge(step.sem, step.next())


def stage_experts(K, gup, down, gup_a, gup_b_t, down_a, down_b_t):
    with ExitStack() as ctx:
        sb, ps = K.scope(ctx)
        IT = I // P
        NC = KT + IT
        LR = 3 * 32
        w_raw = sb("e_w_raw", [P, NC, D])
        la_raw, lb_raw = sb("la_raw", [LR, D + I]), sb("lb_raw", [LR, 2 * D])
        la, lb = sb("la", [LR, D + I], F32R), sb("lb", [LR, 2 * D], F32R)
        w_hi, w_lo = sb("e_w_hi", [P, 2, NC, D], F32R), sb("e_w_lo", [P, 2, NC, D], F32R)
        silu = sb("e_silu", [P, IT, S])
        h_full = sb("e_h", [P, IT, S])
        h_hi, h_lo = sb("e_h_hi", [P, IT, S], F32R), sb("e_h_lo", [P, IT, S], F32R)
        p_h = [ps(f"e_h{n}") for n in range(3)]
        p_d = ps("e_d")
        p_y = [ps(f"e_y{t}") for t in range(TT)]
        H_BANK = [0, 1, 2, 0]

        raw_in = Signal(K, "e_weights_in", per=14, unit=16)
        zeroed = Signal(K, "e_zeroed")
        lora_hi = Signal(K, "e_lora_hi", per=2, credit=2)
        lora_lo = Signal(K, "e_lora_lo", per=2)
        delta_made = Signal(K, "e_delta", per=NC, credit=NC)
        merged = Signal(K, "e_merged", per=NC, credit=1)
        hi_made = Signal(K, "e_weights_hi", per=NC)
        lo_made = Signal(K, "e_weights_lo", per=NC, credit=1)
        h_made = Signal(K, "e_h_product", per=4 * B)
        silu_made = Signal(K, "e_silu_made", per=IT * B, credit=IT)
        h_full_made = Signal(K, "e_h_made", per=IT * B, credit=IT)
        h_hi_made = Signal(K, "e_h_hi_made", per=IT * B)
        h_lo_made = Signal(K, "e_h_lo_made", per=IT * B, credit=IT)
        y_made = Signal(K, "e_product", per=TT * B, credit=TT)
        y_added = Signal(K, "e_added", per=TT * B, credit=TT)
        block = ctx.enter_context(K.nc.Block())
        chunks_at = [[0, 1], [2, 3], [4, 5], []]

        def experts(eng, prepare, run):
            prepare(0, 0)
            with eng.Fori(0, E // 2 - 1) as i:
                for u in range(2):
                    run(i * 2 + u, u, True)
            run(E - 2, 0, True)
            run(E - 1, 1, False)

        def lora_rows(c):
            return slice(c * P, (c + 1) * P), slice(0, D) if c < KT else slice(D, 2 * D)

        @block.sync
        def _(sp):
            def load(e):
                at = slice(e, e + 1) if isinstance(e, int) else bass.ds(e, 1)
                sp.dma_start(w_raw[:, 0:KT, :],
                             gup[at].rearrange("a (k p) n -> p (a k) n", p=P)).then_inc(raw_in.sem, 16)
                sp.dma_start(w_raw[:, KT:NC, :],
                             down[at].rearrange("a (k p) n -> p (a k) n", p=P)).then_inc(raw_in.sem, 16)
                for s in range(3):
                    rows = slice(32 * s, 32 * s + R)
                    for dst, src in ((la_raw[rows, 0:D], gup_a), (la_raw[rows, D:D + I], down_a),
                                     (lb_raw[rows, 0:D], gup_b_t), (lb_raw[rows, D:2 * D], down_b_t)):
                        sp.dma_start(dst, src[at].rearrange("a r n -> (a r) n")).then_inc(raw_in.sem, 16)

            sp.wait_ge(zeroed.sem, zeroed.at(1))
            load(0)
            with sp.Fori(1, E) as e:
                sp.wait_ge(lo_made.sem, lo_made.at(-1, e))
                sp.sem_inc(K.apart, 1)
                sp.wait_ge(delta_made.sem, delta_made.at(-1, e))
                sp.sem_inc(K.apart, 1)
                load(e)

        @block.gpsimd
        def _(pool):
            pool.memset(la_raw[:, :], 0.0).then_inc(zeroed.sem, 1)
            pool.memset(lb_raw[:, :], 0.0).then_inc(zeroed.sem, 1)

        @block.scalar
        def _(act):
            act.sem_inc(silu_made.sem, silu_made.opening)
            act.sem_inc(lora_hi.sem, lora_hi.opening)

            def lora(e):
                act.wait_ge(raw_in.sem, raw_in.at(raw_in.per - 1, e))
                act.wait_ge(delta_made.sem, delta_made.at(-1, e))
                act.activation(la[:, :], la_raw[:, :], ACT.Copy).then_inc(lora_hi.sem, 1)
                act.activation(lb[:, :], lb_raw[:, :], ACT.Copy).then_inc(lora_hi.sem, 1)

            def chunk(e, u, c):
                act.wait_ge(merged.sem, merged.at(c, e))
                act.activation(w_hi[:, u, c, :], w_raw[:, c, :], ACT.Copy).then_inc(hi_made.sem, 1)

            def prepare(e, u):
                lora(e)
                for c in range(NC):
                    chunk(e, u, c)

            def run(e, u, more):
                for b in range(B):
                    if more and b == 0:
                        lora(e + 1)
                    for n in range(IT):
                        act.wait_ge(h_made.sem, h_made.at(4 * b + 2 * n, e))
                        act.wait_ge(h_full_made.sem, h_full_made.at(IT * (b - 1) + n, e))
                        act.activation(silu[:, n, :], p_h[H_BANK[2 * n]][:, :],
                                       ACT.Silu).then_inc(silu_made.sem, 1)
                        act.wait_ge(h_full_made.sem, h_full_made.at(IT * b + n, e))
                        if n == 0:
                            act.wait_ge(y_made.sem, y_made.at(TT * b - 1, e))
                        act.activation(h_hi[:, n, :], h_full[:, n, :], ACT.Copy).then_inc(h_hi_made.sem, 1)
                    if more:
                        for c in chunks_at[b]:
                            chunk(e + 1, 1 - u, c)

            experts(act, prepare, run)

        @block.vector
        def _(dve):
            for s in (merged, lo_made, h_full_made, h_lo_made, y_added):
                dve.sem_inc(s.sem, s.opening)

            def lora(e):
                dve.wait_ge(lora_hi.sem, lora_hi.at(1, e))
                rows = slice(64, 64 + 32)
                dve.tensor_tensor(la[rows, :], la_raw[rows, :], f32(la[rows, :]),
                                  ALU.subtract).then_inc(lora_lo.sem, 1)
                rows = slice(32, 32 + 32)
                dve.tensor_tensor(lb[rows, :], lb_raw[rows, :], f32(lb[rows, :]),
                                  ALU.subtract).then_inc(lora_lo.sem, 1)

            def merge(e, c):
                dve.wait_ge(delta_made.sem, delta_made.at(c, e))
                dve.scalar_tensor_tensor(w_raw[:, c, :], p_d[:, :], 2.0, w_raw[:, c, :],
                                         ALU.mult, ALU.add).then_inc(merged.sem, 1)

            def split(e, u, c):
                dve.wait_ge(hi_made.sem, hi_made.at(c, e))
                dve.tensor_tensor(w_lo[:, u, c, :], w_raw[:, c, :], f32(w_hi[:, u, c, :]),
                                  ALU.subtract).then_inc(lo_made.sem, 1)

            def prepare(e, u):
                lora(e)
                for c in range(NC):
                    merge(e, c)
                    split(e, u, c)

            def run(e, u, more):
                for b in range(B):
                    if more and b == 0:
                        lora(e + 1)
                    chunks = chunks_at[b] if more else []
                    for n in range(IT):
                        dve.wait_ge(h_made.sem, h_made.at(4 * b + 2 * n + 1, e))
                        dve.wait_ge(silu_made.sem, silu_made.at(IT * b + n, e))
                        dve.tensor_tensor(h_full[:, n, :], p_h[H_BANK[2 * n + 1]][:, :],
                                          silu[:, n, :], ALU.mult).then_inc(h_full_made.sem, 1)
                        if n < len(chunks):
                            merge(e + 1, chunks[n])
                        dve.wait_ge(h_hi_made.sem, h_hi_made.at(IT * b + n, e))
                        dve.tensor_tensor(h_lo[:, n, :], h_full[:, n, :], f32(h_hi[:, n, :]),
                                          ALU.subtract).then_inc(h_lo_made.sem, 1)
                    for t in range(TT):
                        dve.wait_ge(y_made.sem, y_made.at(TT * b + t, e))
                        route = K.route[:, b * TT + t, bass.ds(e, 1) if not isinstance(e, int)
                                        else slice(e, e + 1)]
                        dve.scalar_tensor_tensor(K.x[:, b * TT + t, :], p_y[t][:, :], route,
                                                 K.x[:, b * TT + t, :], ALU.mult, ALU.add).then_inc(y_added.sem, 1)
                        if t < len(chunks):
                            split(e + 1, 1 - u, chunks[t])

            experts(dve, prepare, run)

        @block.tensor
        def _(pe):
            pe.sem_inc(delta_made.sem, delta_made.opening)
            pe.sem_inc(y_made.sem, y_made.opening)

            def delta(e, c):
                if c == 0:
                    pe.wait_ge(lora_lo.sem, lora_lo.at(1, e))
                pe.wait_ge(merged.sem, merged.at(c - 1, e))
                rows, cols = lora_rows(c)
                pe.matmul(p_d[:, :], la[:, rows], lb[:, cols], start=True, stop=True).then_inc(delta_made.sem, 1)

            def prepare(e, u):
                for c in range(NC):
                    delta(e, c)

            def hidden(e, u, b, n, half):
                m = 2 * n + half
                if m == 0:
                    pe.wait_ge(h_full_made.sem, h_full_made.at(IT * b - 1, e))
                elif m == 3:
                    pe.wait_ge(silu_made.sem, silu_made.at(IT * b, e))
                elif m == 1:
                    pe.wait_ge(h_full_made.sem, h_full_made.at(IT * (b - 1), e))
                else:
                    pe.wait_ge(silu_made.sem, silu_made.at(IT * (b - 1) + 1, e))
                rows = slice(half * I + n * P, half * I + (n + 1) * P)
                cols = slice(b * S, (b + 1) * S)
                for k in range(KT):
                    ins = three_pass(pe, p_h[H_BANK[m]][:, :], w_hi[:, u, k, rows], w_lo[:, u, k, rows],
                                     K.xt_hi[:, k, cols], K.xt_lo[:, k, cols], k == 0, k == KT - 1)
                ins.then_inc(h_made.sem, 1)

            def output(e, u, b, n):
                pe.wait_ge(h_lo_made.sem, h_lo_made.at(IT * b + n, e))
                for t in range(TT):
                    if n == 0:
                        pe.wait_ge(y_added.sem, y_added.at(TT * (b - 1) + t, e))
                    rows = slice(t * P, (t + 1) * P)
                    ins = three_pass(pe, p_y[t][:, :], h_hi[:, n, rows], h_lo[:, n, rows],
                                     w_hi[:, u, KT + n, :], w_lo[:, u, KT + n, :], n == 0, n == IT - 1)
                    if n == IT - 1:
                        ins.then_inc(y_made.sem, 1)

            def run(e, u, more):
                pe.wait_ge(lo_made.sem, lo_made.at(NC - 1, e))
                for b in range(B):
                    chunks = chunks_at[b] if more else []
                    for n in range(IT):
                        for half in range(2):
                            hidden(e, u, b, n, half)
                        if n < len(chunks):
                            delta(e + 1, chunks[n])
                    for n in range(IT):
                        output(e, u, b, n)

            experts(pe, prepare, run)


def stage_store(K, out):
    with ExitStack() as ctx:
        stored = Signal(K, "result_stored", unit=16)
        block = ctx.enter_context(K.nc.Block())

        @block.sync
        def _(sp):
            sp.dma_start(out.rearrange("(t p) d -> p t d", p=P), K.x[:, :, :]).then_inc(stored.sem, 16)
            sp.wait_ge(stored.sem, stored.at(0))


def flamingo_kernel(nc, a, out, stages=9):
    keys = nc.dram_tensor("keys_split", (B, P, 2, G, S), F32, kind="Internal").ap()
    values = nc.dram_tensor("values_split", (B, P, 2, TT, G * DH), F32, kind="Internal").ap()
    with ExitStack() as ctx:
        K = Kernel(nc, ctx)
        sb, _ = K.scope(ctx)
        K.x = sb("x", [P, T, D])
        K.ident = sb("ident", [P, P])
        K.power = sb("power", [P, 16])
        K.gates_raw, K.gates = sb("gates_raw", [P, 4]), sb("gates", [P, 4])
        K.ln_eps = sb("ln_eps", [P, TT])
        K.gates_made = Signal(K, "gates_made")
        K.apart = ctx.enter_context(nc.semaphore("wait_stands_alone"))
        stage_context(K, a["x"], a["ctx_t"], a["L1_xattn_Wk"], a["L1_xattn_Wv"], a["L1_xattn_k_norm_w"],
                      a["g_xattn"], a["g_ffn"], keys, values)
        if stages >= 2:
            K.xt_hi, K.xt_lo = sb("xt_hi", [P, KT, B * S], F32R), sb("xt_lo", [P, KT, B * S], F32R)
            stage_norm(K, "n1")
            stage_ffn(K, a["w1_t"], a["w2_t"], a["b1_t"], a["L0_ffn_b2"])
        if stages >= 3:
            stage_norm(K, "n2")
            stage_attention(K, a["L1_xattn_Wq"], a["L1_xattn_Wo"], a["L1_xattn_q_norm_w"], keys, values)
        if stages >= 4:
            K.route = sb("route", [P, T, E])
            stage_norm(K, "n3")
            stage_router(K, a["gate_t"], a["L1_ffn_gate_lora_A"], a["gate_b_t"])
            stage_experts(K, a["L1_ffn_gate_up_proj"], a["L1_ffn_down_proj"], a["L1_ffn_gup_lora_A"],
                          a["gup_b_t"], a["L1_ffn_down_lora_A"], a["down_b_t"])
        stage_store(K, out)


def kernel(**inputs):
    import numpy as np
    import concourse.bacc as bacc
    from concourse.bass_utils import run_bass_kernel_spmd

    given = {k: np.asarray(v) for k, v in inputs.items()}
    turned = {
        "x": given["x"].reshape(B * S, D),
        "ctx_t": given["ctx_2048"].transpose(0, 2, 1),
        "w1_t": given["L0_ffn_w1"].T,
        "w2_t": given["L0_ffn_w2"].T,
        "b1_t": given["L0_ffn_b1"].reshape(FT, P).T,
        "gate_t": given["L1_ffn_gate_weight"].T,
        "gate_b_t": given["L1_ffn_gate_lora_B"].T,
        "gup_b_t": given["L1_ffn_gup_lora_B"].transpose(0, 2, 1),
        "down_b_t": given["L1_ffn_down_lora_B"].transpose(0, 2, 1),
    }
    same = ["g_xattn", "g_ffn", "L0_ffn_b2", "L1_xattn_Wq", "L1_xattn_Wk", "L1_xattn_Wv",
            "L1_xattn_Wo", "L1_xattn_q_norm_w", "L1_xattn_k_norm_w", "L1_ffn_gate_lora_A",
            "L1_ffn_gate_up_proj", "L1_ffn_down_proj", "L1_ffn_gup_lora_A", "L1_ffn_down_lora_A"]
    nc = bacc.Bacc("TRN2", target_bir_lowering=False, num_devices=1)
    arrays, aps = {}, {}
    for name, a in [*turned.items(), *((n, given[n]) for n in same)]:
        arrays[f"in_{name}"] = np.ascontiguousarray(a)
        aps[name] = nc.dram_tensor(f"in_{name}", a.shape, mybir.dt.from_np(a.dtype), kind="ExternalInput").ap()
    out = nc.dram_tensor("out", (B * S, D), F32, kind="ExternalOutput").ap()
    flamingo_kernel(nc, aps, out)
    r = run_bass_kernel_spmd(nc, [arrays], core_ids=[0])
    return r.results[0]["out"].reshape(B, S, D)
```

```python
from contextlib import ExitStack

import concourse.bass as bass
from concourse import mybir

F32 = mybir.dt.float32
F32R = mybir.dt.float32r
U32 = mybir.dt.uint32
ALU = mybir.AluOpType
ACT = mybir.ActivationFunctionType
AX = mybir.AxisListType

P = 128
B, S, D = 4, 512, 512
KT = D // P
TT = S // P
T = B * TT
F = 2048
FT = F // P
NH, G, DH = 16, 4, 128
HG = NH // G
E, I, R = 8, 256, 16
LN_EPS, RMS_EPS = 1e-5, 1e-6
FP8_MAX = 448.0
ACT_EPS, W_EPS = 1e-4, 1e-6
EXPONENT = 0x7F800000
FP8_LEAST = 2.0 ** -6
FP8_SHIFT = 1.5 * 2.0 ** 20


class Signal:

    def __init__(self, K, name, per=1, credit=0, unit=1):
        self.sem = K.ctx.enter_context(K.nc.semaphore(name))
        self.per, self.credit, self.unit = per, credit, unit
        self.opening = credit * unit

    def at(self, n, i=0):
        assert not isinstance(i, int) or self.credit + i * self.per + n >= 0
        return i * (self.per * self.unit) + (self.credit + n + 1) * self.unit

    def given(self, n, i):
        return not isinstance(i, int) or i * self.per + n >= 0


class Count:

    def __init__(self, signal, i=0):
        self.sem, self.signals, self.i, self.n = signal.sem, signal, i, 0

    def next(self):
        self.n += 1
        return self.signals.at(self.n - 1, self.i)


class Kernel:

    def __init__(self, nc, ctx):
        self.nc, self.ctx = nc, ctx

    def scope(self, ctx):
        nc = self.nc

        def sb(name, shape, dt=F32):
            return ctx.enter_context(nc.sbuf_tensor(name, shape, dt))

        def ps(name, shape=(P, 512)):
            return ctx.enter_context(nc.psum_tensor(name, list(shape), F32))

        return sb, ps


def three_pass(pe, out, lhs_hi, lhs_lo, rhs_hi, rhs_lo, start, stop):
    pe.matmul(out, lhs_hi, rhs_hi, start=start, stop=False)
    pe.matmul(out, lhs_hi, rhs_lo, start=False, stop=False)
    return pe.matmul(out, lhs_lo, rhs_hi, start=False, stop=stop)


def f32(ap):
    return ap.bitcast(F32)


def layer_norm_stats(dve, x, stats, mv, step, apart):
    for t in range(TT):
        ins = dve.bn_stats(stats[:, t, :], x[:, t, :])
    ins.then_inc(step.sem, 1)
    dve.wait_ge(step.sem, step.next())
    dve.sem_inc(apart, 1)
    for t in range(TT):
        ins = dve.bn_aggr(mv[:, t, :], stats[:, t, :])
    return ins


def quantise(dve, step, v, scale, least, grid, out_scale, safe, amax):
    dve.tensor_scalar(safe, amax, least, None, ALU.max).then_inc(step.sem, 1)
    dve.wait_ge(step.sem, step.next())
    dve.reciprocal(scale, safe).then_inc(step.sem, 1)
    dve.wait_ge(step.sem, step.next())
    dve.tensor_scalar(scale, scale, FP8_MAX, None, ALU.mult).then_inc(step.sem, 1)
    dve.wait_ge(step.sem, step.next())
    dve.tensor_scalar(out_scale, safe, 1.0 / FP8_MAX, None, ALU.mult)
    n = v.shape[1]
    dve.tensor_tensor(v, v, scale.unsqueeze(2).to_broadcast([P, n, P]), ALU.mult).then_inc(step.sem, 1)
    dve.wait_ge(step.sem, step.next())
    dve.tensor_scalar(grid.bitcast(U32), v.bitcast(U32), EXPONENT, None, ALU.bitwise_and).then_inc(step.sem, 1)
    dve.wait_ge(step.sem, step.next())
    dve.tensor_scalar(grid, grid, FP8_LEAST, FP8_SHIFT, ALU.max, ALU.mult).then_inc(step.sem, 1)
    dve.wait_ge(step.sem, step.next())
    dve.tensor_tensor(v, v, grid, ALU.add).then_inc(step.sem, 1)
    dve.wait_ge(step.sem, step.next())
    dve.tensor_tensor(v, v, grid, ALU.subtract).then_inc(step.sem, 1)
    dve.wait_ge(step.sem, step.next())
    return dve.tensor_tensor(v, v, out_scale.unsqueeze(2).to_broadcast([P, n, P]), ALU.mult)


def stage_context(K, x, ctx_t, wk, wv, k_norm_w, g_xattn, g_ffn, keys, values):
    nc = K.nc
    with ExitStack() as ctx:
        sb, ps = K.scope(ctx)
        w_raw = sb("c_w_raw", [P, KT, D])
        wk_hi, wk_lo = sb("wk_hi", [P, KT, D], F32R), sb("wk_lo", [P, KT, D], F32R)
        wv_hi, wv_lo = sb("wv_hi", [P, KT, D], F32R), sb("wv_lo", [P, KT, D], F32R)
        c_raw = sb("c_raw", [P, KT, S])
        c_hi, c_lo = sb("c_hi", [P, KT, S], F32R), sb("c_lo", [P, KT, S], F32R)
        cq_hi, cq_lo = sb("cq_hi", [P, KT, S], F32R), sb("cq_lo", [P, KT, S], F32R)
        grid = sb("grid", [P, KT * 4, P])
        xn = sb("c_xn", [P, TT, D])
        xq_hi, xq_lo = sb("xq_hi", [P, KT, S], F32R), sb("xq_lo", [P, KT, S], F32R)
        k_out = sb("k_out", [P, 2, G, S], F32R)
        v_out = sb("v_out", [P, TT, 2, G * DH], F32R)
        v_full = sb("v_full", [P, 2, G * DH])
        k_sq = sb("k_sq", [P, 2, G * DH])
        k_ms = sb("k_ms", [P, 2, G])
        k_eps = sb("k_eps", [P, 2, G])
        k_rstd = sb("k_rstd", [P, 2, G])
        k_nrm = sb("k_nrm", [P, 2, G * DH])
        k_full = sb("k_full", [P, 2, G * P])
        kw = sb("kw", [P, 1])
        blocks = [sb(f"q_{n}", [P, KT * 4]) for n in ("amax", "amax_all", "safe", "scale", "back", "x_amax",
                                                       "x_safe", "x_scale", "x_back")]
        amax, amax_all, safe, scale, back, x_amax, x_safe, x_scale, x_back = (t[:, :] for t in blocks)
        stats = sb("c_stats", [P, TT, 6])
        mv = sb("c_mv", [P, TT, 2])
        veps = sb("c_veps", [P, TT])
        rstd = sb("c_rstd", [P, TT])

        p_key = [ps(f"p_key{n}") for n in range(2)]
        p_val = [ps(f"p_val{n}") for n in range(2)]
        p_kt = ps("p_kt")
        p_xt = [ps(f"p_xt{n}") for n in range(2)]
        p_y = ps("p_y")

        w_in = [Signal(K, f"c_weight{n}_in", unit=16) for n in range(2)]
        gates_in = Signal(K, "c_gates_in", unit=16)
        kw_in = Signal(K, "c_key_norm_in", unit=16)
        ctx_in = Signal(K, "c_context_in", unit=16)
        x_in = Signal(K, "c_x_in", unit=16)
        w_hi = Signal(K, "c_weight_hi")
        w_lo = Signal(K, "c_weight_lo")
        ident_made = Signal(K, "c_ident_made")
        ctx_hi = Signal(K, "c_context_hi")
        ctx_lo = Signal(K, "c_context_lo")
        ctx_amax = Signal(K, "c_context_amax")
        ctx_amax_all = Signal(K, "c_context_amax_all")
        ctx_quant = Signal(K, "c_context_quantised")
        cq_hi_made = Signal(K, "c_cq_hi", credit=1)
        cq_lo_made = Signal(K, "c_cq_lo", credit=1)
        x_var = Signal(K, "c_x_variance")
        x_rstd = Signal(K, "c_x_rstd")
        x_quant = Signal(K, "c_x_quantised")
        key_made = Signal(K, "c_key_product", per=TT, credit=1)
        val_made = Signal(K, "c_value_product", per=TT, credit=1)
        val_copied = Signal(K, "c_value_copied", per=TT, credit=2)
        val_lo = Signal(K, "c_value_lo", per=TT, credit=2)
        key_sq = Signal(K, "c_key_squares", per=TT)
        key_rstd = Signal(K, "c_key_rstd", per=TT, credit=2)
        key_nrm = Signal(K, "c_key_normalised", per=TT, credit=2)
        key_turned = Signal(K, "c_key_transposed", per=TT, credit=2)
        key_full = Signal(K, "c_key_full", per=TT, credit=1)
        key_hi = Signal(K, "c_key_hi", per=TT)
        key_lo = Signal(K, "c_key_lo", per=TT, credit=2)
        kv_out = Signal(K, "c_kv_stored", per=2, credit=2, unit=16)
        x_turned = Signal(K, "c_x_transposed", per=KT, credit=1)
        xq_hi_made = Signal(K, "c_xq_hi", per=KT)
        xq_lo_made = Signal(K, "c_xq_lo", per=KT, credit=2)
        y_made = Signal(K, "c_product", per=TT, credit=1)
        y_added = Signal(K, "c_added", per=TT, credit=1)
        v_steps = Signal(K, "c_vector_steps", per=19)
        p_steps = Signal(K, "c_pool_steps", per=1 + TT)
        block = ctx.enter_context(nc.Block())

        @block.sync
        def _(sp):
            sp.sem_inc(kv_out.sem, kv_out.opening)
            sp.dma_start(w_raw[:, :, :], wk.rearrange("(k p) n -> p k n", p=P)).then_inc(w_in[0].sem, 16)
            sp.dma_start(K.gates_raw[:, 0:2], g_xattn.partition_broadcast(P)).then_inc(gates_in.sem, 16)
            sp.dma_start(K.gates_raw[:, 2:4], g_ffn.partition_broadcast(P)).then_inc(gates_in.sem, 16)
            sp.dma_start(kw[:, :], k_norm_w.rearrange("(p a) -> p a", a=1)).then_inc(kw_in.sem, 16)
            sp.wait_ge(w_lo.sem, w_lo.at(0))
            sp.dma_start(w_raw[:, :, :], wv.rearrange("(k p) n -> p k n", p=P)).then_inc(w_in[1].sem, 16)
            with sp.Fori(0, B) as b:
                sp.wait_ge(cq_lo_made.sem, cq_lo_made.at(-1, b))
                sp.sem_inc(K.apart, 1)
                sp.wait_ge(cq_hi_made.sem, cq_hi_made.at(-1, b))
                sp.sem_inc(K.apart, 1)
                sp.dma_start(c_raw[:, :, :],
                             ctx_t[bass.ds(b, 1)].rearrange("a (k p) n -> p (a k) n",
                                                            p=P)).then_inc(ctx_in.sem, 16)
                sp.dma_start(K.x[:, bass.ds(b * TT, TT), :],
                             x[bass.ds(b * S, S), :].rearrange("(t p) d -> p t d", p=P)).then_inc(x_in.sem, 16)
                sp.wait_ge(key_lo.sem, key_lo.at(TT - 1, b))
                sp.sem_inc(K.apart, 1)
                sp.wait_ge(val_lo.sem, val_lo.at(TT - 1, b))
                sp.sem_inc(K.apart, 1)
                sp.dma_start(keys[bass.ds(b, 1)].rearrange("a p h g n -> p (a h) g n"),
                             f32(k_out[:, :, :, :])).then_inc(kv_out.sem, 16)
                sp.dma_start(values[bass.ds(b, 1)].rearrange("a p t h n -> p (a t) h n"),
                             f32(v_out[:, :, :, :])).then_inc(kv_out.sem, 16)
            sp.wait_ge(kv_out.sem, kv_out.at(1, B - 1))

        @block.scalar
        def _(act):
            for s in (cq_hi_made, val_copied, key_nrm, key_full):
                act.sem_inc(s.sem, s.opening)
            for n, hi in enumerate((wk_hi, wv_hi)):
                act.wait_ge(w_in[n].sem, w_in[n].at(0))
                act.activation(hi[:, :, :], w_raw[:, :, :], ACT.Copy).then_inc(w_hi.sem, 1)
            act.wait_ge(gates_in.sem, gates_in.at(1))
            act.activation(K.gates[:, :], K.gates_raw[:, :], ACT.Tanh).then_inc(K.gates_made.sem, 1)
            act.wait_ge(kw_in.sem, kw_in.at(0))
            with act.Fori(0, B) as b:
                act.wait_ge(ctx_in.sem, ctx_in.at(0, b))
                act.wait_ge(val_made.sem, val_made.at(-1, b))
                act.activation(c_hi[:, :, :], c_raw[:, :, :], ACT.Copy).then_inc(ctx_hi.sem, 1)

                def values_and_squares(j):
                    act.wait_ge(val_made.sem, val_made.at(j, b))
                    if j == 0:
                        act.wait_ge(kv_out.sem, kv_out.at(-1, b))
                    act.wait_ge(val_lo.sem, val_lo.at(j - 2, b))
                    act.activation(v_out[:, j, 0, :], p_val[j % 2][:, :], ACT.Copy)
                    act.activation(v_full[:, j % 2, :], p_val[j % 2][:, :], ACT.Copy).then_inc(val_copied.sem, 1)
                    act.wait_ge(key_made.sem, key_made.at(j, b))
                    act.wait_ge(key_rstd.sem, key_rstd.at(j - 2, b))
                    for g in range(G):
                        cols = slice(g * DH, (g + 1) * DH)
                        ins = act.activation(k_sq[:, j % 2, cols], p_key[j % 2][:, cols], ACT.Square,
                                             accum_out=k_ms[:, j % 2, g:g + 1])
                    ins.then_inc(key_sq.sem, 1)

                def normalise_keys(j):
                    act.wait_ge(key_rstd.sem, key_rstd.at(j, b))
                    act.wait_ge(key_turned.sem, key_turned.at(j - 2, b))
                    for g in range(G):
                        cols = slice(g * DH, (g + 1) * DH)
                        ins = act.activation(k_nrm[:, j % 2, cols], p_key[j % 2][:, cols], ACT.Copy,
                                             scale=k_rstd[:, j % 2, g:g + 1])
                    ins.then_inc(key_nrm.sem, 1)
                    act.wait_ge(key_turned.sem, key_turned.at(j, b))
                    act.wait_ge(key_lo.sem, key_lo.at(j - 2, b))
                    act.activation(k_full[:, j % 2, :], p_kt[:, :], ACT.Copy,
                                   scale=kw[:, 0:1]).then_inc(key_full.sem, 1)

                for j in range(TT):
                    values_and_squares(j)
                    if j >= 1:
                        normalise_keys(j - 1)
                normalise_keys(TT - 1)
                act.wait_ge(ctx_quant.sem, ctx_quant.at(0, b))
                act.wait_ge(y_made.sem, y_made.at(-1, b))
                act.activation(cq_hi[:, :, :], c_raw[:, :, :], ACT.Copy).then_inc(cq_hi_made.sem, 1)
                for k in range(KT):
                    act.wait_ge(x_turned.sem, x_turned.at(k, b))
                    act.activation(xq_hi[:, k, :], p_xt[k % 2][:, :], ACT.Copy).then_inc(xq_hi_made.sem, 1)

        @block.gpsimd
        def _(pool):
            for s in (val_lo, key_rstd, key_lo):
                pool.sem_inc(s.sem, s.opening)
            pool.memset(K.power[:, :], -0.5)
            pool.memset(K.ln_eps[:, :], LN_EPS)
            step = Count(ident_made)
            pool.memset(K.ident[:, :], 0.0).then_inc(step.sem, 1)
            pool.wait_ge(step.sem, step.next())
            pool.affine_select(out=K.ident[:, :], in_=K.ident[:, :], compare_op=ALU.not_equal, fill=1.0,
                               base=0, pattern=[[-1, P]], channel_multiplier=1).then_inc(step.sem, 1)
            pool.wait_ge(step.sem, step.next())
            with pool.Fori(0, B) as b:
                step = Count(p_steps, b)
                pool.wait_ge(ctx_hi.sem, ctx_hi.at(0, b))
                pool.tensor_tensor(c_lo[:, :, :], c_raw[:, :, :], f32(c_hi[:, :, :]),
                                   ALU.subtract).then_inc(ctx_lo.sem, 1)
                pool.wait_ge(ctx_amax.sem, ctx_amax.at(0, b))
                pool.sem_inc(K.apart, 1)
                pool.partition_all_reduce(amax_all, amax, P,
                                          bass.bass_isa.ReduceOp.max).then_inc(ctx_amax_all.sem, 1)
                pool.wait_ge(x_var.sem, x_var.at(0, b))
                pool.sem_inc(K.apart, 1)
                pool.tensor_scalar(veps[:, :], mv[:, :, 1], LN_EPS, None, ALU.add).then_inc(step.sem, 1)
                pool.wait_ge(step.sem, step.next())
                pool.tensor_tensor(rstd[:, :], veps[:, :], K.power[:, 0:TT], ALU.pow).then_inc(x_rstd.sem, 1)

                def rstd_and_values_lo(j):
                    pool.wait_ge(key_sq.sem, key_sq.at(j, b))
                    pool.wait_ge(key_nrm.sem, key_nrm.at(j - 2, b))
                    pool.sem_inc(K.apart, 1)
                    pool.tensor_scalar(k_eps[:, j % 2, :], k_ms[:, j % 2, :], 1.0 / DH, RMS_EPS,
                                       ALU.mult, ALU.add).then_inc(step.sem, 1)
                    pool.wait_ge(step.sem, step.next())
                    pool.tensor_tensor(k_rstd[:, j % 2, :], k_eps[:, j % 2, :],
                                       K.power[:, 0:G], ALU.pow).then_inc(key_rstd.sem, 1)
                    pool.wait_ge(val_copied.sem, val_copied.at(j, b))
                    pool.tensor_tensor(v_out[:, j, 1, :], v_full[:, j % 2, :],
                                       f32(v_out[:, j, 0, :]), ALU.subtract).then_inc(val_lo.sem, 1)

                def split_keys(j):
                    cols = slice(j * P, (j + 1) * P)
                    whole = k_full[:, j % 2, :].rearrange("p (g n) -> p g n", g=G)
                    pool.wait_ge(key_full.sem, key_full.at(j, b))
                    pool.sem_inc(K.apart, 1)
                    pool.tensor_copy(k_out[:, 0, :, cols], whole).then_inc(key_hi.sem, 1)
                    pool.wait_ge(key_hi.sem, key_hi.at(j, b))
                    pool.tensor_tensor(k_out[:, 1, :, cols], whole, f32(k_out[:, 0, :, cols]),
                                       ALU.subtract).then_inc(key_lo.sem, 1)

                for j in range(TT):
                    if j == 0:
                        pool.wait_ge(kv_out.sem, kv_out.at(-1, b))
                    rstd_and_values_lo(j)
                    if j >= 1:
                        split_keys(j - 1)
                split_keys(TT - 1)
                assert step.n == p_steps.per

        @block.vector
        def _(dve):
            for s in (cq_lo_made, xq_lo_made, y_added):
                dve.sem_inc(s.sem, s.opening)
            for n, (hi, lo) in enumerate(((wk_hi, wk_lo), (wv_hi, wv_lo))):
                dve.wait_ge(w_hi.sem, w_hi.at(n))
                dve.tensor_tensor(lo[:, :, :], w_raw[:, :, :], f32(hi[:, :, :]),
                                  ALU.subtract).then_inc(w_lo.sem, 1)
            dve.wait_ge(K.gates_made.sem, K.gates_made.at(0))
            with dve.Fori(0, B) as b:
                step = Count(v_steps, b)
                c_blocks = c_raw[:, :, :].rearrange("p k (c n) -> p (k c) n", n=P)
                dve.wait_ge(ctx_in.sem, ctx_in.at(0, b))
                dve.tensor_reduce(amax, c_blocks, AX.X, ALU.max,
                                  apply_absolute_value=True).then_inc(ctx_amax.sem, 1)
                dve.wait_ge(x_in.sem, x_in.at(0, b))
                xs = K.x[:, bass.ds(b * TT, TT), :]
                layer_norm_stats(dve, xs, stats, mv, step, K.apart).then_inc(x_var.sem, 1)
                dve.wait_ge(ctx_amax_all.sem, ctx_amax_all.at(0, b))
                dve.wait_ge(ctx_hi.sem, ctx_hi.at(0, b))
                dve.wait_ge(ctx_lo.sem, ctx_lo.at(0, b))
                quantise(dve, step, c_blocks, scale, W_EPS, grid[:, :, :], back, safe,
                         amax_all).then_inc(ctx_quant.sem, 1)
                dve.wait_ge(cq_hi_made.sem, cq_hi_made.at(0, b))
                dve.tensor_tensor(cq_lo[:, :, :], c_raw[:, :, :], f32(cq_hi[:, :, :]),
                                  ALU.subtract).then_inc(cq_lo_made.sem, 1)
                dve.wait_ge(x_rstd.sem, x_rstd.at(0, b))
                dve.wait_ge(x_turned.sem, x_turned.at(-1, b))
                for t in range(TT):
                    ins = dve.tensor_scalar(xn[:, t, :], xs[:, t, :], mv[:, t, 0:1], rstd[:, t:t + 1],
                                            ALU.subtract, ALU.mult)
                ins.then_inc(step.sem, 1)
                dve.wait_ge(step.sem, step.next())
                x_blocks = xn[:, :, :].rearrange("p t (c n) -> p (t c) n", n=P)
                dve.tensor_reduce(x_amax, x_blocks, AX.X, ALU.max,
                                  apply_absolute_value=True).then_inc(step.sem, 1)
                dve.wait_ge(step.sem, step.next())
                quantise(dve, step, x_blocks, x_scale, ACT_EPS, grid[:, :, :], x_back, x_safe,
                         x_amax).then_inc(x_quant.sem, 1)
                for k in range(KT):
                    dve.wait_ge(xq_hi_made.sem, xq_hi_made.at(k, b))
                    if k == 0:
                        dve.wait_ge(y_made.sem, y_made.at(-1, b))
                    dve.tensor_tensor(xq_lo[:, k, :], p_xt[k % 2][:, :], f32(xq_hi[:, k, :]),
                                      ALU.subtract).then_inc(xq_lo_made.sem, 1)
                for t in range(TT):
                    dve.wait_ge(y_made.sem, y_made.at(t, b))
                    dve.scalar_tensor_tensor(xs[:, t, :], p_y[:, :], K.gates[:, 0:1], xs[:, t, :],
                                             ALU.mult, ALU.add).then_inc(y_added.sem, 1)
                assert step.n == v_steps.per

        @block.tensor
        def _(pe):
            for s in (key_made, val_made, key_turned, x_turned, y_made):
                pe.sem_inc(s.sem, s.opening)
            pe.wait_ge(w_lo.sem, w_lo.at(1))
            pe.wait_ge(ident_made.sem, ident_made.at(1))
            with pe.Fori(0, B) as b:
                pe.wait_ge(ctx_lo.sem, ctx_lo.at(0, b))
                pe.wait_ge(ctx_hi.sem, ctx_hi.at(0, b))

                def keys_and_values(j):
                    rows = slice(j * P, (j + 1) * P)
                    pe.wait_ge(key_nrm.sem, key_nrm.at(j - 2, b))
                    for k in range(KT):
                        ins = three_pass(pe, p_key[j % 2][:, :], c_hi[:, k, rows], c_lo[:, k, rows],
                                         wk_hi[:, k, :], wk_lo[:, k, :], k == 0, k == KT - 1)
                    ins.then_inc(key_made.sem, 1)
                    pe.wait_ge(val_copied.sem, val_copied.at(j - 2, b))
                    for k in range(KT):
                        ins = three_pass(pe, p_val[j % 2][:, :], c_hi[:, k, rows], c_lo[:, k, rows],
                                         wv_hi[:, k, :], wv_lo[:, k, :], k == 0, k == KT - 1)
                    ins.then_inc(val_made.sem, 1)

                def turn_keys(j):
                    pe.wait_ge(key_nrm.sem, key_nrm.at(j, b))
                    pe.wait_ge(key_full.sem, key_full.at(j - 1, b))
                    for g in range(G):
                        ins = pe.transpose(p_kt[:, g * P:(g + 1) * P], k_nrm[:, j % 2, g * DH:(g + 1) * DH],
                                           K.ident[:, :])
                    ins.then_inc(key_turned.sem, 1)

                for j in range(TT):
                    keys_and_values(j)
                    if j >= 1:
                        turn_keys(j - 1)
                turn_keys(TT - 1)
                pe.wait_ge(x_quant.sem, x_quant.at(0, b))
                for k in range(KT):
                    pe.wait_ge(xq_lo_made.sem, xq_lo_made.at(k - 2, b))
                    for t in range(TT):
                        ins = pe.transpose(p_xt[k % 2][:, t * P:(t + 1) * P], xn[:, t, k * P:(k + 1) * P],
                                           K.ident[:, :])
                    ins.then_inc(x_turned.sem, 1)
                pe.wait_ge(xq_lo_made.sem, xq_lo_made.at(KT - 1, b))
                pe.wait_ge(cq_lo_made.sem, cq_lo_made.at(0, b))
                for t in range(TT):
                    rows = slice(t * P, (t + 1) * P)
                    pe.wait_ge(y_added.sem, y_added.at(t - 1, b))
                    for k in range(KT):
                        ins = three_pass(pe, p_y[:, :], xq_hi[:, k, rows], xq_lo[:, k, rows],
                                         cq_hi[:, k, :], cq_lo[:, k, :], k == 0, k == KT - 1)
                    ins.then_inc(y_made.sem, 1)


def stage_norm(K, tag):
    with ExitStack() as ctx:
        sb, ps = K.scope(ctx)
        xn = sb(f"{tag}_xn", [P, 2, TT, D])
        stats = sb(f"{tag}_stats", [P, TT, 6])
        mv = sb(f"{tag}_mv", [P, TT, 2])
        veps = sb(f"{tag}_veps", [P, TT])
        rstd = sb(f"{tag}_rstd", [P, TT])
        p_t = [ps(f"{tag}_p{k}") for k in range(2 * KT)]

        var = Signal(K, f"{tag}_variance", per=2)
        rstd_made = Signal(K, f"{tag}_rstd", per=2)
        normed = Signal(K, f"{tag}_normalised", per=2)
        turned = Signal(K, f"{tag}_transposed", per=2 * KT, credit=2 * KT)
        hi_made = Signal(K, f"{tag}_hi", per=2 * KT)
        lo_made = Signal(K, f"{tag}_lo", per=2 * KT, credit=2 * KT)
        steps = Signal(K, f"{tag}_vector_steps", per=2)
        p_steps = Signal(K, f"{tag}_pool_steps", per=2)
        block = ctx.enter_context(K.nc.Block())

        @block.vector
        def _(dve):
            dve.sem_inc(lo_made.sem, lo_made.opening)
            with dve.Fori(0, B // 2) as i:
                step = Count(steps, i)
                for u in range(2):
                    xs = K.x[:, bass.ds(i * (2 * TT) + u * TT, TT), :]
                    if u == 1:
                        dve.wait_ge(normed.sem, normed.at(0, i))
                    layer_norm_stats(dve, xs, stats, mv, step, K.apart).then_inc(var.sem, 1)
                    dve.wait_ge(rstd_made.sem, rstd_made.at(u, i))
                    dve.wait_ge(turned.sem, turned.at((u - 2) * KT + KT - 1, i))
                    for t in range(TT):
                        ins = dve.tensor_scalar(xn[:, u, t, :], xs[:, t, :], mv[:, t, 0:1], rstd[:, t:t + 1],
                                                ALU.subtract, ALU.mult)
                    ins.then_inc(normed.sem, 1)
                for u in range(2):
                    for k in range(KT):
                        dve.wait_ge(hi_made.sem, hi_made.at(u * KT + k, i))
                        cols = bass.ds(i * (2 * S) + u * S, S)
                        dve.tensor_tensor(K.xt_lo[:, k, cols], p_t[u * KT + k][:, :],
                                          f32(K.xt_hi[:, k, cols]), ALU.subtract).then_inc(lo_made.sem, 1)

        @block.gpsimd
        def _(pool):
            with pool.Fori(0, B // 2) as i:
                step = Count(p_steps, i)
                for u in range(2):
                    pool.wait_ge(var.sem, var.at(u, i))
                    pool.tensor_tensor(veps[:, :], mv[:, :, 1], K.ln_eps[:, :], ALU.add).then_inc(step.sem, 1)
                    pool.wait_ge(step.sem, step.next())
                    pool.tensor_tensor(rstd[:, :], veps[:, :], K.power[:, 0:TT],
                                       ALU.pow).then_inc(rstd_made.sem, 1)

        @block.tensor
        def _(pe):
            pe.sem_inc(turned.sem, turned.opening)
            with pe.Fori(0, B // 2) as i:
                for u in range(2):
                    pe.wait_ge(normed.sem, normed.at(u, i))
                    for k in range(KT):
                        pe.wait_ge(lo_made.sem, lo_made.at((u - 2) * KT + k, i))
                        for t in range(TT):
                            ins = pe.transpose(p_t[u * KT + k][:, t * P:(t + 1) * P],
                                               xn[:, u, t, k * P:(k + 1) * P], K.ident[:, :])
                        ins.then_inc(turned.sem, 1)

        @block.scalar
        def _(act):
            with act.Fori(0, B // 2) as i:
                for u in range(2):
                    for k in range(KT):
                        act.wait_ge(turned.sem, turned.at(u * KT + k, i))
                        act.activation(K.xt_hi[:, k, bass.ds(i * (2 * S) + u * S, S)],
                                       p_t[u * KT + k][:, :], ACT.Copy).then_inc(hi_made.sem, 1)


def stage_ffn(K, w1_t, w2_t, b1_t, b2):
    with ExitStack() as ctx:
        sb, ps = K.scope(ctx)
        CH = 4
        w1q, w2q = sb("w1q", [P, KT, F], F32R), sb("w2q", [P, FT, D], F32R)
        raw = sb("f_raw", [P, 2, F])
        least = sb("f_least", [P, F])
        sums = sb("f_sums", [P, CH, 32])
        total = sb("f_total", [P, 2])
        total_all = sb("f_total_all", [P, 2])
        thr, neg_thr = sb("f_thr", [P, 2]), sb("f_neg_thr", [P, 2])
        b1_c = sb("b1_c", [P, FT])
        b2_r, b2_g = sb("b2_r", [P, D]), sb("b2_g", [P, D])
        act_out = sb("f_act", [P, 2, S])
        h_hi, h_lo = sb("h_hi", [P, 2, S], F32R), sb("h_lo", [P, 2, S], F32R)
        p_h = [ps(f"p_h{n}") for n in range(2)]
        p_y = [ps(f"f_y{t}") for t in range(TT)]

        bias_in = Signal(K, "f_bias_in", unit=16)
        w_in = [Signal(K, f"f_weights_in{n}", unit=16) for n in range(2)]
        w_used = Signal(K, "f_weights_used")
        totals = Signal(K, "f_totals")
        total_made = Signal(K, "f_total_all_made")
        w_made = Signal(K, "f_ternary_made")
        b2_made = Signal(K, "f_b2_scaled")
        b2_added = Signal(K, "f_b2_added", per=TT)
        h_made = Signal(K, "f_h_product", per=FT)
        gelu_made = Signal(K, "f_gelu", per=FT, credit=2)
        hi_made = Signal(K, "f_h_hi", per=FT, credit=2)
        lo_made = Signal(K, "f_h_lo", per=FT, credit=2)
        h_used = Signal(K, "f_h_used", per=FT, credit=2)
        y_added = Signal(K, "f_added", per=TT, credit=TT)
        steps = Signal(K, "f_vector_steps")
        block = ctx.enter_context(K.nc.Block())
        chunks = [w1_t.rearrange("(k p) f -> k p f", p=P)[c] for c in range(CH)]
        chunks2 = [w2_t.rearrange("(c k p) n -> c p k n", p=P, k=CH)[c] for c in range(CH)]
        loads = [(w, c) for w in range(2) for _ in range(2) for c in range(CH)]

        @block.sync
        def _(sp):
            sp.dma_start(b1_c[:, :], b1_t).then_inc(bias_in.sem, 16)
            sp.dma_start(b2_r[:, :], b2.partition_broadcast(P)).then_inc(bias_in.sem, 16)
            for n, (w, c) in enumerate(loads):
                if n >= 2:
                    sp.wait_ge(w_used.sem, w_used.at(n - 2))
                dst = raw[:, n % 2, :]
                if w == 0:
                    sp.dma_start(dst, chunks[c]).then_inc(w_in[n % 2].sem, 16)
                else:
                    sp.dma_start(dst.rearrange("p (k n) -> p k n", k=CH), chunks2[c]).then_inc(w_in[n % 2].sem,
                                                                                               16)

        @block.gpsimd
        def _(pool):
            for w in range(2):
                pool.wait_ge(totals.sem, totals.at(w))
                pool.partition_all_reduce(total_all[:, w:w + 1], total[:, w:w + 1], P,
                                          bass.bass_isa.ReduceOp.add).then_inc(total_made.sem, 1)
            pool.wait_ge(b2_made.sem, b2_made.at(0))
            for t in range(T):
                pool.tensor_tensor(K.x[:, t, :], K.x[:, t, :], b2_g[:, :], ALU.add).then_inc(b2_added.sem, 1)

        @block.vector
        def _(dve):
            dve.sem_inc(lo_made.sem, lo_made.opening)
            dve.sem_inc(y_added.sem, y_added.opening)
            step = Count(steps)
            dve.wait_ge(bias_in.sem, bias_in.at(1))
            dve.tensor_scalar(b2_g[:, :], b2_r[:, :], K.gates[:, 2:3], None, ALU.mult).then_inc(b2_made.sem, 1)
            n = 0
            for w, wq in enumerate((w1q[:, :, :], w2q[:, :, :])):
                for c in range(CH):
                    dve.wait_ge(w_in[n % 2].sem, w_in[n % 2].at(n // 2))
                    dve.tensor_reduce(sums[:, c, :],
                                      raw[:, n % 2, :].rearrange("p (a n) -> p a n", a=32),
                                      AX.X, ALU.add, apply_absolute_value=True).then_inc(w_used.sem, 1)
                    n += 1
                dve.wait_ge(w_used.sem, w_used.at(n - 1))
                dve.tensor_reduce(total[:, w:w + 1], sums[:, :, :], AX.XY, ALU.add).then_inc(totals.sem, 1)
                dve.wait_ge(total_made.sem, total_made.at(w))
                dve.tensor_scalar(thr[:, w:w + 1], total_all[:, w:w + 1], 1.0 / (D * F), 0.7,
                                  ALU.mult, ALU.mult)
                dve.tensor_scalar(neg_thr[:, w:w + 1], total_all[:, w:w + 1], -1.0 / (D * F), 0.7,
                                  ALU.mult, ALU.mult).then_inc(step.sem, 1)
                dve.wait_ge(step.sem, step.next())
                for c in range(CH):
                    dve.wait_ge(w_in[n % 2].sem, w_in[n % 2].at(n // 2))
                    dve.wait_ge(w_used.sem, w_used.at(n - 1))
                    part = wq.rearrange("p k n -> p (k n)")[:, c * F:(c + 1) * F]
                    dve.tensor_scalar(least[:, :], raw[:, n % 2, :], neg_thr[:, w:w + 1], None,
                                      ALU.is_le).then_inc(step.sem, 1)
                    dve.wait_ge(step.sem, step.next())
                    dve.scalar_tensor_tensor(part, raw[:, n % 2, :], thr[:, w:w + 1],
                                             least[:, :], ALU.is_ge, ALU.subtract).then_inc(w_used.sem, 1)
                    n += 1
            with dve.Fori(0, B) as b:
                for f in range(FT):
                    dve.wait_ge(hi_made.sem, hi_made.at(f, b))
                    dve.wait_ge(h_used.sem, h_used.at(f - 2, b))
                    dve.tensor_tensor(h_lo[:, f % 2, :], act_out[:, f % 2, :],
                                      f32(h_hi[:, f % 2, :]), ALU.subtract).then_inc(lo_made.sem, 1)
                dve.wait_ge(h_used.sem, h_used.at(FT - 1, b))
                dve.wait_ge(b2_added.sem, b2_added.at(TT - 1, b))
                for t in range(TT):
                    xt = K.x[:, bass.ds(b * TT + t, 1), :].rearrange("p a n -> p (a n)")
                    dve.scalar_tensor_tensor(xt, p_y[t][:, :], K.gates[:, 2:3], xt,
                                             ALU.mult, ALU.add).then_inc(y_added.sem, 1)

        @block.scalar
        def _(act):
            act.sem_inc(gelu_made.sem, gelu_made.opening)
            act.sem_inc(hi_made.sem, hi_made.opening)
            act.wait_ge(bias_in.sem, bias_in.at(1))
            with act.Fori(0, B) as b:
                for f in range(FT):
                    act.wait_ge(h_made.sem, h_made.at(f, b))
                    act.wait_ge(lo_made.sem, lo_made.at(f - 2, b))
                    act.activation(act_out[:, f % 2, :], p_h[f % 2][:, :], ACT.Gelu,
                                   bias=b1_c[:, f:f + 1]).then_inc(gelu_made.sem, 1)
                    act.wait_ge(gelu_made.sem, gelu_made.at(f, b))
                    act.wait_ge(h_used.sem, h_used.at(f - 2, b))
                    act.activation(h_hi[:, f % 2, :], act_out[:, f % 2, :], ACT.Copy).then_inc(hi_made.sem, 1)

        @block.tensor
        def _(pe):
            pe.sem_inc(h_used.sem, h_used.opening)
            pe.wait_ge(w_used.sem, w_used.at(2 * CH - 1))

            def hidden(b, f):
                pe.wait_ge(gelu_made.sem, gelu_made.at(f - 2, b))
                for k in range(KT):
                    w = w1q[:, k, f * P:(f + 1) * P]
                    cols = bass.ds(b * S, S)
                    pe.matmul(p_h[f % 2][:, :], w, K.xt_hi[:, k, cols], start=k == 0, stop=False)
                    ins = pe.matmul(p_h[f % 2][:, :], w, K.xt_lo[:, k, cols], start=False, stop=k == KT - 1)
                ins.then_inc(h_made.sem, 1)

            def output(b, f):
                pe.wait_ge(lo_made.sem, lo_made.at(f, b))
                for t in range(TT):
                    rows = slice(t * P, (t + 1) * P)
                    if f == 0:
                        pe.wait_ge(y_added.sem, y_added.at(t - TT, b))
                    pe.matmul(p_y[t][:, :], h_hi[:, f % 2, rows], w2q[:, f, :], start=f == 0, stop=False)
                    ins = pe.matmul(p_y[t][:, :], h_lo[:, f % 2, rows], w2q[:, f, :], start=False,
                                    stop=f == FT - 1)
                ins.then_inc(h_used.sem, 1)

            with pe.Fori(0, B) as b:
                for f in range(FT):
                    hidden(b, f)
                    if f == 1:
                        pe.wait_ge(w_used.sem, w_used.at(4 * CH - 1))
                    if f >= 1:
                        output(b, f - 1)
                output(b, FT - 1)


def stage_attention(K, wq, wo, q_norm_w, keys, values):
    with ExitStack() as ctx:
        sb, ps = K.scope(ctx)
        U = HG * TT
        HALF = S // 2
        ITS = G * B
        HP = HG // 2
        LAST_STEP = U + 11
        NP = 2 * TT
        w_raw = sb("a_w_raw", [P, KT, HG * DH])
        wq_hi, wq_lo = sb("wq_hi", [P, KT, HG * DH], F32R), sb("wq_lo", [P, KT, HG * DH], F32R)
        wo_hi, wo_lo = sb("wo_hi", [P, HG, D], F32R), sb("wo_lo", [P, HG, D], F32R)
        k_in = sb("k_in", [P, 2, 2, S], F32R)
        v_in = sb("v_in", [P, TT, 2, DH], F32R)
        q_hi, q_lo = sb("q_hi", [P, 2, S], F32R), sb("q_lo", [P, 2, S], F32R)
        q_sq = sb("q_sq", [P, S])
        q_ms = sb("q_ms", [P, 2, TT])
        q_rs = sb("q_rs", [P, 2, TT])
        neg_max = sb("neg_max", [P, U])
        bias = sb("a_bias", [P, U])
        total = sb("a_total", [P, U])
        inv = sb("a_inv", [P, U])
        prob = sb("prob", [P, 4, S])
        pt_hi, pt_lo = sb("pt_hi", [P, 2, TT, HALF], F32R), sb("pt_lo", [P, 2, TT, HALF], F32R)
        o_hi, o_lo = sb("o_hi", [P, HG, S], F32R), sb("o_lo", [P, HG, S], F32R)
        ones = sb("a_ones", [P, 1])
        qw = sb("qw", [P, 1])
        p_s = [ps(f"p_s{n}") for n in range(4)]
        p_t = [ps(f"p_t{n}") for n in range(2)]
        p_q = ps("p_q")
        p_o = ps("p_o")

        qw_in = Signal(K, "a_query_norm_in", unit=16)
        w_in = Signal(K, "a_weights_in", per=2, unit=16)
        wq_hi0 = Signal(K, "a_first_wq_hi")
        wq_lo0 = Signal(K, "a_first_wq_lo")
        w_steps = Signal(K, "a_weights_hi", per=2 * HG)
        wq_made = Signal(K, "a_wq_split", per=HG)
        wo_made = Signal(K, "a_wo_split", per=HG)
        keys_in = Signal(K, "a_keys_in", unit=16)
        values_in = [Signal(K, f"a_values_in{n}", unit=16) for n in range(2)]
        ones_made = Signal(K, "a_ones_made")
        q_made = Signal(K, "a_q_product", per=HG)
        q_squared = Signal(K, "a_q_squared", per=HG)
        q_hi_made = Signal(K, "a_q_hi", per=HG)
        q_lo_made = Signal(K, "a_q_lo", per=HG)
        ms_made = Signal(K, "a_q_square_sums", per=HG)
        ms_read = Signal(K, "a_q_square_sums_read", per=HG)
        rs_made = Signal(K, "a_q_scale", per=HG)
        s_made = Signal(K, "a_scores", per=U)
        max_made = Signal(K, "a_max", per=U)
        bias_made = Signal(K, "a_bias_made", per=U)
        exp_made = Signal(K, "a_exp", per=U)
        inv_made = Signal(K, "a_inverse", per=U)
        p_made = Signal(K, "a_probabilities", per=U)
        t_made = Signal(K, "a_transposed", per=U)
        pt_hi_made = Signal(K, "a_pt_hi", per=U)
        pt_lo_made = Signal(K, "a_pt_lo", per=U)
        o_made = Signal(K, "a_heads_out", per=U)
        o_hi_made = Signal(K, "a_o_hi", per=HG)
        o_lo_made = Signal(K, "a_o_lo", per=HG)
        y_made = Signal(K, "a_product", per=NP, credit=NP)
        y_added = Signal(K, "a_added", per=NP)
        block = ctx.enter_context(K.nc.Block())
        wq_v = wq.rearrange("(k p) n -> p k n", p=P)
        wo_v = wo.rearrange("(h p) n -> p h n", p=P)

        def home(it, n, per):
            if isinstance(it, int) and not 0 <= it * per + n < ITS * per:
                return None
            return it + n // per if n // per else it, n % per

        def query_head(it, u):
            return home(it, (u + 5) // TT, HG)

        def projected(it, u):
            return home(it, (u - 13) // TT * 2 + u % TT - 1, NP)

        @block.sync
        def _(sp):
            def load_wq(g):
                sp.dma_start(w_raw[:, :, :], wq_v[:, :, bass.ds(g * (HG * DH), HG * DH)]).then_inc(w_in.sem, 16)

            def load_wo(g):
                sp.dma_start(w_raw[:, :, :], wo_v[:, bass.ds(g * HG, HG), :]).then_inc(w_in.sem, 16)

            def load_keys(it):
                if s_made.given(-U - 1, it):
                    sp.wait_ge(s_made.sem, s_made.at(-U - 1, it))
                    sp.sem_inc(K.apart, 1)
                if keys_in.given(-1, it):
                    sp.wait_ge(keys_in.sem, keys_in.at(-1, it))
                    sp.sem_inc(K.apart, 1)
                sp.dma_start(
                    f32(k_in[:, bass.ds(it % 2, 1), :, :]).rearrange("p s h n -> p (s h) n"),
                    keys[bass.ds(it % B, 1), :, :, bass.ds(it // B, 1), :].rearrange("a p h c n -> p (a h c) n")
                ).then_inc(keys_in.sem, 16)

            def load_values(it):
                for n in range(2):
                    tiles = slice(n * TT // 2, (n + 1) * TT // 2)
                    if o_made.given(n - 2, it):
                        sp.wait_ge(o_made.sem, o_made.at(n - 2, it))
                        sp.sem_inc(K.apart, 1)
                    sp.dma_start(
                        f32(v_in[:, tiles, :, :]),
                        values[bass.ds(it % B, 1), :, tiles, :, bass.ds(it // B * DH, DH)].rearrange(
                            "a p t h n -> p (a t) h n")).then_inc(values_in[n].sem, 16)

            def loads(it):
                load_values(it)
                load_keys(it + 1)

            sp.dma_start(qw[:, :], q_norm_w.rearrange("(p a) -> p a", a=1)).then_inc(qw_in.sem, 16)
            load_wq(0)
            load_keys(0)
            load_values(0)
            load_keys(1)
            sp.wait_ge(wq_lo0.sem, wq_lo0.at(0))
            load_wo(0)
            with sp.Fori(0, G - 1) as g:
                loads(g * B + 1)
                sp.wait_ge(wo_made.sem, wo_made.at(HG - 1, g))
                sp.sem_inc(K.apart, 1)
                load_wq(g + 1)
                loads(g * B + 2)
                loads(g * B + 3)
                sp.wait_ge(wq_made.sem, wq_made.at(HG - 1, g + 1))
                sp.sem_inc(K.apart, 1)
                load_wo(g + 1)
                loads(g * B + 4)
            loads(ITS - 3)
            loads(ITS - 2)
            load_values(ITS - 1)

        @block.gpsimd
        def _(pool):
            pool.memset(ones[:, :], 1.0).then_inc(ones_made.sem, 1)
            pool.sem_inc(wq_made.sem, HG)
            def query_scale(it, j):
                pool.wait_ge(ms_read.sem, ms_read.at(j, it))
                pool.tensor_tensor(q_rs[:, j % 2, :], q_ms[:, j % 2, :], K.power[:, 0:TT],
                                   ALU.pow).then_inc(rs_made.sem, 1)

            def split_wo(g, h):
                if h == 0:
                    pool.wait_ge(w_in.sem, w_in.at(1, g))
                pool.wait_ge(y_made.sem, y_made.at((h // HP + 1) * TT - 1 - NP, g * B))
                pool.sem_inc(K.apart, 1)
                pool.tensor_copy(wo_hi[:, h, :], w_raw[:, h, :]).then_inc(w_steps.sem, 1)
                pool.wait_ge(w_steps.sem, w_steps.at(h, g))
                pool.tensor_tensor(wo_lo[:, h, :], w_raw[:, h, :], f32(wo_hi[:, h, :]),
                                   ALU.subtract).then_inc(wo_made.sem, 1)

            def split_wq(g, h):
                cols = slice(h * DH, (h + 1) * DH)
                if h == 0:
                    pool.wait_ge(w_in.sem, w_in.at(0, g + 1))
                pool.wait_ge(q_made.sem, q_made.at(h, g * B + B - 1))
                pool.sem_inc(K.apart, 1)
                pool.tensor_copy(wq_hi[:, :, cols], w_raw[:, :, cols]).then_inc(w_steps.sem, 1)
                pool.wait_ge(w_steps.sem, w_steps.at(HG + h, g))
                pool.tensor_tensor(wq_lo[:, :, cols], w_raw[:, :, cols], f32(wq_hi[:, :, cols]),
                                   ALU.subtract).then_inc(wq_made.sem, 1)

            query_scale(0, 0)
            with pool.Fori(0, G - 1) as g:
                for h in range(HG):
                    query_scale(g * B, h + 1)
                    split_wo(g, h)
                with pool.Fori(1, B - 1) as b:
                    for h in range(HG):
                        query_scale(g * B + b, h + 1)
                for h in range(HG):
                    query_scale(g * B + (B - 1), h + 1)
                    split_wq(g, h)
            for h in range(HG):
                query_scale(ITS - B, h + 1)
                split_wo(G - 1, h)
            with pool.Fori(ITS - B + 1, ITS - 1) as it:
                for h in range(HG):
                    query_scale(it, h + 1)
            for h in range(HG - 1):
                query_scale(ITS - 1, h + 1)

        @block.scalar
        def _(act):
            act.wait_ge(w_in.sem, w_in.at(0))
            act.activation(wq_hi[:, :, :], w_raw[:, :, :], ACT.Copy).then_inc(wq_hi0.sem, 1)
            act.wait_ge(qw_in.sem, qw_in.at(0))

            def split_query(it, h):
                act.wait_ge(q_made.sem, q_made.at(h, it))
                if s_made.given((h - 1) * TT - 1, it):
                    act.wait_ge(s_made.sem, s_made.at((h - 1) * TT - 1, it))
                act.activation(q_hi[:, h % 2, :], p_q[:, :], ACT.Copy, scale=qw[:, 0:1]).then_inc(q_hi_made.sem, 1)
                if ms_made.given(h - 1, it):
                    act.wait_ge(ms_made.sem, ms_made.at(h - 1, it))
                act.activation(q_sq[:, :], p_q[:, :], ACT.Square).then_inc(q_squared.sem, 1)

            def exp(it, u):
                act.wait_ge(bias_made.sem, bias_made.at(u, it))
                if t_made.given(u - 4, it):
                    act.wait_ge(t_made.sem, t_made.at(u - 4, it))
                act.activation(prob[:, u % 4, :], p_s[u % 4][:, :], ACT.Exp, bias=bias[:, u:u + 1],
                               scale=q_rs[:, u // TT % 2, u % TT:u % TT + 1],
                               accum_out=total[:, u:u + 1]).then_inc(exp_made.sem, 1)

            def transposed_hi(it, u):
                act.wait_ge(t_made.sem, t_made.at(u, it))
                if u % 2 == 0 and o_made.given(u - 3, it):
                    act.wait_ge(o_made.sem, o_made.at(u - 3, it))
                act.activation(pt_hi[:, u // 2 % 2, :, (u % 2) * P:(u % 2 + 1) * P],
                               p_t[u % 2][:, :].rearrange("p (t n) -> p t n", t=TT),
                               ACT.Copy).then_inc(pt_hi_made.sem, 1)

            def head_out(it, h):
                act.wait_ge(o_made.sem, o_made.at(4 * h + 3, it))
                act.wait_ge(y_made.sem, y_made.at((h // HP + 1) * TT - 1 - NP, it))
                act.activation(o_hi[:, h, :], p_o[:, :], ACT.Copy).then_inc(o_hi_made.sem, 1)

            def step(it, u):
                if u % TT == 2 and (at := home(it, (u - 6) // TT, HG)):
                    head_out(*at)
                if u % TT == 0 and (at := query_head(it, u - 1)):
                    split_query(*at)
                if at := home(it, u, U):
                    transposed_hi(*at)
                if at := home(it, u + 2, U):
                    exp(*at)

            for u in range(-5, U):
                step(0, u)
            with act.Fori(1, ITS - 1) as it:
                for u in range(U):
                    step(it, u)
            for u in range(LAST_STEP + 1):
                step(ITS - 1, u)

        @block.vector
        def _(dve):
            dve.wait_ge(wq_hi0.sem, wq_hi0.at(0))
            dve.tensor_tensor(wq_lo[:, :, :], w_raw[:, :, :], f32(wq_hi[:, :, :]),
                              ALU.subtract).then_inc(wq_lo0.sem, 1)
            dve.wait_ge(qw_in.sem, qw_in.at(0))

            def split_query(it, h):
                dve.wait_ge(q_hi_made.sem, q_hi_made.at(h, it))
                dve.wait_ge(q_squared.sem, q_squared.at(h, it))
                dve.scalar_tensor_tensor(q_lo[:, h % 2, :], p_q[:, :], qw[:, 0:1], f32(q_hi[:, h % 2, :]),
                                         ALU.mult, ALU.subtract).then_inc(q_lo_made.sem, 1)

            def read_sums(it, h):
                dve.wait_ge(ms_made.sem, ms_made.at(h, it))
                dve.tensor_scalar(q_ms[:, h % 2, :], p_q[:, 0:TT], DH * RMS_EPS, None,
                                  ALU.add).then_inc(ms_read.sem, 1)

            def maximum(it, u):
                dve.wait_ge(s_made.sem, s_made.at(u, it))
                dve.tensor_reduce(neg_max[:, u:u + 1], p_s[u % 4][:, :], AX.X, ALU.max,
                                  negate=True).then_inc(max_made.sem, 1)

            def shift(it, u):
                dve.wait_ge(max_made.sem, max_made.at(u, it))
                if u % TT == 0:
                    dve.wait_ge(rs_made.sem, rs_made.at(u // TT, it))
                dve.tensor_tensor(bias[:, u:u + 1], neg_max[:, u:u + 1],
                                  q_rs[:, u // TT % 2, u % TT:u % TT + 1], ALU.mult).then_inc(bias_made.sem, 1)

            def invert(it, u):
                dve.wait_ge(exp_made.sem, exp_made.at(u, it))
                dve.reciprocal(inv[:, u:u + 1], total[:, u:u + 1]).then_inc(inv_made.sem, 1)

            def normalise(it, u):
                dve.wait_ge(inv_made.sem, inv_made.at(u, it))
                dve.tensor_scalar(prob[:, u % 4, :], prob[:, u % 4, :], inv[:, u:u + 1], None,
                                  ALU.mult).then_inc(p_made.sem, 1)

            def transposed_lo(it, u):
                dve.wait_ge(pt_hi_made.sem, pt_hi_made.at(u, it))
                dve.tensor_tensor(pt_lo[:, u // 2 % 2, :, (u % 2) * P:(u % 2 + 1) * P],
                                  p_t[u % 2][:, :].rearrange("p (t n) -> p t n", t=TT),
                                  f32(pt_hi[:, u // 2 % 2, :, (u % 2) * P:(u % 2 + 1) * P]),
                                  ALU.subtract).then_inc(pt_lo_made.sem, 1)

            def head_out(it, h):
                dve.wait_ge(o_hi_made.sem, o_hi_made.at(h, it))
                dve.tensor_tensor(o_lo[:, h, :], p_o[:, :], f32(o_hi[:, h, :]),
                                  ALU.subtract).then_inc(o_lo_made.sem, 1)

            def add(it, n):
                dve.wait_ge(y_made.sem, y_made.at(n, it))
                xt = K.x[:, bass.ds(it % B * TT + n % TT, 1), :].rearrange("p a n -> p (a n)")
                dve.scalar_tensor_tensor(xt, p_q[:, :], K.gates[:, 1:2], xt, ALU.mult,
                                         ALU.add).then_inc(y_added.sem, 1)

            def step(it, u):
                if at := home(it, u + 2, U):
                    maximum(*at)
                if at := home(it, u + 1, U):
                    invert(*at)
                if at := home(it, u + 2, U):
                    shift(*at)
                if at := home(it, u + 1, U):
                    normalise(*at)
                if u % TT == 0 and (at := query_head(it, u - 1)):
                    split_query(*at)
                if u % TT == 1 and (at := query_head(it, u - 2)):
                    read_sums(*at)
                if u % TT in (2, 3) and (at := projected(it, u - 1)):
                    add(*at)
                if u % TT == 2 and (at := home(it, (u - 6) // TT, HG)):
                    head_out(*at)
                if at := home(it, u, U):
                    transposed_lo(*at)

            for u in range(-5, U):
                step(0, u)
            with dve.Fori(1, ITS - 1) as it:
                for u in range(U):
                    step(it, u)
            for u in range(LAST_STEP + 1):
                step(ITS - 1, u)

        @block.tensor
        def _(pe):
            pe.sem_inc(y_made.sem, y_made.opening)
            pe.wait_ge(ones_made.sem, ones_made.at(0))
            pe.wait_ge(wq_lo0.sem, wq_lo0.at(0))

            def query(it, h):
                pe.wait_ge(wq_made.sem, wq_made.at(h, it // B))
                if ms_read.given(h - 1, it):
                    pe.wait_ge(ms_read.sem, ms_read.at(h - 1, it))
                if y_added.given(2 * h - NP - 1, it):
                    pe.wait_ge(y_added.sem, y_added.at(2 * h - NP - 1, it))
                heads = slice(h * DH, (h + 1) * DH)
                cols = bass.ds(it % B * S, S)
                for k in range(KT):
                    ins = three_pass(pe, p_q[:, :], wq_hi[:, k, heads], wq_lo[:, k, heads],
                                     K.xt_hi[:, k, cols], K.xt_lo[:, k, cols], k == 0, k == KT - 1)
                ins.then_inc(q_made.sem, 1)

            def square_sums(it, h):
                pe.wait_ge(q_squared.sem, q_squared.at(h, it))
                pe.wait_ge(q_lo_made.sem, q_lo_made.at(h, it))
                for t in range(TT):
                    ins = pe.matmul(p_q[:, t:t + 1], q_sq[:, t * P:(t + 1) * P], ones[:, :],
                                    start=True, stop=True)
                ins.then_inc(ms_made.sem, 1)

            def scores(it, u):
                h, qt = divmod(u, TT)
                if u == 0:
                    pe.wait_ge(keys_in.sem, keys_in.at(0, it))
                if exp_made.given(u - 4, it):
                    pe.wait_ge(exp_made.sem, exp_made.at(u - 4, it))
                if qt == 0:
                    pe.wait_ge(q_lo_made.sem, q_lo_made.at(h, it))
                rows = slice(qt * P, (qt + 1) * P)
                slot = bass.ds(it % 2, 1)
                k_hi = k_in[:, slot, 0, :].rearrange("p s n -> p (s n)")
                k_lo = k_in[:, slot, 1, :].rearrange("p s n -> p (s n)")
                three_pass(pe, p_s[u % 4][:, :], q_hi[:, h % 2, rows], q_lo[:, h % 2, rows],
                           k_hi, k_lo, True, True).then_inc(s_made.sem, 1)

            def turn(it, u):
                pe.wait_ge(p_made.sem, p_made.at(u, it))
                if pt_lo_made.given(u - 2, it):
                    pe.wait_ge(pt_lo_made.sem, pt_lo_made.at(u - 2, it))
                for t in range(TT):
                    ins = pe.transpose(p_t[u % 2][:, t * P:(t + 1) * P], prob[:, u % 4, t * P:(t + 1) * P],
                                       K.ident[:, :])
                ins.then_inc(t_made.sem, 1)

            def weigh_values(it, n):
                m = n // 2
                pe.wait_ge(pt_lo_made.sem, pt_lo_made.at(2 * m + 1, it))
                if m == 0:
                    pe.wait_ge(values_in[n].sem, values_in[n].at(0, it))
                if n % 4 == 0 and o_lo_made.given(n // 4 - 1, it):
                    pe.wait_ge(o_lo_made.sem, o_lo_made.at(n // 4 - 1, it))
                for t in range(n % 2 * TT // 2, (n % 2 + 1) * TT // 2):
                    ins = three_pass(pe, p_o[:, (m % 2) * HALF:(m % 2 + 1) * HALF], v_in[:, t, 0, :],
                                     v_in[:, t, 1, :], pt_hi[:, m % 2, t, :], pt_lo[:, m % 2, t, :],
                                     t == 0, t == TT - 1)
                ins.then_inc(o_made.sem, 1)

            def project(it, n):
                pair, t = divmod(n, TT)
                if t == 0:
                    pe.wait_ge(wo_made.sem, wo_made.at(pair * HP + HP - 1, it // B))
                    pe.wait_ge(o_lo_made.sem, o_lo_made.at(pair * HP + HP - 1, it))
                if y_added.given(n - 1, it):
                    pe.wait_ge(y_added.sem, y_added.at(n - 1, it))
                rows = slice(t * P, (t + 1) * P)
                for h in range(pair * HP, (pair + 1) * HP):
                    ins = three_pass(pe, p_q[:, :], o_hi[:, h, rows], o_lo[:, h, rows], wo_hi[:, h, :],
                                     wo_lo[:, h, :], h % HP == 0, h % HP == HP - 1)
                ins.then_inc(y_made.sem, 1)

            def step(it, u):
                if at := home(it, u - 3, U):
                    weigh_values(*at)
                if u % TT == 1 and (at := query_head(it, u - 2)):
                    square_sums(*at)
                if at := home(it, u, U):
                    turn(*at)
                if at := home(it, u + 3, U):
                    scores(*at)
                if u % TT in (1, 2) and (at := projected(it, u)):
                    if u % TT == 1 and (head := query_head(it, u - 2)):
                        pe.wait_ge(ms_read.sem, ms_read.at(head[1], head[0]))
                    project(*at)
                if u % TT == 3 and (at := query_head(it, u)):
                    query(*at)

            for u in range(-5, U):
                step(0, u)
            with pe.Fori(1, ITS - 1) as it:
                for u in range(U):
                    step(it, u)
            for u in range(LAST_STEP + 1):
                step(ITS - 1, u)


def stage_router(K, gate_t, lora_a, lora_b_t):
    with ExitStack() as ctx:
        sb, ps = K.scope(ctx)
        g_raw, g_full = sb("g_raw", [P, KT, E]), sb("g_full", [P, KT, E])
        a_raw, b_raw = sb("ga_raw", [R, D]), sb("gb_raw", [R, E])
        g_hi, g_lo = sb("g_hi", [P, KT, P], F32R), sb("g_lo", [P, KT, P], F32R)
        flat = sb("r_logits_t", [E, B * S])
        logit = sb("r_logits", [P, T, E])
        prob = sb("r_prob", [P, T, E])
        most, total, inv = sb("r_max", [P, T]), sb("r_total", [P, T]), sb("r_inv", [P, T])
        top = sb("r_top", [P, T, 8])
        index = sb("r_index", [P, T, 8], U32)
        place = sb("r_place", [P, T, 2])
        number_i, number = sb("r_number_i", [P, E], mybir.dt.int32), sb("r_number", [P, E])
        mask, other = sb("r_mask", [P, T, E]), sb("r_other", [P, T, E])
        p_g = ps("p_g")
        p_l = [ps(f"p_l{b}") for b in range(B)]
        p_t = ps("r_pt")

        loaded = Signal(K, "r_loaded", unit=16)
        zeroed = Signal(K, "r_zeroed")
        numbered = Signal(K, "r_numbered")
        delta_made = Signal(K, "r_delta")
        gate_made = Signal(K, "r_gate_split")
        logits_made = Signal(K, "r_logits_made")
        logits_read = Signal(K, "r_logits_read")
        turned = Signal(K, "r_transposed")
        shifted = Signal(K, "r_shifted")
        exp_made = Signal(K, "r_exp")
        steps = Signal(K, "r_vector_steps")
        block = ctx.enter_context(K.nc.Block())

        @block.sync
        def _(sp):
            sp.dma_start(g_raw[:, :, :], gate_t.rearrange("(k p) e -> p k e", p=P)).then_inc(loaded.sem, 16)
            sp.dma_start(a_raw[:, :], lora_a).then_inc(loaded.sem, 16)
            sp.dma_start(b_raw[:, :], lora_b_t).then_inc(loaded.sem, 16)

        @block.gpsimd
        def _(pool):
            pool.memset(f32(g_hi[:, :, :]), 0.0).then_inc(zeroed.sem, 1)
            pool.memset(f32(g_lo[:, :, :]), 0.0).then_inc(zeroed.sem, 1)
            pool.iota(number_i[:, :], pattern=[[1, E]], base=0, channel_multiplier=0).then_inc(numbered.sem, 1)

        @block.tensor
        def _(pe):
            pe.wait_ge(loaded.sem, loaded.at(2))
            for k in range(KT):
                ins = pe.matmul(p_g[:, k * E:(k + 1) * E], a_raw[:, k * P:(k + 1) * P], b_raw[:, :],
                                start=True, stop=True)
            ins.then_inc(delta_made.sem, 1)
            pe.wait_ge(gate_made.sem, gate_made.at(1))
            for b in range(B):
                cols = slice(b * S, (b + 1) * S)
                for k in range(KT):
                    ins = three_pass(pe, p_l[b][:, :], g_hi[:, k, :], g_lo[:, k, :],
                                     K.xt_hi[:, k, cols], K.xt_lo[:, k, cols], k == 0, k == KT - 1)
                ins.then_inc(logits_made.sem, 1)
            for t in range(T):
                if t % TT == 0:
                    pe.wait_ge(logits_read.sem, logits_read.at(t // TT))
                ins = pe.transpose(p_t[:, t * E:(t + 1) * E], flat[:, t * P:(t + 1) * P], K.ident[0:E, 0:E])
            ins.then_inc(turned.sem, 1)

        @block.scalar
        def _(act):
            for b in range(B):
                act.wait_ge(logits_made.sem, logits_made.at(b))
                act.activation(flat[:, b * S:(b + 1) * S], p_l[b][0:E, :], ACT.Copy).then_inc(logits_read.sem, 1)
            act.wait_ge(shifted.sem, shifted.at(0))
            act.activation(prob[:, :, :], logit[:, :, :], ACT.Exp).then_inc(exp_made.sem, 1)

        @block.vector
        def _(dve):
            step = Count(steps)

            def over(ap, shape=(P, T, E)):
                return ap.to_broadcast(list(shape))

            dve.wait_ge(loaded.sem, loaded.at(2))
            dve.wait_ge(delta_made.sem, delta_made.at(0))
            dve.scalar_tensor_tensor(g_full[:, :, :], p_g[:, 0:KT * E].rearrange("p (k e) -> p k e", k=KT),
                                     2.0, g_raw[:, :, :], ALU.mult, ALU.add).then_inc(step.sem, 1)
            dve.wait_ge(step.sem, step.next())
            dve.wait_ge(zeroed.sem, zeroed.at(1))
            dve.tensor_copy(g_hi[:, :, 0:E], g_full[:, :, :]).then_inc(gate_made.sem, 1)
            dve.wait_ge(gate_made.sem, gate_made.at(0))
            dve.tensor_tensor(g_lo[:, :, 0:E], g_full[:, :, :], f32(g_hi[:, :, 0:E]),
                              ALU.subtract).then_inc(gate_made.sem, 1)
            dve.wait_ge(numbered.sem, numbered.at(0))
            dve.tensor_copy(number[:, :], number_i[:, :]).then_inc(step.sem, 1)
            dve.wait_ge(step.sem, step.next())
            dve.wait_ge(turned.sem, turned.at(0))
            dve.tensor_copy(logit[:, :, :],
                            p_t[:, 0:T * E].rearrange("p (t e) -> p t e", t=T)).then_inc(step.sem, 1)
            dve.wait_ge(step.sem, step.next())
            dve.tensor_reduce(most[:, :], logit[:, :, :], AX.X, ALU.max).then_inc(step.sem, 1)
            dve.wait_ge(step.sem, step.next())
            dve.tensor_tensor(logit[:, :, :], logit[:, :, :], over(most[:, :].unsqueeze(2)),
                              ALU.subtract).then_inc(shifted.sem, 1)
            dve.wait_ge(exp_made.sem, exp_made.at(0))
            dve.tensor_reduce(total[:, :], prob[:, :, :], AX.X, ALU.add).then_inc(step.sem, 1)
            dve.wait_ge(step.sem, step.next())
            dve.reciprocal(inv[:, :], total[:, :]).then_inc(step.sem, 1)
            dve.wait_ge(step.sem, step.next())
            dve.tensor_tensor(prob[:, :, :], prob[:, :, :], over(inv[:, :].unsqueeze(2)),
                              ALU.mult).then_inc(step.sem, 1)
            dve.wait_ge(step.sem, step.next())
            for t in range(T):
                ins = dve.max(top[:, t, :], prob[:, t, :])
            ins.then_inc(step.sem, 1)
            dve.wait_ge(step.sem, step.next())
            for t in range(T):
                ins = dve.max_index(index[:, t, :], top[:, t, :], prob[:, t, :])
            ins.then_inc(step.sem, 1)
            dve.wait_ge(step.sem, step.next())
            dve.tensor_copy(place[:, :, :], index[:, :, 0:2]).then_inc(step.sem, 1)
            dve.wait_ge(step.sem, step.next())
            every = number[:, :].unsqueeze(1).to_broadcast([P, T, E])
            dve.tensor_tensor(mask[:, :, :], every, over(place[:, :, 0:1]), ALU.is_equal)
            dve.tensor_tensor(other[:, :, :], every, over(place[:, :, 1:2]), ALU.is_equal).then_inc(step.sem, 1)
            dve.wait_ge(step.sem, step.next())
            dve.tensor_tensor(mask[:, :, :], mask[:, :, :], other[:, :, :], ALU.add).then_inc(step.sem, 1)
            dve.wait_ge(step.sem, step.next())
            dve.tensor_tensor(total[:, :], top[:, :, 0], top[:, :, 1], ALU.add).then_inc(step.sem, 1)
            dve.wait_ge(step.sem, step.next())
            dve.reciprocal(inv[:, :], total[:, :]).then_inc(step.sem, 1)
            dve.wait_ge(step.sem, step.next())
            dve.tensor_scalar(inv[:, :], inv[:, :], K.gates[:, 3:4], None, ALU.mult).then_inc(step.sem, 1)
            dve.wait_ge(step.sem, step.next())
            dve.tensor_tensor(mask[:, :, :], mask[:, :, :], prob[:, :, :], ALU.mult).then_inc(step.sem, 1)
            dve.wait_ge(step.sem, step.next())
            dve.tensor_tensor(K.route[:, :, :], mask[:, :, :], over(inv[:, :].unsqueeze(2)),
                              ALU.mult).then_inc(step.sem, 1)
            dve.wait_ge(step.sem, step.next())


def stage_experts(K, gup, down, gup_a, gup_b_t, down_a, down_b_t):
    with ExitStack() as ctx:
        sb, ps = K.scope(ctx)
        IT = I // P
        NC = KT + IT
        LR = 3 * 32
        w_raw = sb("e_w_raw", [P, NC, D])
        la_raw, lb_raw = sb("la_raw", [LR, D + I]), sb("lb_raw", [LR, 2 * D])
        la, lb = sb("la", [LR, D + I], F32R), sb("lb", [LR, 2 * D], F32R)
        w_hi, w_lo = sb("e_w_hi", [P, 2, NC, D], F32R), sb("e_w_lo", [P, 2, NC, D], F32R)
        silu = sb("e_silu", [P, IT, S])
        h_full = sb("e_h", [P, IT, S])
        h_hi, h_lo = sb("e_h_hi", [P, IT, S], F32R), sb("e_h_lo", [P, IT, S], F32R)
        p_h = [ps(f"e_h{n}") for n in range(3)]
        p_d = ps("e_d")
        p_y = [ps(f"e_y{t}") for t in range(TT)]
        H_BANK = [0, 1, 2, 0]

        raw_in = Signal(K, "e_weights_in", per=14, unit=16)
        zeroed = Signal(K, "e_zeroed")
        lora_hi = Signal(K, "e_lora_hi", per=2, credit=2)
        lora_lo = Signal(K, "e_lora_lo", per=2)
        delta_made = Signal(K, "e_delta", per=NC, credit=NC)
        merged = Signal(K, "e_merged", per=NC, credit=1)
        hi_made = Signal(K, "e_weights_hi", per=NC)
        lo_made = Signal(K, "e_weights_lo", per=NC, credit=1)
        h_made = Signal(K, "e_h_product", per=4 * B)
        silu_made = Signal(K, "e_silu_made", per=IT * B, credit=IT)
        h_full_made = Signal(K, "e_h_made", per=IT * B, credit=IT)
        h_hi_made = Signal(K, "e_h_hi_made", per=IT * B)
        h_lo_made = Signal(K, "e_h_lo_made", per=IT * B, credit=IT)
        y_made = Signal(K, "e_product", per=TT * B, credit=TT)
        y_added = Signal(K, "e_added", per=TT * B, credit=TT)
        block = ctx.enter_context(K.nc.Block())
        chunks_at = [[0, 1], [2, 3], [4, 5], []]

        def experts(eng, prepare, run):
            prepare(0, 0)
            with eng.Fori(0, E // 2 - 1) as i:
                for u in range(2):
                    run(i * 2 + u, u, True)
            run(E - 2, 0, True)
            run(E - 1, 1, False)

        def lora_rows(c):
            return slice(c * P, (c + 1) * P), slice(0, D) if c < KT else slice(D, 2 * D)

        @block.sync
        def _(sp):
            def load(e):
                at = slice(e, e + 1) if isinstance(e, int) else bass.ds(e, 1)
                sp.dma_start(w_raw[:, 0:KT, :],
                             gup[at].rearrange("a (k p) n -> p (a k) n", p=P)).then_inc(raw_in.sem, 16)
                sp.dma_start(w_raw[:, KT:NC, :],
                             down[at].rearrange("a (k p) n -> p (a k) n", p=P)).then_inc(raw_in.sem, 16)
                for s in range(3):
                    rows = slice(32 * s, 32 * s + R)
                    for dst, src in ((la_raw[rows, 0:D], gup_a), (la_raw[rows, D:D + I], down_a),
                                     (lb_raw[rows, 0:D], gup_b_t), (lb_raw[rows, D:2 * D], down_b_t)):
                        sp.dma_start(dst, src[at].rearrange("a r n -> (a r) n")).then_inc(raw_in.sem, 16)

            sp.wait_ge(zeroed.sem, zeroed.at(1))
            load(0)
            with sp.Fori(1, E) as e:
                sp.wait_ge(lo_made.sem, lo_made.at(-1, e))
                sp.sem_inc(K.apart, 1)
                sp.wait_ge(delta_made.sem, delta_made.at(-1, e))
                sp.sem_inc(K.apart, 1)
                load(e)

        @block.gpsimd
        def _(pool):
            pool.memset(la_raw[:, :], 0.0).then_inc(zeroed.sem, 1)
            pool.memset(lb_raw[:, :], 0.0).then_inc(zeroed.sem, 1)

        @block.scalar
        def _(act):
            act.sem_inc(silu_made.sem, silu_made.opening)
            act.sem_inc(lora_hi.sem, lora_hi.opening)

            def lora(e):
                act.wait_ge(raw_in.sem, raw_in.at(raw_in.per - 1, e))
                act.wait_ge(delta_made.sem, delta_made.at(-1, e))
                act.activation(la[:, :], la_raw[:, :], ACT.Copy).then_inc(lora_hi.sem, 1)
                act.activation(lb[:, :], lb_raw[:, :], ACT.Copy).then_inc(lora_hi.sem, 1)

            def chunk(e, u, c):
                act.wait_ge(merged.sem, merged.at(c, e))
                act.activation(w_hi[:, u, c, :], w_raw[:, c, :], ACT.Copy).then_inc(hi_made.sem, 1)

            def prepare(e, u):
                lora(e)
                for c in range(NC):
                    chunk(e, u, c)

            def run(e, u, more):
                for b in range(B):
                    if more and b == 0:
                        lora(e + 1)
                    for n in range(IT):
                        act.wait_ge(h_made.sem, h_made.at(4 * b + 2 * n, e))
                        act.wait_ge(h_full_made.sem, h_full_made.at(IT * (b - 1) + n, e))
                        act.activation(silu[:, n, :], p_h[H_BANK[2 * n]][:, :],
                                       ACT.Silu).then_inc(silu_made.sem, 1)
                        act.wait_ge(h_full_made.sem, h_full_made.at(IT * b + n, e))
                        if n == 0:
                            act.wait_ge(y_made.sem, y_made.at(TT * b - 1, e))
                        act.activation(h_hi[:, n, :], h_full[:, n, :], ACT.Copy).then_inc(h_hi_made.sem, 1)
                    if more:
                        for c in chunks_at[b]:
                            chunk(e + 1, 1 - u, c)

            experts(act, prepare, run)

        @block.vector
        def _(dve):
            for s in (merged, lo_made, h_full_made, h_lo_made, y_added):
                dve.sem_inc(s.sem, s.opening)

            def lora(e):
                dve.wait_ge(lora_hi.sem, lora_hi.at(1, e))
                rows = slice(64, 64 + 32)
                dve.tensor_tensor(la[rows, :], la_raw[rows, :], f32(la[rows, :]),
                                  ALU.subtract).then_inc(lora_lo.sem, 1)
                rows = slice(32, 32 + 32)
                dve.tensor_tensor(lb[rows, :], lb_raw[rows, :], f32(lb[rows, :]),
                                  ALU.subtract).then_inc(lora_lo.sem, 1)

            def merge(e, c):
                dve.wait_ge(delta_made.sem, delta_made.at(c, e))
                dve.scalar_tensor_tensor(w_raw[:, c, :], p_d[:, :], 2.0, w_raw[:, c, :],
                                         ALU.mult, ALU.add).then_inc(merged.sem, 1)

            def split(e, u, c):
                dve.wait_ge(hi_made.sem, hi_made.at(c, e))
                dve.tensor_tensor(w_lo[:, u, c, :], w_raw[:, c, :], f32(w_hi[:, u, c, :]),
                                  ALU.subtract).then_inc(lo_made.sem, 1)

            def prepare(e, u):
                lora(e)
                for c in range(NC):
                    merge(e, c)
                    split(e, u, c)

            def run(e, u, more):
                for b in range(B):
                    if more and b == 0:
                        lora(e + 1)
                    chunks = chunks_at[b] if more else []
                    for n in range(IT):
                        dve.wait_ge(h_made.sem, h_made.at(4 * b + 2 * n + 1, e))
                        dve.wait_ge(silu_made.sem, silu_made.at(IT * b + n, e))
                        dve.tensor_tensor(h_full[:, n, :], p_h[H_BANK[2 * n + 1]][:, :],
                                          silu[:, n, :], ALU.mult).then_inc(h_full_made.sem, 1)
                        if n < len(chunks):
                            merge(e + 1, chunks[n])
                        dve.wait_ge(h_hi_made.sem, h_hi_made.at(IT * b + n, e))
                        dve.tensor_tensor(h_lo[:, n, :], h_full[:, n, :], f32(h_hi[:, n, :]),
                                          ALU.subtract).then_inc(h_lo_made.sem, 1)
                    for t in range(TT):
                        dve.wait_ge(y_made.sem, y_made.at(TT * b + t, e))
                        route = K.route[:, b * TT + t, bass.ds(e, 1) if not isinstance(e, int)
                                        else slice(e, e + 1)]
                        dve.scalar_tensor_tensor(K.x[:, b * TT + t, :], p_y[t][:, :], route,
                                                 K.x[:, b * TT + t, :], ALU.mult, ALU.add).then_inc(y_added.sem, 1)
                        if t < len(chunks):
                            split(e + 1, 1 - u, chunks[t])

            experts(dve, prepare, run)

        @block.tensor
        def _(pe):
            pe.sem_inc(delta_made.sem, delta_made.opening)
            pe.sem_inc(y_made.sem, y_made.opening)

            def delta(e, c):
                if c == 0:
                    pe.wait_ge(lora_lo.sem, lora_lo.at(1, e))
                pe.wait_ge(merged.sem, merged.at(c - 1, e))
                rows, cols = lora_rows(c)
                pe.matmul(p_d[:, :], la[:, rows], lb[:, cols], start=True, stop=True).then_inc(delta_made.sem, 1)

            def prepare(e, u):
                for c in range(NC):
                    delta(e, c)

            def hidden(e, u, b, n, half):
                m = 2 * n + half
                if m == 0:
                    pe.wait_ge(h_full_made.sem, h_full_made.at(IT * b - 1, e))
                elif m == 3:
                    pe.wait_ge(silu_made.sem, silu_made.at(IT * b, e))
                elif m == 1:
                    pe.wait_ge(h_full_made.sem, h_full_made.at(IT * (b - 1), e))
                else:
                    pe.wait_ge(silu_made.sem, silu_made.at(IT * (b - 1) + 1, e))
                rows = slice(half * I + n * P, half * I + (n + 1) * P)
                cols = slice(b * S, (b + 1) * S)
                for k in range(KT):
                    ins = three_pass(pe, p_h[H_BANK[m]][:, :], w_hi[:, u, k, rows], w_lo[:, u, k, rows],
                                     K.xt_hi[:, k, cols], K.xt_lo[:, k, cols], k == 0, k == KT - 1)
                ins.then_inc(h_made.sem, 1)

            def output(e, u, b, n):
                pe.wait_ge(h_lo_made.sem, h_lo_made.at(IT * b + n, e))
                for t in range(TT):
                    if n == 0:
                        pe.wait_ge(y_added.sem, y_added.at(TT * (b - 1) + t, e))
                    rows = slice(t * P, (t + 1) * P)
                    ins = three_pass(pe, p_y[t][:, :], h_hi[:, n, rows], h_lo[:, n, rows],
                                     w_hi[:, u, KT + n, :], w_lo[:, u, KT + n, :], n == 0, n == IT - 1)
                    if n == IT - 1:
                        ins.then_inc(y_made.sem, 1)

            def run(e, u, more):
                pe.wait_ge(lo_made.sem, lo_made.at(NC - 1, e))
                for b in range(B):
                    chunks = chunks_at[b] if more else []
                    for n in range(IT):
                        for half in range(2):
                            hidden(e, u, b, n, half)
                        if n < len(chunks):
                            delta(e + 1, chunks[n])
                    for n in range(IT):
                        output(e, u, b, n)

            experts(pe, prepare, run)


def stage_store(K, out):
    with ExitStack() as ctx:
        stored = Signal(K, "result_stored", unit=16)
        block = ctx.enter_context(K.nc.Block())

        @block.sync
        def _(sp):
            sp.dma_start(out.rearrange("(t p) d -> p t d", p=P), K.x[:, :, :]).then_inc(stored.sem, 16)
            sp.wait_ge(stored.sem, stored.at(0))


def flamingo_kernel(nc, a, out, stages=9):
    keys = nc.dram_tensor("keys_split", (B, P, 2, G, S), F32, kind="Internal").ap()
    values = nc.dram_tensor("values_split", (B, P, TT, 2, G * DH), F32, kind="Internal").ap()
    with ExitStack() as ctx:
        K = Kernel(nc, ctx)
        sb, _ = K.scope(ctx)
        K.x = sb("x", [P, T, D])
        K.ident = sb("ident", [P, P])
        K.power = sb("power", [P, 16])
        K.gates_raw, K.gates = sb("gates_raw", [P, 4]), sb("gates", [P, 4])
        K.ln_eps = sb("ln_eps", [P, TT])
        K.gates_made = Signal(K, "gates_made")
        K.apart = ctx.enter_context(nc.semaphore("wait_stands_alone"))
        stage_context(K, a["x"], a["ctx_t"], a["L1_xattn_Wk"], a["L1_xattn_Wv"], a["L1_xattn_k_norm_w"],
                      a["g_xattn"], a["g_ffn"], keys, values)
        if stages >= 2:
            K.xt_hi, K.xt_lo = sb("xt_hi", [P, KT, B * S], F32R), sb("xt_lo", [P, KT, B * S], F32R)
            stage_norm(K, "n1")
            stage_ffn(K, a["w1_t"], a["w2_t"], a["b1_t"], a["L0_ffn_b2"])
        if stages >= 3:
            stage_norm(K, "n2")
            stage_attention(K, a["L1_xattn_Wq"], a["L1_xattn_Wo"], a["L1_xattn_q_norm_w"], keys, values)
        if stages >= 4:
            K.route = sb("route", [P, T, E])
            stage_norm(K, "n3")
            stage_router(K, a["gate_t"], a["L1_ffn_gate_lora_A"], a["gate_b_t"])
            stage_experts(K, a["L1_ffn_gate_up_proj"], a["L1_ffn_down_proj"], a["L1_ffn_gup_lora_A"],
                          a["gup_b_t"], a["L1_ffn_down_lora_A"], a["down_b_t"])
        stage_store(K, out)


def kernel(**inputs):
    import numpy as np
    import concourse.bacc as bacc
    from concourse.bass_utils import run_bass_kernel_spmd

    given = {k: np.asarray(v) for k, v in inputs.items()}
    turned = {
        "x": given["x"].reshape(B * S, D),
        "ctx_t": given["ctx_2048"].transpose(0, 2, 1),
        "w1_t": given["L0_ffn_w1"].T,
        "w2_t": given["L0_ffn_w2"].T,
        "b1_t": given["L0_ffn_b1"].reshape(FT, P).T,
        "gate_t": given["L1_ffn_gate_weight"].T,
        "gate_b_t": given["L1_ffn_gate_lora_B"].T,
        "gup_b_t": given["L1_ffn_gup_lora_B"].transpose(0, 2, 1),
        "down_b_t": given["L1_ffn_down_lora_B"].transpose(0, 2, 1),
    }
    same = ["g_xattn", "g_ffn", "L0_ffn_b2", "L1_xattn_Wq", "L1_xattn_Wk", "L1_xattn_Wv",
            "L1_xattn_Wo", "L1_xattn_q_norm_w", "L1_xattn_k_norm_w", "L1_ffn_gate_lora_A",
            "L1_ffn_gate_up_proj", "L1_ffn_down_proj", "L1_ffn_gup_lora_A", "L1_ffn_down_lora_A"]
    nc = bacc.Bacc("TRN2", target_bir_lowering=False, num_devices=1)
    arrays, aps = {}, {}
    for name, a in [*turned.items(), *((n, given[n]) for n in same)]:
        arrays[f"in_{name}"] = np.ascontiguousarray(a)
        aps[name] = nc.dram_tensor(f"in_{name}", a.shape, mybir.dt.from_np(a.dtype), kind="ExternalInput").ap()
    out = nc.dram_tensor("out", (B * S, D), F32, kind="ExternalOutput").ap()
    flamingo_kernel(nc, aps, out)
    r = run_bass_kernel_spmd(nc, [arrays], core_ids=[0])
    return r.results[0]["out"].reshape(B, S, D)
```

```python
from contextlib import ExitStack

import concourse.bass as bass
from concourse import mybir

F32 = mybir.dt.float32
F32R = mybir.dt.float32r
U32 = mybir.dt.uint32
ALU = mybir.AluOpType
ACT = mybir.ActivationFunctionType
AX = mybir.AxisListType

P = 128
B, S, D = 4, 512, 512
KT = D // P
TT = S // P
T = B * TT
F = 2048
FT = F // P
NH, G, DH = 16, 4, 128
HG = NH // G
E, I, R = 8, 256, 16
LN_EPS, RMS_EPS = 1e-5, 1e-6
FP8_MAX = 448.0
ACT_EPS, W_EPS = 1e-4, 1e-6
EXPONENT = 0x7F800000
FP8_LEAST = 2.0 ** -6
FP8_SHIFT = 1.5 * 2.0 ** 20


class Signal:

    def __init__(self, K, name, per=1, credit=0, unit=1):
        self.sem = K.ctx.enter_context(K.nc.semaphore(name))
        self.per, self.credit, self.unit = per, credit, unit
        self.opening = credit * unit

    def at(self, n, i=0):
        assert not isinstance(i, int) or self.credit + i * self.per + n >= 0
        return i * (self.per * self.unit) + (self.credit + n + 1) * self.unit

    def given(self, n, i):
        return not isinstance(i, int) or i * self.per + n >= 0


class Count:

    def __init__(self, signal, i=0):
        self.sem, self.signals, self.i, self.n = signal.sem, signal, i, 0

    def next(self):
        self.n += 1
        return self.signals.at(self.n - 1, self.i)


class Kernel:

    def __init__(self, nc, ctx):
        self.nc, self.ctx = nc, ctx

    def scope(self, ctx):
        nc = self.nc

        def sb(name, shape, dt=F32):
            return ctx.enter_context(nc.sbuf_tensor(name, shape, dt))

        def ps(name, shape=(P, 512)):
            return ctx.enter_context(nc.psum_tensor(name, list(shape), F32))

        return sb, ps


def three_pass(pe, out, lhs_hi, lhs_lo, rhs_hi, rhs_lo, start, stop):
    pe.matmul(out, lhs_hi, rhs_hi, start=start, stop=False)
    pe.matmul(out, lhs_hi, rhs_lo, start=False, stop=False)
    return pe.matmul(out, lhs_lo, rhs_hi, start=False, stop=stop)


def f32(ap):
    return ap.bitcast(F32)


def layer_norm_stats(dve, x, stats, mv, step, apart):
    for t in range(TT):
        ins = dve.bn_stats(stats[:, t, :], x[:, t, :])
    ins.then_inc(step.sem, 1)
    dve.wait_ge(step.sem, step.next())
    dve.sem_inc(apart, 1)
    for t in range(TT):
        ins = dve.bn_aggr(mv[:, t, :], stats[:, t, :])
    return ins


def block_scales(dve, step, scale, least, out_scale, safe, amax):
    dve.tensor_scalar(safe, amax, least, None, ALU.max).then_inc(step.sem, 1)
    dve.wait_ge(step.sem, step.next())
    dve.reciprocal(scale, safe).then_inc(step.sem, 1)
    dve.wait_ge(step.sem, step.next())
    dve.tensor_scalar(scale, scale, FP8_MAX, None, ALU.mult)
    return dve.tensor_scalar(out_scale, safe, 1.0 / FP8_MAX, None, ALU.mult)


def round_blocks(dve, step, v, grid):
    dve.tensor_scalar(grid.bitcast(U32), v.bitcast(U32), EXPONENT, None, ALU.bitwise_and).then_inc(step.sem, 1)
    dve.wait_ge(step.sem, step.next())
    dve.tensor_scalar(grid, grid, FP8_LEAST, FP8_SHIFT, ALU.max, ALU.mult).then_inc(step.sem, 1)
    dve.wait_ge(step.sem, step.next())
    dve.tensor_tensor(v, v, grid, ALU.add).then_inc(step.sem, 1)
    dve.wait_ge(step.sem, step.next())
    return dve.tensor_tensor(v, v, grid, ALU.subtract)


def stage_context(K, x, ctx_t, wk, wv, k_norm_w, g_xattn, g_ffn, w1_t, keys, values):
    nc = K.nc
    with ExitStack() as ctx:
        sb, ps = K.scope(ctx)
        wk_hi, wv_hi, c_hi, cq_hi = (K.xt_hi[:, n, :].rearrange("p (k n) -> p k n", k=KT) for n in range(4))
        wk_lo, wv_lo, c_lo, cq_lo = (K.xt_lo[:, n, :].rearrange("p (k n) -> p k n", k=KT) for n in range(4))
        c_raw = sb("c_raw", [P, 2, KT, S])
        grid = sb("grid", [P, KT * 4, P])
        xn = sb("c_xn", [P, TT, D])
        xq_hi, xq_lo = sb("xq_hi", [P, KT, S], F32R), sb("xq_lo", [P, KT, S], F32R)
        k_out = sb("k_out", [P, 2, G, S], F32R)
        v_out = sb("v_out", [P, TT, 2, G * DH], F32R)
        v_full = sb("v_full", [P, 2, G * DH])
        k_sq = sb("k_sq", [P, G * DH])
        k_ms = sb("k_ms", [P, 2, G])
        k_eps = sb("k_eps", [P, 2, G])
        k_rstd = sb("k_rstd", [P, 2, G])
        k_nrm = sb("k_nrm", [P, 2, G * DH])
        k_full = sb("k_full", [P, 2, G * P])
        kw = sb("kw", [P, 1])
        blocks = [sb(f"q_{n}", [P, KT * 4]) for n in ("amax", "amax_all", "safe", "scale", "back", "x_amax",
                                                       "x_safe", "x_scale", "x_back")]
        amax, amax_all, safe, scale, back, x_amax, x_safe, x_scale, x_back = (t[:, :] for t in blocks)
        stats = sb("c_stats", [P, TT, 6])
        mv = sb("c_mv", [P, TT, 2])
        veps = sb("c_veps", [P, TT])
        rstd = sb("c_rstd", [P, TT])

        p_key = [ps(f"p_key{n}") for n in range(2)]
        p_val = [ps(f"p_val{n}") for n in range(2)]
        p_kt = ps("p_kt")
        p_x = [ps(f"p_x{n}") for n in range(3)]
        p_x.append(p_x[0])

        w_in = [Signal(K, f"c_weight{n}_in", unit=16) for n in range(2)]
        gates_in = Signal(K, "c_gates_in", unit=16)
        kw_in = Signal(K, "c_key_norm_in", unit=16)
        ctx_in = Signal(K, "c_context_in", unit=16)
        x_in = Signal(K, "c_x_in", unit=16)
        w_hi = Signal(K, "c_weight_hi")
        w_lo = Signal(K, "c_weight_lo")
        ident_made = Signal(K, "c_ident_made")
        ctx_hi = Signal(K, "c_context_hi")
        ctx_lo = Signal(K, "c_context_lo")
        ctx_lo0 = Signal(K, "c_first_context_lo")
        ctx_amax = Signal(K, "c_context_amax")
        ctx_amax_all = Signal(K, "c_context_amax_all")
        ctx_rounded = Signal(K, "c_context_rounded")
        ctx_quant = Signal(K, "c_context_quantised")
        cq_hi_made = Signal(K, "c_cq_hi")
        cq_lo_made = Signal(K, "c_cq_lo")
        x_var = Signal(K, "c_x_variance")
        x_rstd = Signal(K, "c_x_rstd")
        x_quant = Signal(K, "c_x_quantised")
        key_made = Signal(K, "c_key_product", per=TT)
        val_made = Signal(K, "c_value_product", per=TT)
        val_copied = Signal(K, "c_value_copied", per=TT)
        val_lo = Signal(K, "c_value_lo", per=TT)
        key_sq = Signal(K, "c_key_squares", per=TT)
        key_rstd = Signal(K, "c_key_rstd", per=TT)
        key_nrm = Signal(K, "c_key_normalised", per=TT)
        key_turned = Signal(K, "c_key_transposed", per=TT)
        key_full = Signal(K, "c_key_full", per=TT)
        key_lo = Signal(K, "c_key_lo", per=TT)
        kv_out = Signal(K, "c_kv_stored", per=2, unit=16)
        x_turned = Signal(K, "c_x_transposed", per=KT)
        xq_hi_made = Signal(K, "c_xq_hi", per=KT)
        xq_lo_made = Signal(K, "c_xq_lo", per=KT)
        y_made = Signal(K, "c_product", per=TT, credit=TT)
        y_added = Signal(K, "c_added", per=TT, credit=TT)
        v_steps = Signal(K, "c_vector_steps", per=18)
        p_steps = Signal(K, "c_pool_steps", per=1 + TT)
        block = ctx.enter_context(nc.Block())

        def context(b):
            return c_raw[:, bass.ds(b % 2, 1), :, :].rearrange("p s k n -> p (s k) n")

        @block.sync
        def _(sp):
            def load(b):
                if ctx_in.given(-1, b):
                    if cq_lo_made.given(-2, b):
                        sp.wait_ge(cq_lo_made.sem, cq_lo_made.at(-2, b))
                        sp.sem_inc(K.apart, 1)
                    sp.wait_ge(ctx_in.sem, ctx_in.at(-1, b))
                    sp.sem_inc(K.apart, 1)
                    sp.wait_ge(x_in.sem, x_in.at(-1, b))
                    sp.sem_inc(K.apart, 1)
                sp.dma_start(context(b), ctx_t[bass.ds(b, 1)].rearrange("a (k p) n -> p (a k) n",
                                                                        p=P)).then_inc(ctx_in.sem, 16)
                sp.dma_start(K.x[:, bass.ds(b * TT, TT), :],
                             x[bass.ds(b * S, S), :].rearrange("(t p) d -> p t d", p=P)).then_inc(x_in.sem, 16)

            def store(b):
                sp.wait_ge(key_lo.sem, key_lo.at(TT - 1, b))
                sp.sem_inc(K.apart, 1)
                sp.wait_ge(val_lo.sem, val_lo.at(TT - 1, b))
                sp.sem_inc(K.apart, 1)
                sp.dma_start(keys[bass.ds(b, 1)].rearrange("a p h g n -> p (a h) g n"),
                             f32(k_out[:, :, :, :])).then_inc(kv_out.sem, 16)
                sp.dma_start(values[bass.ds(b, 1)].rearrange("a p t h n -> p (a t) h n"),
                             f32(v_out[:, :, :, :])).then_inc(kv_out.sem, 16)

            sp.dma_start(xn[:, :, :], wk.rearrange("(k p) n -> p k n", p=P)).then_inc(w_in[0].sem, 16)
            load(0)
            sp.dma_start(grid[:, :, :].rearrange("p (k c) n -> p k (c n)", k=KT),
                         wv.rearrange("(k p) n -> p k n", p=P)).then_inc(w_in[1].sem, 16)
            sp.dma_start(kw[:, :], k_norm_w.rearrange("(p a) -> p a", a=1)).then_inc(kw_in.sem, 16)
            sp.dma_start(K.gates_raw[:, 0:2], g_xattn.partition_broadcast(P)).then_inc(gates_in.sem, 16)
            sp.dma_start(K.gates_raw[:, 2:4], g_ffn.partition_broadcast(P)).then_inc(gates_in.sem, 16)
            load(1)
            store(0)
            sp.dma_start(K.w_early[0][:, :, :].rearrange("p k n -> p (k n)"),
                         w1_t[0:P, :]).then_inc(K.w1_in[0].sem, 16)
            with sp.Fori(1, B - 1) as b:
                load(b + 1)
                store(b)
            sp.dma_start(K.w_early[1][:, :, :].rearrange("p k n -> p (k n)"),
                         w1_t[P:2 * P, :]).then_inc(K.w1_in[1].sem, 16)
            store(B - 1)
            sp.wait_ge(kv_out.sem, kv_out.at(1, B - 1))

        @block.scalar
        def _(act):
            def split_context(b):
                act.wait_ge(ctx_in.sem, ctx_in.at(0, b))
                if val_made.given(-1, b):
                    act.wait_ge(val_made.sem, val_made.at(-1, b))
                act.activation(c_hi[:, :, :], context(b), ACT.Copy).then_inc(ctx_hi.sem, 1)

            def copy_values(b, j):
                act.wait_ge(val_made.sem, val_made.at(j, b))
                if j == 0 and kv_out.given(-1, b):
                    act.wait_ge(kv_out.sem, kv_out.at(-1, b))
                if val_lo.given(j - 2, b):
                    act.wait_ge(val_lo.sem, val_lo.at(j - 2, b))
                act.activation(v_out[:, j, 0, :], p_val[j % 2][:, :], ACT.Copy)
                act.activation(v_full[:, j % 2, :], p_val[j % 2][:, :], ACT.Copy).then_inc(val_copied.sem, 1)

            def squares(b, j):
                act.wait_ge(key_made.sem, key_made.at(j, b))
                if key_rstd.given(j - 2, b):
                    act.wait_ge(key_rstd.sem, key_rstd.at(j - 2, b))
                if key_sq.given(j - 1, b):
                    act.wait_ge(key_sq.sem, key_sq.at(j - 1, b))
                for g in range(G):
                    cols = slice(g * DH, (g + 1) * DH)
                    ins = act.activation(k_sq[:, cols], p_key[j % 2][:, cols], ACT.Square,
                                         accum_out=k_ms[:, j % 2, g:g + 1])
                ins.then_inc(key_sq.sem, 1)

            def normalise_keys(b, j):
                act.wait_ge(key_rstd.sem, key_rstd.at(j, b))
                if key_turned.given(j - 2, b):
                    act.wait_ge(key_turned.sem, key_turned.at(j - 2, b))
                for g in range(G):
                    cols = slice(g * DH, (g + 1) * DH)
                    ins = act.activation(k_nrm[:, j % 2, cols], p_key[j % 2][:, cols], ACT.Copy,
                                         scale=k_rstd[:, j % 2, g:g + 1])
                ins.then_inc(key_nrm.sem, 1)

            def keys_out(b, j):
                act.wait_ge(key_turned.sem, key_turned.at(j, b))
                if key_lo.given(j - 2, b):
                    act.wait_ge(key_lo.sem, key_lo.at(j - 2, b))
                act.activation(k_out[:, 0, :, j * P:(j + 1) * P], p_kt[:, :].rearrange("p (g n) -> p g n", g=G),
                               ACT.Copy, scale=kw[:, 0:1])
                act.activation(k_full[:, j % 2, :], p_kt[:, :], ACT.Copy,
                               scale=kw[:, 0:1]).then_inc(key_full.sem, 1)

            def keys_and_values(b):
                for j in range(TT + 1):
                    if j < TT:
                        squares(b, j)
                    if j >= 1:
                        normalise_keys(b, j - 1)
                    if j < TT:
                        copy_values(b, j)
                    if j >= 1:
                        keys_out(b, j - 1)

            def split_product(b):
                act.wait_ge(ctx_quant.sem, ctx_quant.at(0, b))
                if y_made.given(-1, b):
                    act.wait_ge(y_made.sem, y_made.at(-1, b))
                act.activation(cq_hi[:, :, :], context(b), ACT.Copy).then_inc(cq_hi_made.sem, 1)
                for k in range(KT):
                    act.wait_ge(x_turned.sem, x_turned.at(k, b))
                    act.activation(xq_hi[:, k, :], p_x[k][:, :], ACT.Copy).then_inc(xq_hi_made.sem, 1)

            act.wait_ge(w_in[0].sem, w_in[0].at(0))
            act.activation(wk_hi[:, :, :], xn[:, :, :], ACT.Copy).then_inc(w_hi.sem, 1)
            split_context(0)
            act.wait_ge(w_in[1].sem, w_in[1].at(0))
            act.activation(wv_hi[:, :, :].rearrange("p k (c n) -> p (k c) n", n=P), grid[:, :, :],
                           ACT.Copy).then_inc(w_hi.sem, 1)
            act.wait_ge(gates_in.sem, gates_in.at(1))
            act.activation(K.gates[:, :], K.gates_raw[:, :], ACT.Tanh).then_inc(K.gates_made.sem, 1)
            act.wait_ge(kw_in.sem, kw_in.at(0))
            keys_and_values(0)
            with act.Fori(1, B) as b:
                split_context(b)
                split_product(b - 1)
                keys_and_values(b)
            split_product(B - 1)

        @block.gpsimd
        def _(pool):
            def start(b):
                if isinstance(b, int):
                    pool.sem_inc(ctx_lo.sem, 1)
                else:
                    pool.wait_ge(ctx_hi.sem, ctx_hi.at(0, b))
                    pool.sem_inc(K.apart, 1)
                    pool.tensor_tensor(c_lo[:, :, :], context(b), f32(c_hi[:, :, :]),
                                       ALU.subtract).then_inc(ctx_lo.sem, 1)
                pool.wait_ge(ctx_amax.sem, ctx_amax.at(0, b))
                pool.sem_inc(K.apart, 1)
                pool.partition_all_reduce(amax_all, amax, P,
                                          bass.bass_isa.ReduceOp.max).then_inc(ctx_amax_all.sem, 1)
                pool.wait_ge(x_var.sem, x_var.at(0, b))
                pool.sem_inc(K.apart, 1)
                pool.tensor_scalar(veps[:, :], mv[:, :, 1], LN_EPS, None, ALU.add).then_inc(p_steps.sem, 1)
                pool.wait_ge(p_steps.sem, p_steps.at(0, b))
                pool.tensor_tensor(rstd[:, :], veps[:, :], K.power[:, 0:TT], ALU.pow).then_inc(x_rstd.sem, 1)

            def key_scale(b, j):
                pool.wait_ge(key_sq.sem, key_sq.at(j, b))
                if key_nrm.given(j - 2, b):
                    pool.wait_ge(key_nrm.sem, key_nrm.at(j - 2, b))
                pool.sem_inc(K.apart, 1)
                pool.tensor_scalar(k_eps[:, j % 2, :], k_ms[:, j % 2, :], 1.0 / DH, RMS_EPS,
                                   ALU.mult, ALU.add).then_inc(p_steps.sem, 1)
                pool.wait_ge(p_steps.sem, p_steps.at(1 + j, b))
                pool.tensor_tensor(k_rstd[:, j % 2, :], k_eps[:, j % 2, :], K.power[:, 0:G],
                                   ALU.pow).then_inc(key_rstd.sem, 1)

            def values_lo(b, j):
                pool.wait_ge(val_copied.sem, val_copied.at(j, b))
                pool.tensor_tensor(v_out[:, j, 1, :], v_full[:, j % 2, :],
                                   f32(v_out[:, j, 0, :]), ALU.subtract).then_inc(val_lo.sem, 1)

            def keys_lo(b, j):
                cols = slice(j * P, (j + 1) * P)
                pool.wait_ge(key_full.sem, key_full.at(j, b))
                pool.tensor_tensor(k_out[:, 1, :, cols], k_full[:, j % 2, :].rearrange("p (g n) -> p g n", g=G),
                                   f32(k_out[:, 0, :, cols]), ALU.subtract).then_inc(key_lo.sem, 1)

            def split_product(b):
                pool.wait_ge(cq_hi_made.sem, cq_hi_made.at(0, b))
                pool.sem_inc(K.apart, 1)
                pool.tensor_tensor(cq_lo[:, :, :], context(b), f32(cq_hi[:, :, :]),
                                   ALU.subtract).then_inc(cq_lo_made.sem, 1)

            def batch(b, after):
                start(b)
                for j in range(TT):
                    key_scale(b, j)
                    if j == 1 and after:
                        split_product(b - 1)
                    if j == 0 and kv_out.given(-1, b):
                        pool.wait_ge(kv_out.sem, kv_out.at(-1, b))
                    values_lo(b, j)
                    if j >= 1:
                        keys_lo(b, j - 1)
                keys_lo(b, TT - 1)
                c_blocks = context(b).rearrange("p k (c n) -> p (k c) n", n=P)
                pool.wait_ge(ctx_rounded.sem, ctx_rounded.at(0, b))
                pool.sem_inc(K.apart, 1)
                pool.tensor_tensor(c_blocks, c_blocks, back.unsqueeze(2).to_broadcast([P, KT * TT, P]),
                                   ALU.mult).then_inc(ctx_quant.sem, 1)

            pool.memset(K.power[:, :], -0.5)
            pool.memset(K.ln_eps[:, :], LN_EPS)
            pool.memset(K.ident[:, :], 0.0).then_inc(ident_made.sem, 1)
            pool.wait_ge(ident_made.sem, ident_made.at(0))
            pool.affine_select(out=K.ident[:, :], in_=K.ident[:, :], compare_op=ALU.not_equal, fill=1.0,
                               base=0, pattern=[[-1, P]], channel_multiplier=1).then_inc(ident_made.sem, 1)
            batch(0, False)
            with pool.Fori(1, B) as b:
                batch(b, True)
            split_product(B - 1)

        @block.vector
        def _(dve):
            def context_amax(b):
                dve.wait_ge(ctx_in.sem, ctx_in.at(0, b))
                dve.tensor_reduce(amax, context(b).rearrange("p k (c n) -> p (k c) n", n=P), AX.X, ALU.max,
                                  apply_absolute_value=True).then_inc(ctx_amax.sem, 1)

            def split_product(b):
                for k in range(KT):
                    dve.wait_ge(xq_hi_made.sem, xq_hi_made.at(k, b))
                    dve.tensor_tensor(xq_lo[:, k, :], p_x[k][:, :], f32(xq_hi[:, k, :]),
                                      ALU.subtract).then_inc(xq_lo_made.sem, 1)

            def add(b, t):
                xt = K.x[:, bass.ds(b * TT + t, 1), :].rearrange("p a n -> p (a n)")
                dve.wait_ge(y_made.sem, y_made.at(t, b))
                dve.scalar_tensor_tensor(xt, p_x[t][:, :], K.gates[:, 0:1], xt,
                                         ALU.mult, ALU.add).then_inc(y_added.sem, 1)

            def quantise_operands(b, add_product):
                step = Count(v_steps, b)
                xs = K.x[:, bass.ds(b * TT, TT), :]
                dve.wait_ge(x_in.sem, x_in.at(0, b))
                layer_norm_stats(dve, xs, stats, mv, step, K.apart).then_inc(x_var.sem, 1)
                c_blocks = context(b).rearrange("p k (c n) -> p (k c) n", n=P)
                dve.wait_ge(ctx_amax_all.sem, ctx_amax_all.at(0, b))
                dve.wait_ge(ctx_hi.sem, ctx_hi.at(0, b))
                if isinstance(b, int):
                    dve.wait_ge(ctx_lo0.sem, ctx_lo0.at(0))
                dve.wait_ge(ctx_lo.sem, ctx_lo.at(0, b))
                block_scales(dve, step, scale, W_EPS, back, safe, amax_all).then_inc(step.sem, 1)
                dve.wait_ge(step.sem, step.next())
                dve.tensor_tensor(c_blocks, c_blocks, scale.unsqueeze(2).to_broadcast([P, KT * TT, P]),
                                  ALU.mult).then_inc(step.sem, 1)
                dve.wait_ge(step.sem, step.next())
                round_blocks(dve, step, c_blocks, grid[:, :, :]).then_inc(ctx_rounded.sem, 1)
                dve.wait_ge(ctx_rounded.sem, ctx_rounded.at(0, b))
                dve.wait_ge(x_rstd.sem, x_rstd.at(0, b))
                if x_turned.given(-1, b):
                    dve.wait_ge(x_turned.sem, x_turned.at(-1, b))
                for t in range(TT):
                    ins = dve.tensor_scalar(xn[:, t, :], xs[:, t, :], mv[:, t, 0:1], rstd[:, t:t + 1],
                                            ALU.subtract, ALU.mult)
                ins.then_inc(step.sem, 1)
                dve.wait_ge(step.sem, step.next())
                x_blocks = xn[:, :, :].rearrange("p t (c n) -> p (t c) n", n=P)
                dve.tensor_reduce(x_amax, x_blocks, AX.X, ALU.max, apply_absolute_value=True).then_inc(step.sem, 1)
                dve.wait_ge(step.sem, step.next())
                block_scales(dve, step, x_scale, ACT_EPS, x_back, x_safe, x_amax).then_inc(step.sem, 1)
                dve.wait_ge(step.sem, step.next())
                dve.tensor_tensor(x_blocks, x_blocks, x_scale.unsqueeze(2).to_broadcast([P, TT * KT, P]),
                                  ALU.mult).then_inc(step.sem, 1)
                dve.wait_ge(step.sem, step.next())
                round_blocks(dve, step, x_blocks, grid[:, :, :]).then_inc(step.sem, 1)
                dve.wait_ge(step.sem, step.next())
                if add_product:
                    add(b - 1, 0)
                dve.tensor_tensor(x_blocks, x_blocks, x_back.unsqueeze(2).to_broadcast([P, TT * KT, P]),
                                  ALU.mult).then_inc(x_quant.sem, 1)
                if add_product:
                    for t in range(1, TT):
                        add(b - 1, t)
                assert step.n == v_steps.per

            dve.sem_inc(y_added.sem, y_added.opening)
            for n, (raw, hi, lo) in enumerate(((xn[:, :, :], wk_hi, wk_lo),
                                               (grid[:, :, :].rearrange("p (k c) n -> p k (c n)", k=KT),
                                                wv_hi, wv_lo))):
                dve.wait_ge(w_hi.sem, w_hi.at(n))
                dve.tensor_tensor(lo[:, :, :], raw, f32(hi[:, :, :]), ALU.subtract).then_inc(w_lo.sem, 1)
                if n == 0:
                    dve.wait_ge(ctx_hi.sem, ctx_hi.at(0))
                    dve.tensor_tensor(c_lo, context(0), f32(c_hi), ALU.subtract).then_inc(ctx_lo0.sem, 1)
                    context_amax(0)
            dve.wait_ge(K.gates_made.sem, K.gates_made.at(0))
            dve.wait_ge(w_lo.sem, w_lo.at(1))
            quantise_operands(0, False)
            with dve.Fori(1, B) as b:
                context_amax(b)
                split_product(b - 1)
                quantise_operands(b, True)
            split_product(B - 1)
            for t in range(TT):
                add(B - 1, t)

        @block.tensor
        def _(pe):
            def key_and_value_products(b, j):
                rows = slice(j * P, (j + 1) * P)
                if key_nrm.given(j - 2, b):
                    pe.wait_ge(key_nrm.sem, key_nrm.at(j - 2, b))
                if j == 0 and not val_copied.given(-1, b):
                    pe.wait_ge(w_lo.sem, w_lo.at(0))
                for k in range(KT):
                    ins = three_pass(pe, p_key[j % 2][:, :], c_hi[:, k, rows], c_lo[:, k, rows],
                                     wk_hi[:, k, :], wk_lo[:, k, :], k == 0, k == KT - 1)
                ins.then_inc(key_made.sem, 1)
                if val_copied.given(j - 2, b):
                    pe.wait_ge(val_copied.sem, val_copied.at(j - 2, b))
                else:
                    pe.wait_ge(w_lo.sem, w_lo.at(1))
                for k in range(KT):
                    ins = three_pass(pe, p_val[j % 2][:, :], c_hi[:, k, rows], c_lo[:, k, rows],
                                     wv_hi[:, k, :], wv_lo[:, k, :], k == 0, k == KT - 1)
                ins.then_inc(val_made.sem, 1)

            def turn_keys(b, j):
                pe.wait_ge(key_nrm.sem, key_nrm.at(j, b))
                if key_full.given(j - 1, b):
                    pe.wait_ge(key_full.sem, key_full.at(j - 1, b))
                for g in range(G):
                    ins = pe.transpose(p_kt[:, g * P:(g + 1) * P], k_nrm[:, j % 2, g * DH:(g + 1) * DH],
                                       K.ident[:, :])
                ins.then_inc(key_turned.sem, 1)

            def keys_and_values(b):
                if isinstance(b, int):
                    pe.wait_ge(ctx_lo0.sem, ctx_lo0.at(0))
                pe.wait_ge(ctx_lo.sem, ctx_lo.at(0, b))
                pe.wait_ge(ctx_hi.sem, ctx_hi.at(0, b))
                for j in range(TT):
                    key_and_value_products(b, j)
                    if j >= 1:
                        turn_keys(b, j - 1)

            def turn_x(b):
                pe.wait_ge(x_quant.sem, x_quant.at(0, b))
                for k in range(KT):
                    if k == 3:
                        pe.wait_ge(xq_lo_made.sem, xq_lo_made.at(0, b))
                    elif k == 0 and y_added.given(-1, b):
                        pe.wait_ge(y_added.sem, y_added.at(-1, b))
                    for t in range(TT):
                        ins = pe.transpose(p_x[k][:, t * P:(t + 1) * P], xn[:, t, k * P:(k + 1) * P],
                                           K.ident[:, :])
                    ins.then_inc(x_turned.sem, 1)

            def product(b, tiles):
                if tiles[0] == 0:
                    pe.wait_ge(xq_lo_made.sem, xq_lo_made.at(KT - 1, b))
                    pe.wait_ge(cq_lo_made.sem, cq_lo_made.at(0, b))
                for t in tiles:
                    rows = slice(t * P, (t + 1) * P)
                    if t == 3:
                        pe.wait_ge(y_added.sem, y_added.at(0, b))
                    for k in range(KT):
                        ins = three_pass(pe, p_x[t][:, :], xq_hi[:, k, rows], xq_lo[:, k, rows],
                                         cq_hi[:, k, :], cq_lo[:, k, :], k == 0, k == KT - 1)
                    ins.then_inc(y_made.sem, 1)

            pe.sem_inc(y_made.sem, y_made.opening)
            pe.wait_ge(ident_made.sem, ident_made.at(1))
            keys_and_values(0)
            turn_keys(0, TT - 1)
            with pe.Fori(1, B) as b:
                turn_x(b - 1)
                keys_and_values(b)
                product(b - 1, [0])
                turn_keys(b, TT - 1)
                product(b - 1, [1, 2, 3])
            turn_x(B - 1)
            product(B - 1, list(range(TT)))


class Norm:

    def __init__(self, K, sb, tag, banks, first_banks=()):
        self.K, self.banks = K, banks
        self.first_banks = first_banks
        self.xn = sb(f"{tag}_xn", [P, TT, D])
        self.stats = sb(f"{tag}_stats", [P, TT, 6])
        self.mv = sb(f"{tag}_mv", [P, TT, 2])
        self.veps = sb(f"{tag}_veps", [P, TT])
        self.rstd = sb(f"{tag}_rstd", [P, TT])
        self.var = Signal(K, f"{tag}_variance")
        self.rstd_made = Signal(K, f"{tag}_rstd")
        self.normed = Signal(K, f"{tag}_normalised", credit=1)
        self.turned = Signal(K, f"{tag}_transposed", per=KT, credit=KT)
        self.hi_made = Signal(K, f"{tag}_hi", per=KT)
        self.lo_made = Signal(K, f"{tag}_lo", per=KT, credit=KT)
        self.steps = Signal(K, f"{tag}_vector_steps")
        self.p_steps = Signal(K, f"{tag}_pool_steps")

    def bank(self, n, k):
        return self.first_banks[k] if self.first_banks and n == 0 else self.banks[k % len(self.banks)]

    def vector_stats(self, dve, n, b):
        x = self.K.x[:, bass.ds(b * TT, TT), :]
        dve.wait_ge(self.normed.sem, self.normed.at(-1, n))
        layer_norm_stats(dve, x, self.stats, self.mv, Count(self.steps, n), self.K.apart).then_inc(self.var.sem, 1)

    def pool_rstd(self, pool, n):
        pool.wait_ge(self.var.sem, self.var.at(0, n))
        pool.tensor_tensor(self.veps[:, :], self.mv[:, :, 1], self.K.ln_eps[:, :],
                           ALU.add).then_inc(self.p_steps.sem, 1)
        pool.wait_ge(self.p_steps.sem, self.p_steps.at(0, n))
        pool.tensor_tensor(self.rstd[:, :], self.veps[:, :], self.K.power[:, 0:TT],
                           ALU.pow).then_inc(self.rstd_made.sem, 1)

    def vector_scale(self, dve, n, b):
        x = self.K.x[:, bass.ds(b * TT, TT), :]
        dve.wait_ge(self.rstd_made.sem, self.rstd_made.at(0, n))
        dve.wait_ge(self.turned.sem, self.turned.at(-1, n))
        for t in range(TT):
            ins = dve.tensor_scalar(self.xn[:, t, :], x[:, t, :], self.mv[:, t, 0:1], self.rstd[:, t:t + 1],
                                    ALU.subtract, ALU.mult)
        ins.then_inc(self.normed.sem, 1)

    def tensor_turn(self, pe, n, k):
        if k == 0:
            pe.wait_ge(self.normed.sem, self.normed.at(0, n))
        if not (self.first_banks and n == 0):
            pe.wait_ge(self.lo_made.sem, self.lo_made.at(k - len(self.banks), n))
        for t in range(TT):
            ins = pe.transpose(self.bank(n, k)[:, t * P:(t + 1) * P], self.xn[:, t, k * P:(k + 1) * P],
                               self.K.ident[:, :])
        ins.then_inc(self.turned.sem, 1)

    def scalar_hi(self, act, n, b, k):
        act.wait_ge(self.turned.sem, self.turned.at(k, n))
        act.activation(self.K.xt_hi[:, k, bass.ds(b * S, S)], self.bank(n, k)[:, :],
                       ACT.Copy).then_inc(self.hi_made.sem, 1)

    def vector_lo(self, dve, n, b, k):
        cols = bass.ds(b * S, S)
        dve.wait_ge(self.hi_made.sem, self.hi_made.at(k, n))
        dve.tensor_tensor(self.K.xt_lo[:, k, cols], self.bank(n, k)[:, :], f32(self.K.xt_hi[:, k, cols]),
                          ALU.subtract).then_inc(self.lo_made.sem, 1)


def stage_ffn(K, w1_t, w2_t, b1_t, b2, wq):
    with ExitStack() as ctx:
        sb, ps = K.scope(ctx)
        CH = 4
        BEHIND_AT, AHEAD_AT = 2, 9
        w1q, w2q = sb("w1q", [P, KT, F], F32R), sb("w2q", [P, FT, D], F32R)
        least = sb("f_least", [P, F])
        sums = sb("f_sums", [P, 2, 2 * CH])
        total = sb("f_total", [P, 2])
        total_all = sb("f_total_all", [P, 2])
        thr, neg_thr = sb("f_thr", [P, 2]), sb("f_neg_thr", [P, 2])
        b1_c = sb("b1_c", [P, FT])
        b2_g = sb("b2_g", [P, D])
        act_out = sb("f_act", [P, 2, S])
        h_hi, h_lo = sb("h_hi", [P, 2, S], F32R), sb("h_lo", [P, 2, S], F32R)
        p_h = [ps(f"p_h{n}") for n in range(2)]
        p_y = [ps(f"f_y{t}") for t in range(TT)]
        norm = Norm(K, sb, "n", [ps(f"n_p{k}") for k in range(2)])

        bias_in = Signal(K, "f_bias_in", unit=16)
        w1_late_in = Signal(K, "f_late_weight_in", unit=16)
        w2_in = [Signal(K, f"f_weight2_in{n}", credit=1, unit=16) for n in range(2)]
        summed = Signal(K, "f_weights_summed", per=2 * CH)
        totals = Signal(K, "f_totals")
        total_made = Signal(K, "f_total_all_made")
        w1_made = Signal(K, "f_ternary1_made")
        w2_made = Signal(K, "f_ternary2_made")
        b2_made = Signal(K, "f_b2_scaled")
        b2_added = Signal(K, "f_b2_added", per=TT)
        h_made = Signal(K, "f_h_product", per=FT)
        gelu_made = Signal(K, "f_gelu", per=FT, credit=2)
        hi_made = Signal(K, "f_h_hi", per=FT, credit=2)
        lo_made = Signal(K, "f_h_lo", per=FT, credit=2)
        h_used = Signal(K, "f_h_used", per=FT, credit=2)
        y_added = Signal(K, "f_added", per=TT, credit=TT)
        steps = Signal(K, "f_vector_steps")
        block = ctx.enter_context(K.nc.Block())

        def ahead_of(b):
            return b * 2 - 1 if not isinstance(b, int) or b else 0

        def raw_chunk(w, c):
            if w == 0 and c < 2:
                return K.w_early[c][:, :, :].rearrange("p k n -> p (k n)")
            return f32((w1q, w2q)[w][:, :, :].rearrange("p k n -> p (k n)")[:, c * F:(c + 1) * F])

        w1_v = w1_t.rearrange("(k p) f -> p k f", p=P)
        w2_v = w2_t.rearrange("(k p) n -> p k n", p=P)

        @block.sync
        def _(sp):
            sp.dma_start(b1_c[:, :], b1_t).then_inc(bias_in.sem, 16)
            sp.dma_start(b2_g[:, :], b2.partition_broadcast(P)).then_inc(bias_in.sem, 16)
            with sp.Fori(0, 2) as i:
                cols = bass.ds(i * (F // 2), F // 2)
                sp.dma_start(f32(w1q[:, 2:KT, cols]), w1_v[:, 2:KT, cols]).then_inc(w1_late_in.sem, 16)
            for n in range(2):
                sp.sem_inc(w2_in[n].sem, w2_in[n].opening)
            with sp.Fori(0, CH // 2) as i:
                for n in range(2):
                    sp.wait_ge(w2_in[n].sem, w2_in[n].at(-1, i))
                    sp.sem_inc(K.apart, 1)
                    rows = bass.ds(i * (2 * CH) + n * CH, CH)
                    sp.dma_start(f32(w2q[:, rows, :]), w2_v[:, rows, :]).then_inc(w2_in[n].sem, 16)
            sp.wait_ge(w1_made.sem, w1_made.at(CH - 1))
            sp.dma_start(K.wq_raw[:, :, :], wq.rearrange("(k p) n -> p k n",
                                                         p=P)[:, :, 0:HG * DH]).then_inc(K.wq_in.sem, 16)

        @block.gpsimd
        def _(pool):
            norm.pool_rstd(pool, 0)
            for w in range(2):
                pool.wait_ge(totals.sem, totals.at(w))
                pool.partition_all_reduce(total_all[:, w:w + 1], total[:, w:w + 1], P,
                                          bass.bass_isa.ReduceOp.add).then_inc(total_made.sem, 1)
            pool.wait_ge(b2_made.sem, b2_made.at(0))

            def add_bias(b):
                pool.wait_ge(norm.normed.sem, norm.normed.at(0, ahead_of(b)))
                pool.sem_inc(K.apart, 1)
                for t in range(TT):
                    xt = K.x[:, bass.ds(b * TT + t, 1), :].rearrange("p a n -> p (a n)")
                    pool.tensor_tensor(xt, xt, b2_g[:, :], ALU.add).then_inc(b2_added.sem, 1)

            def mlp(b, behind, ahead):
                if behind:
                    norm.pool_rstd(pool, b * 2)
                if ahead:
                    norm.pool_rstd(pool, b * 2 + 1)
                    add_bias(b + 1)

            add_bias(0)
            mlp(0, False, True)
            with pool.Fori(1, B - 1) as b:
                mlp(b, True, True)
            mlp(B - 1, True, False)
            norm.pool_rstd(pool, 2 * B - 1)

        @block.vector
        def _(dve):
            dve.sem_inc(lo_made.sem, lo_made.opening)
            dve.sem_inc(y_added.sem, y_added.opening)
            dve.sem_inc(norm.normed.sem, norm.normed.opening)
            dve.sem_inc(norm.lo_made.sem, norm.lo_made.opening)
            norm.vector_stats(dve, 0, 0)
            norm.vector_scale(dve, 0, 0)
            for k in range(KT):
                norm.vector_lo(dve, 0, 0, k)
            step = Count(steps)
            dve.wait_ge(bias_in.sem, bias_in.at(1))
            dve.tensor_scalar(b2_g[:, :], b2_g[:, :], K.gates[:, 2:3], None, ALU.mult).then_inc(b2_made.sem, 1)
            def threshold(w):
                dve.wait_ge(summed.sem, summed.at(2 * CH - 1, w))
                dve.tensor_reduce(total[:, w:w + 1], sums[:, w, :], AX.X, ALU.add).then_inc(totals.sem, 1)
                dve.wait_ge(total_made.sem, total_made.at(w))
                dve.tensor_scalar(thr[:, w:w + 1], total_all[:, w:w + 1], 1.0 / (D * F), 0.7,
                                  ALU.mult, ALU.mult)
                dve.tensor_scalar(neg_thr[:, w:w + 1], total_all[:, w:w + 1], -1.0 / (D * F), 0.7,
                                  ALU.mult, ALU.mult).then_inc(step.sem, 1)
                dve.wait_ge(step.sem, step.next())

            def ternary1(c):
                cols = slice(c * F // CH, (c + 1) * F // CH)
                if c:
                    dve.wait_ge(w2_made.sem, w2_made.at(c - 1))
                for k in range(KT):
                    ins = dve.tensor_scalar(least[:, k * F // CH:(k + 1) * F // CH], raw_chunk(0, k)[:, cols],
                                            neg_thr[:, 0:1], None, ALU.is_le)
                ins.then_inc(step.sem, 1)
                dve.wait_ge(step.sem, step.next())
                for k in range(KT):
                    ins = dve.scalar_tensor_tensor(w1q[:, k, cols], raw_chunk(0, k)[:, cols], thr[:, 0:1],
                                                   least[:, k * F // CH:(k + 1) * F // CH], ALU.is_ge,
                                                   ALU.subtract)
                ins.then_inc(w1_made.sem, 1)

            def ternary2(c):
                dve.wait_ge(w1_made.sem, w1_made.at(c))
                dve.tensor_scalar(least[:, :], raw_chunk(1, c), neg_thr[:, 1:2], None,
                                  ALU.is_le).then_inc(step.sem, 1)
                dve.wait_ge(step.sem, step.next())
                dve.scalar_tensor_tensor(w2q[:, :, :].rearrange("p k n -> p (k n)")[:, c * F:(c + 1) * F],
                                         raw_chunk(1, c), thr[:, 1:2], least[:, :], ALU.is_ge,
                                         ALU.subtract).then_inc(w2_made.sem, 1)

            threshold(0)
            ternary1(0)
            threshold(1)
            ternary2(0)

            def mlp(b, behind, ahead):
                norms = [(BEHIND_AT, b * 2, b - 1)] * behind + [(AHEAD_AT, b * 2 + 1, b + 1)] * ahead
                for f in range(FT):
                    dve.wait_ge(hi_made.sem, hi_made.at(f, b))
                    dve.wait_ge(h_used.sem, h_used.at(f - 2, b))
                    dve.tensor_tensor(h_lo[:, f % 2, :], act_out[:, f % 2, :], f32(h_hi[:, f % 2, :]),
                                      ALU.subtract).then_inc(lo_made.sem, 1)
                    if not behind and f in (1, 4, 6):
                        ternary1((1, 4, 6).index(f) + 1)
                    if not behind and f in (2, 5, 7):
                        ternary2((2, 5, 7).index(f) + 1)
                    for at, n, batch in norms:
                        if f == at:
                            if at == BEHIND_AT:
                                dve.wait_ge(y_added.sem, y_added.at(-1, b))
                            norm.vector_stats(dve, n, batch)
                        if f == at + 1:
                            norm.vector_scale(dve, n, batch)
                        if at + 2 <= f < at + 2 + KT:
                            norm.vector_lo(dve, n, batch, f - at - 2)
                dve.wait_ge(h_used.sem, h_used.at(FT - 1, b))
                dve.wait_ge(b2_added.sem, b2_added.at(TT - 1, b))
                for t in range(TT):
                    xt = K.x[:, bass.ds(b * TT + t, 1), :].rearrange("p a n -> p (a n)")
                    dve.scalar_tensor_tensor(xt, p_y[t][:, :], K.gates[:, 2:3], xt, ALU.mult,
                                             ALU.add).then_inc(y_added.sem, 1)

            mlp(0, False, True)
            with dve.Fori(1, B - 1) as b:
                mlp(b, True, True)
            mlp(B - 1, True, False)
            dve.wait_ge(y_added.sem, y_added.at(TT - 1, B - 1))
            norm.vector_stats(dve, 2 * B - 1, B - 1)
            norm.vector_scale(dve, 2 * B - 1, B - 1)
            for k in range(KT):
                norm.vector_lo(dve, 2 * B - 1, B - 1, k)

        @block.scalar
        def _(act):
            act.sem_inc(gelu_made.sem, gelu_made.opening)
            act.sem_inc(hi_made.sem, hi_made.opening)

            def add_up(w, c):
                if w == 1:
                    act.wait_ge(w2_in[c % 2].sem, w2_in[c % 2].at(0, c // 2))
                elif c < 2:
                    act.wait_ge(K.w1_in[c].sem, K.w1_in[c].at(0))
                else:
                    act.wait_ge(w1_late_in.sem, w1_late_in.at(1))
                for n in range(2 * c, 2 * c + 2):
                    if w + n:
                        act.wait_ge(summed.sem, summed.at(n - 1, w))
                    act.activation(act_out[:, :, :].rearrange("p a n -> p (a n)"),
                                   raw_chunk(w, c)[:, n % 2 * 2 * S:(n % 2 + 1) * 2 * S], ACT.Abs,
                                   accum_out=sums[:, w, n:n + 1]).then_inc(summed.sem, 1)

            add_up(0, 0)
            add_up(0, 1)
            for k in range(KT):
                norm.scalar_hi(act, 0, 0, k)
            add_up(0, 2)
            add_up(0, 3)
            for c in range(CH):
                add_up(1, c)
            act.wait_ge(summed.sem, summed.at(2 * CH - 1, 1))
            act.wait_ge(bias_in.sem, bias_in.at(1))

            def mlp(b, behind, ahead):
                norms = [(BEHIND_AT, b * 2, b - 1)] * behind + [(AHEAD_AT, b * 2 + 1, b + 1)] * ahead
                for f in range(FT):
                    act.wait_ge(h_made.sem, h_made.at(f, b))
                    act.wait_ge(lo_made.sem, lo_made.at(f - 2, b))
                    act.activation(act_out[:, f % 2, :], p_h[f % 2][:, :], ACT.Gelu,
                                   bias=b1_c[:, f:f + 1]).then_inc(gelu_made.sem, 1)
                    act.wait_ge(gelu_made.sem, gelu_made.at(f, b))
                    act.wait_ge(h_used.sem, h_used.at(f - 2, b))
                    act.activation(h_hi[:, f % 2, :], act_out[:, f % 2, :], ACT.Copy).then_inc(hi_made.sem, 1)
                    for at, n, batch in norms:
                        if at + 2 <= f < at + 2 + KT:
                            norm.scalar_hi(act, n, batch, f - at - 2)

            mlp(0, False, True)
            with act.Fori(1, B - 1) as b:
                mlp(b, True, True)
            mlp(B - 1, True, False)
            for k in range(KT):
                norm.scalar_hi(act, 2 * B - 1, B - 1, k)

        @block.tensor
        def _(pe):
            pe.sem_inc(h_used.sem, h_used.opening)
            pe.sem_inc(norm.turned.sem, norm.turned.opening)
            for k in range(KT):
                norm.tensor_turn(pe, 0, k)

            def hidden(b, f, first):
                if first and f % CH == 0:
                    pe.wait_ge(w1_made.sem, w1_made.at(f // CH))
                if f == 0:
                    pe.wait_ge(norm.lo_made.sem, norm.lo_made.at(KT - 1, ahead_of(b)))
                pe.wait_ge(gelu_made.sem, gelu_made.at(f - 2, b))
                for k in range(KT):
                    w = w1q[:, k, f * P:(f + 1) * P]
                    cols = bass.ds(b * S, S)
                    pe.matmul(p_h[f % 2][:, :], w, K.xt_hi[:, k, cols], start=k == 0, stop=False)
                    ins = pe.matmul(p_h[f % 2][:, :], w, K.xt_lo[:, k, cols], start=False, stop=k == KT - 1)
                ins.then_inc(h_made.sem, 1)

            def output(b, f, first):
                pe.wait_ge(lo_made.sem, lo_made.at(f, b))
                if first and f % CH == 0:
                    pe.wait_ge(w2_made.sem, w2_made.at(f // CH))
                for t in range(TT):
                    rows = slice(t * P, (t + 1) * P)
                    if f == 0:
                        pe.wait_ge(y_added.sem, y_added.at(t - TT, b))
                    pe.matmul(p_y[t][:, :], h_hi[:, f % 2, rows], w2q[:, f, :], start=f == 0, stop=False)
                    ins = pe.matmul(p_y[t][:, :], h_lo[:, f % 2, rows], w2q[:, f, :], start=False,
                                    stop=f == FT - 1)
                ins.then_inc(h_used.sem, 1)

            def mlp(b, behind, ahead):
                norms = [(BEHIND_AT, b * 2)] * behind + [(AHEAD_AT, b * 2 + 1)] * ahead
                for f in range(FT):
                    hidden(b, f, not behind)
                    if f >= 1:
                        output(b, f - 1, not behind)
                    for at, n in norms:
                        if at + 2 <= f < at + 2 + KT:
                            norm.tensor_turn(pe, n, f - at - 2)
                output(b, FT - 1, not behind)

            mlp(0, False, True)
            with pe.Fori(1, B - 1) as b:
                mlp(b, True, True)
            mlp(B - 1, True, False)
            for k in range(KT):
                norm.tensor_turn(pe, 2 * B - 1, k)


def stage_attention(K, wq, wo, q_norm_w, keys, values):
    with ExitStack() as ctx:
        sb, ps = K.scope(ctx)
        U = HG * TT
        HALF = S // 2
        ITS = G * B
        HP = HG // 2
        LAST_STEP = U + 11
        NP = 2 * TT
        FIRST_COLS = (slice(0, DH), slice(DH, HG * DH))
        w_raw = K.wq_raw
        wq_hi, wq_lo = sb("wq_hi", [P, KT, HG * DH], F32R), sb("wq_lo", [P, KT, HG * DH], F32R)
        wo_hi, wo_lo = sb("wo_hi", [P, HG, D], F32R), sb("wo_lo", [P, HG, D], F32R)
        k_in = sb("k_in", [P, 2, 2, S], F32R)
        v_in = sb("v_in", [P, TT, 2, DH], F32R)
        q_hi, q_lo = sb("q_hi", [P, 2, S], F32R), sb("q_lo", [P, 2, S], F32R)
        q_sq = sb("q_sq", [P, S])
        q_ms = sb("q_ms", [P, 2, TT])
        q_rs = sb("q_rs", [P, 2, TT])
        neg_max = sb("neg_max", [P, U])
        bias = sb("a_bias", [P, U])
        total = sb("a_total", [P, U])
        inv = sb("a_inv", [P, U])
        prob = sb("prob", [P, 4, S])
        pt_hi, pt_lo = sb("pt_hi", [P, 2, TT, HALF], F32R), sb("pt_lo", [P, 2, TT, HALF], F32R)
        o_hi, o_lo = sb("o_hi", [P, HG, S], F32R), sb("o_lo", [P, HG, S], F32R)
        ones = sb("a_ones", [P, 1])
        qw = sb("qw", [P, 1])
        p_s = [ps(f"p_s{n}") for n in range(4)]
        p_t = [ps(f"p_t{n}") for n in range(2)]
        p_q = ps("p_q")
        p_o = ps("p_o")

        qw_in = Signal(K, "a_query_norm_in", unit=16)
        w_in = K.wq_in
        wq_hi0 = Signal(K, "a_first_wq_hi")
        wq_lo0 = Signal(K, "a_first_wq_lo")
        w_steps = Signal(K, "a_weights_hi", per=2 * HG)
        wq_made = Signal(K, "a_wq_split", per=HG)
        wo_made = Signal(K, "a_wo_split", per=HG)
        keys_in = Signal(K, "a_keys_in", unit=16)
        values_in = [Signal(K, f"a_values_in{n}", unit=16) for n in range(2)]
        ones_made = Signal(K, "a_ones_made")
        q_made = Signal(K, "a_q_product", per=HG)
        q_squared = Signal(K, "a_q_squared", per=HG)
        q_hi_made = Signal(K, "a_q_hi", per=HG)
        q_lo_made = Signal(K, "a_q_lo", per=HG)
        ms_made = Signal(K, "a_q_square_sums", per=HG)
        ms_read = Signal(K, "a_q_square_sums_read", per=HG)
        rs_made = Signal(K, "a_q_scale", per=HG)
        s_made = Signal(K, "a_scores", per=U)
        max_made = Signal(K, "a_max", per=U)
        bias_made = Signal(K, "a_bias_made", per=U)
        exp_made = Signal(K, "a_exp", per=U)
        inv_made = Signal(K, "a_inverse", per=U)
        p_made = Signal(K, "a_probabilities", per=U)
        t_made = Signal(K, "a_transposed", per=U)
        pt_hi_made = Signal(K, "a_pt_hi", per=U)
        pt_lo_made = Signal(K, "a_pt_lo", per=U)
        o_made = Signal(K, "a_heads_out", per=U)
        o_hi_made = Signal(K, "a_o_hi", per=HG)
        o_lo_made = Signal(K, "a_o_lo", per=HG)
        y_made = Signal(K, "a_product", per=NP, credit=NP)
        y_added = Signal(K, "a_added", per=NP)
        block = ctx.enter_context(K.nc.Block())
        wq_v = wq.rearrange("(k p) n -> p k n", p=P)
        wo_v = wo.rearrange("(h p) n -> p h n", p=P)

        def home(it, n, per):
            if isinstance(it, int) and not 0 <= it * per + n < ITS * per:
                return None
            return it + n // per if n // per else it, n % per

        def query_head(it, u):
            return home(it, (u + 5) // TT, HG)

        def projected(it, u):
            return home(it, (u - 13) // TT * 2 + u % TT - 1, NP)

        @block.sync
        def _(sp):
            def load_wq(g):
                sp.dma_start(w_raw[:, :, :], wq_v[:, :, bass.ds(g * (HG * DH), HG * DH)]).then_inc(w_in.sem, 16)

            def load_wo(g):
                sp.dma_start(w_raw[:, :, :], wo_v[:, bass.ds(g * HG, HG), :]).then_inc(w_in.sem, 16)

            def load_keys(it):
                if s_made.given(-U - 1, it):
                    sp.wait_ge(s_made.sem, s_made.at(-U - 1, it))
                    sp.sem_inc(K.apart, 1)
                if keys_in.given(-1, it):
                    sp.wait_ge(keys_in.sem, keys_in.at(-1, it))
                    sp.sem_inc(K.apart, 1)
                sp.dma_start(
                    f32(k_in[:, bass.ds(it % 2, 1), :, :]).rearrange("p s h n -> p (s h) n"),
                    keys[bass.ds(it % B, 1), :, :, bass.ds(it // B, 1), :].rearrange("a p h c n -> p (a h c) n")
                ).then_inc(keys_in.sem, 16)

            def load_values(it):
                for n in range(2):
                    tiles = slice(n * TT // 2, (n + 1) * TT // 2)
                    if o_made.given(n - 2, it):
                        sp.wait_ge(o_made.sem, o_made.at(n - 2, it))
                        sp.sem_inc(K.apart, 1)
                    sp.dma_start(
                        f32(v_in[:, tiles, :, :]),
                        values[bass.ds(it % B, 1), :, tiles, :, bass.ds(it // B * DH, DH)].rearrange(
                            "a p t h n -> p (a t) h n")).then_inc(values_in[n].sem, 16)

            def loads(it):
                load_values(it)
                load_keys(it + 1)

            sp.dma_start(qw[:, :], q_norm_w.rearrange("(p a) -> p a", a=1)).then_inc(qw_in.sem, 16)
            load_keys(0)
            load_values(0)
            load_keys(1)
            sp.wait_ge(wq_lo0.sem, wq_lo0.at(1))
            load_wo(0)
            with sp.Fori(0, G - 1) as g:
                loads(g * B + 1)
                sp.wait_ge(wo_made.sem, wo_made.at(HG - 1, g))
                sp.sem_inc(K.apart, 1)
                load_wq(g + 1)
                loads(g * B + 2)
                loads(g * B + 3)
                sp.wait_ge(wq_made.sem, wq_made.at(HG - 1, g + 1))
                sp.sem_inc(K.apart, 1)
                load_wo(g + 1)
                loads(g * B + 4)
            loads(ITS - 3)
            loads(ITS - 2)
            load_values(ITS - 1)

        @block.gpsimd
        def _(pool):
            pool.memset(ones[:, :], 1.0).then_inc(ones_made.sem, 1)
            pool.sem_inc(wq_made.sem, HG)
            def query_scale(it, j):
                pool.wait_ge(ms_read.sem, ms_read.at(j, it))
                pool.tensor_tensor(q_rs[:, j % 2, :], q_ms[:, j % 2, :], K.power[:, 0:TT],
                                   ALU.pow).then_inc(rs_made.sem, 1)

            def split_wo(g, h):
                if h == 0:
                    pool.wait_ge(w_in.sem, w_in.at(1, g))
                pool.wait_ge(y_made.sem, y_made.at((h // HP + 1) * TT - 1 - NP, g * B))
                pool.sem_inc(K.apart, 1)
                pool.tensor_copy(wo_hi[:, h, :], w_raw[:, h, :]).then_inc(w_steps.sem, 1)
                pool.wait_ge(w_steps.sem, w_steps.at(h, g))
                pool.tensor_tensor(wo_lo[:, h, :], w_raw[:, h, :], f32(wo_hi[:, h, :]),
                                   ALU.subtract).then_inc(wo_made.sem, 1)

            def split_wq(g, h):
                cols = slice(h * DH, (h + 1) * DH)
                if h == 0:
                    pool.wait_ge(w_in.sem, w_in.at(0, g + 1))
                pool.wait_ge(q_made.sem, q_made.at(h, g * B + B - 1))
                pool.sem_inc(K.apart, 1)
                pool.tensor_copy(wq_hi[:, :, cols], w_raw[:, :, cols]).then_inc(w_steps.sem, 1)
                pool.wait_ge(w_steps.sem, w_steps.at(HG + h, g))
                pool.tensor_tensor(wq_lo[:, :, cols], w_raw[:, :, cols], f32(wq_hi[:, :, cols]),
                                   ALU.subtract).then_inc(wq_made.sem, 1)

            query_scale(0, 0)
            with pool.Fori(0, G - 1) as g:
                for h in range(HG):
                    query_scale(g * B, h + 1)
                    split_wo(g, h)
                with pool.Fori(1, B - 1) as b:
                    for h in range(HG):
                        query_scale(g * B + b, h + 1)
                for h in range(HG):
                    query_scale(g * B + (B - 1), h + 1)
                    split_wq(g, h)
            for h in range(HG):
                query_scale(ITS - B, h + 1)
                split_wo(G - 1, h)
            with pool.Fori(ITS - B + 1, ITS - 1) as it:
                for h in range(HG):
                    query_scale(it, h + 1)
            for h in range(HG - 1):
                query_scale(ITS - 1, h + 1)

        @block.scalar
        def _(act):
            act.wait_ge(w_in.sem, w_in.at(0))
            for cols in FIRST_COLS:
                act.activation(wq_hi[:, :, cols], w_raw[:, :, cols], ACT.Copy).then_inc(wq_hi0.sem, 1)
            act.wait_ge(qw_in.sem, qw_in.at(0))

            def split_query(it, h):
                act.wait_ge(q_made.sem, q_made.at(h, it))
                if s_made.given((h - 1) * TT - 1, it):
                    act.wait_ge(s_made.sem, s_made.at((h - 1) * TT - 1, it))
                act.activation(q_hi[:, h % 2, :], p_q[:, :], ACT.Copy, scale=qw[:, 0:1]).then_inc(q_hi_made.sem, 1)
                if ms_made.given(h - 1, it):
                    act.wait_ge(ms_made.sem, ms_made.at(h - 1, it))
                act.activation(q_sq[:, :], p_q[:, :], ACT.Square).then_inc(q_squared.sem, 1)

            def exp(it, u):
                act.wait_ge(bias_made.sem, bias_made.at(u, it))
                if t_made.given(u - 4, it):
                    act.wait_ge(t_made.sem, t_made.at(u - 4, it))
                act.activation(prob[:, u % 4, :], p_s[u % 4][:, :], ACT.Exp, bias=bias[:, u:u + 1],
                               scale=q_rs[:, u // TT % 2, u % TT:u % TT + 1],
                               accum_out=total[:, u:u + 1]).then_inc(exp_made.sem, 1)

            def transposed_hi(it, u):
                act.wait_ge(t_made.sem, t_made.at(u, it))
                if u % 2 == 0 and o_made.given(u - 3, it):
                    act.wait_ge(o_made.sem, o_made.at(u - 3, it))
                act.activation(pt_hi[:, u // 2 % 2, :, (u % 2) * P:(u % 2 + 1) * P],
                               p_t[u % 2][:, :].rearrange("p (t n) -> p t n", t=TT),
                               ACT.Copy).then_inc(pt_hi_made.sem, 1)

            def head_out(it, h):
                act.wait_ge(o_made.sem, o_made.at(4 * h + 3, it))
                act.wait_ge(y_made.sem, y_made.at((h // HP + 1) * TT - 1 - NP, it))
                act.activation(o_hi[:, h, :], p_o[:, :], ACT.Copy).then_inc(o_hi_made.sem, 1)

            def step(it, u):
                if u % TT == 2 and (at := home(it, (u - 6) // TT, HG)):
                    head_out(*at)
                if u % TT == 0 and (at := query_head(it, u - 1)):
                    split_query(*at)
                if at := home(it, u, U):
                    transposed_hi(*at)
                if at := home(it, u + 2, U):
                    exp(*at)

            for u in range(-5, U):
                step(0, u)
            with act.Fori(1, ITS - 1) as it:
                for u in range(U):
                    step(it, u)
            for u in range(LAST_STEP + 1):
                step(ITS - 1, u)

        @block.vector
        def _(dve):
            for n, cols in enumerate(FIRST_COLS):
                dve.wait_ge(wq_hi0.sem, wq_hi0.at(n))
                dve.tensor_tensor(wq_lo[:, :, cols], w_raw[:, :, cols], f32(wq_hi[:, :, cols]),
                                  ALU.subtract).then_inc(wq_lo0.sem, 1)
            dve.wait_ge(qw_in.sem, qw_in.at(0))

            def split_query(it, h):
                dve.wait_ge(q_hi_made.sem, q_hi_made.at(h, it))
                dve.wait_ge(q_squared.sem, q_squared.at(h, it))
                dve.scalar_tensor_tensor(q_lo[:, h % 2, :], p_q[:, :], qw[:, 0:1], f32(q_hi[:, h % 2, :]),
                                         ALU.mult, ALU.subtract).then_inc(q_lo_made.sem, 1)

            def read_sums(it, h):
                dve.wait_ge(ms_made.sem, ms_made.at(h, it))
                dve.tensor_scalar(q_ms[:, h % 2, :], p_q[:, 0:TT], DH * RMS_EPS, None,
                                  ALU.add).then_inc(ms_read.sem, 1)

            def maximum(it, u):
                dve.wait_ge(s_made.sem, s_made.at(u, it))
                dve.tensor_reduce(neg_max[:, u:u + 1], p_s[u % 4][:, :], AX.X, ALU.max,
                                  negate=True).then_inc(max_made.sem, 1)

            def shift(it, u):
                dve.wait_ge(max_made.sem, max_made.at(u, it))
                if u % TT == 0:
                    dve.wait_ge(rs_made.sem, rs_made.at(u // TT, it))
                dve.tensor_tensor(bias[:, u:u + 1], neg_max[:, u:u + 1],
                                  q_rs[:, u // TT % 2, u % TT:u % TT + 1], ALU.mult).then_inc(bias_made.sem, 1)

            def invert(it, u):
                dve.wait_ge(exp_made.sem, exp_made.at(u, it))
                dve.reciprocal(inv[:, u:u + 1], total[:, u:u + 1]).then_inc(inv_made.sem, 1)

            def normalise(it, u):
                dve.wait_ge(inv_made.sem, inv_made.at(u, it))
                dve.tensor_scalar(prob[:, u % 4, :], prob[:, u % 4, :], inv[:, u:u + 1], None,
                                  ALU.mult).then_inc(p_made.sem, 1)

            def transposed_lo(it, u):
                dve.wait_ge(pt_hi_made.sem, pt_hi_made.at(u, it))
                dve.tensor_tensor(pt_lo[:, u // 2 % 2, :, (u % 2) * P:(u % 2 + 1) * P],
                                  p_t[u % 2][:, :].rearrange("p (t n) -> p t n", t=TT),
                                  f32(pt_hi[:, u // 2 % 2, :, (u % 2) * P:(u % 2 + 1) * P]),
                                  ALU.subtract).then_inc(pt_lo_made.sem, 1)

            def head_out(it, h):
                dve.wait_ge(o_hi_made.sem, o_hi_made.at(h, it))
                dve.tensor_tensor(o_lo[:, h, :], p_o[:, :], f32(o_hi[:, h, :]),
                                  ALU.subtract).then_inc(o_lo_made.sem, 1)

            def add(it, n):
                dve.wait_ge(y_made.sem, y_made.at(n, it))
                xt = K.x[:, bass.ds(it % B * TT + n % TT, 1), :].rearrange("p a n -> p (a n)")
                dve.scalar_tensor_tensor(xt, p_q[:, :], K.gates[:, 1:2], xt, ALU.mult,
                                         ALU.add).then_inc(y_added.sem, 1)

            def step(it, u):
                if at := home(it, u + 2, U):
                    maximum(*at)
                if at := home(it, u + 1, U):
                    invert(*at)
                if at := home(it, u + 2, U):
                    shift(*at)
                if u % TT in (2, 3) and (at := projected(it, u - 1)):
                    add(*at)
                if u % TT == 1 and (at := query_head(it, u - 2)):
                    read_sums(*at)
                if at := home(it, u + 1, U):
                    normalise(*at)
                if u % TT == 0 and (at := query_head(it, u - 1)):
                    split_query(*at)
                if u % TT == 2 and (at := home(it, (u - 6) // TT, HG)):
                    head_out(*at)
                if at := home(it, u, U):
                    transposed_lo(*at)

            for u in range(-5, U):
                step(0, u)
            with dve.Fori(1, ITS - 1) as it:
                for u in range(U):
                    step(it, u)
            for u in range(LAST_STEP + 1):
                step(ITS - 1, u)

        @block.tensor
        def _(pe):
            pe.sem_inc(y_made.sem, y_made.opening)
            pe.wait_ge(ones_made.sem, ones_made.at(0))

            def query(it, h):
                if isinstance(it, int) and it == 0 and h < 2:
                    pe.wait_ge(wq_lo0.sem, wq_lo0.at(h))
                pe.wait_ge(wq_made.sem, wq_made.at(h, it // B))
                if ms_read.given(h - 1, it):
                    pe.wait_ge(ms_read.sem, ms_read.at(h - 1, it))
                if y_added.given(2 * h - NP - 1, it):
                    pe.wait_ge(y_added.sem, y_added.at(2 * h - NP - 1, it))
                heads = slice(h * DH, (h + 1) * DH)
                cols = bass.ds(it % B * S, S)
                for k in range(KT):
                    ins = three_pass(pe, p_q[:, :], wq_hi[:, k, heads], wq_lo[:, k, heads],
                                     K.xt_hi[:, k, cols], K.xt_lo[:, k, cols], k == 0, k == KT - 1)
                ins.then_inc(q_made.sem, 1)

            def square_sums(it, h):
                pe.wait_ge(q_squared.sem, q_squared.at(h, it))
                pe.wait_ge(q_lo_made.sem, q_lo_made.at(h, it))
                for t in range(TT):
                    ins = pe.matmul(p_q[:, t:t + 1], q_sq[:, t * P:(t + 1) * P], ones[:, :],
                                    start=True, stop=True)
                ins.then_inc(ms_made.sem, 1)

            def scores(it, u):
                h, qt = divmod(u, TT)
                if u == 0:
                    pe.wait_ge(keys_in.sem, keys_in.at(0, it))
                if exp_made.given(u - 4, it):
                    pe.wait_ge(exp_made.sem, exp_made.at(u - 4, it))
                if qt == 0:
                    pe.wait_ge(q_lo_made.sem, q_lo_made.at(h, it))
                rows = slice(qt * P, (qt + 1) * P)
                slot = bass.ds(it % 2, 1)
                k_hi = k_in[:, slot, 0, :].rearrange("p s n -> p (s n)")
                k_lo = k_in[:, slot, 1, :].rearrange("p s n -> p (s n)")
                three_pass(pe, p_s[u % 4][:, :], q_hi[:, h % 2, rows], q_lo[:, h % 2, rows],
                           k_hi, k_lo, True, True).then_inc(s_made.sem, 1)

            def turn(it, u):
                pe.wait_ge(p_made.sem, p_made.at(u, it))
                if pt_lo_made.given(u - 2, it):
                    pe.wait_ge(pt_lo_made.sem, pt_lo_made.at(u - 2, it))
                for t in range(TT):
                    ins = pe.transpose(p_t[u % 2][:, t * P:(t + 1) * P], prob[:, u % 4, t * P:(t + 1) * P],
                                       K.ident[:, :])
                ins.then_inc(t_made.sem, 1)

            def weigh_values(it, n):
                m = n // 2
                pe.wait_ge(pt_lo_made.sem, pt_lo_made.at(2 * m + 1, it))
                if m == 0:
                    pe.wait_ge(values_in[n].sem, values_in[n].at(0, it))
                if n % 4 == 0 and o_lo_made.given(n // 4 - 1, it):
                    pe.wait_ge(o_lo_made.sem, o_lo_made.at(n // 4 - 1, it))
                for t in range(n % 2 * TT // 2, (n % 2 + 1) * TT // 2):
                    ins = three_pass(pe, p_o[:, (m % 2) * HALF:(m % 2 + 1) * HALF], v_in[:, t, 0, :],
                                     v_in[:, t, 1, :], pt_hi[:, m % 2, t, :], pt_lo[:, m % 2, t, :],
                                     t == 0, t == TT - 1)
                ins.then_inc(o_made.sem, 1)

            def project(it, n):
                pair, t = divmod(n, TT)
                if t == 0:
                    pe.wait_ge(wo_made.sem, wo_made.at(pair * HP + HP - 1, it // B))
                    pe.wait_ge(o_lo_made.sem, o_lo_made.at(pair * HP + HP - 1, it))
                if y_added.given(n - 1, it):
                    pe.wait_ge(y_added.sem, y_added.at(n - 1, it))
                rows = slice(t * P, (t + 1) * P)
                for h in range(pair * HP, (pair + 1) * HP):
                    ins = three_pass(pe, p_q[:, :], o_hi[:, h, rows], o_lo[:, h, rows], wo_hi[:, h, :],
                                     wo_lo[:, h, :], h % HP == 0, h % HP == HP - 1)
                ins.then_inc(y_made.sem, 1)

            def step(it, u):
                if u % 2 == 0 and (at := home(it, u - 3, U)):
                    weigh_values(*at)
                if at := home(it, u, U):
                    turn(*at)
                if u % 2 == 1 and (at := home(it, u - 3, U)):
                    weigh_values(*at)
                if u % TT == 1 and (at := query_head(it, u - 2)):
                    square_sums(*at)
                if at := home(it, u + 3, U):
                    scores(*at)
                if u % TT in (1, 2) and (at := projected(it, u)):
                    if u % TT == 1 and (head := query_head(it, u - 2)):
                        pe.wait_ge(ms_read.sem, ms_read.at(head[1], head[0]))
                    project(*at)
                if u % TT == 3 and (at := query_head(it, u)):
                    query(*at)

            for u in range(-5, U):
                step(0, u)
            with pe.Fori(1, ITS - 1) as it:
                for u in range(U):
                    step(it, u)
            for u in range(LAST_STEP + 1):
                step(ITS - 1, u)


class Router:

    def __init__(self, K, sb, bank):
        self.K, self.bank = K, bank
        self.g_raw, self.g_full = sb("g_raw", [P, KT, E]), sb("g_full", [P, KT, E])
        self.a_raw, self.b_raw = sb("ga_raw", [R, D]), sb("gb_raw", [R, E])
        self.g_hi, self.g_lo = sb("g_hi", [P, KT, P], F32R), sb("g_lo", [P, KT, P], F32R)
        self.flat = sb("r_logits_t", [E, S])
        self.logit = sb("r_logits", [P, TT, E])
        self.prob = sb("r_prob", [P, TT, E])
        self.most, self.total, self.inv = sb("r_max", [P, TT]), sb("r_total", [P, TT]), sb("r_inv", [P, TT])
        self.top = sb("r_top", [P, TT, 8])
        self.index = sb("r_index", [P, TT, 8], U32)
        self.place = sb("r_place", [P, TT, 2])
        self.number_i, self.number = sb("r_number_i", [P, E], mybir.dt.int32), sb("r_number", [P, E])
        self.mask, self.other = sb("r_mask", [P, TT, E]), sb("r_other", [P, TT, E])
        self.loaded = Signal(K, "r_loaded", unit=16)
        self.zeroed = Signal(K, "r_zeroed")
        self.numbered = Signal(K, "r_numbered")
        self.delta_made = Signal(K, "r_delta")
        self.gate_made = Signal(K, "r_gate_split")
        self.logits_made = Signal(K, "r_logits_made")
        self.logits_read = Signal(K, "r_logits_read")
        self.turned = Signal(K, "r_transposed")
        self.turned_read = Signal(K, "r_transposed_read")
        self.shifted = Signal(K, "r_shifted")
        self.exp_made = Signal(K, "r_exp")
        self.steps = Signal(K, "r_vector_steps", per=14)
        self.gate_steps = Signal(K, "r_gate_steps")

    def sync_loads(self, sp, gate_t, lora_a, lora_b_t):
        sp.dma_start(self.g_raw[:, :, :], gate_t.rearrange("(k p) e -> p k e", p=P)).then_inc(self.loaded.sem, 16)
        sp.dma_start(self.a_raw[:, :], lora_a).then_inc(self.loaded.sem, 16)
        sp.dma_start(self.b_raw[:, :], lora_b_t).then_inc(self.loaded.sem, 16)

    def pool_constants(self, pool):
        pool.memset(f32(self.g_hi[:, :, :]), 0.0).then_inc(self.zeroed.sem, 1)
        pool.memset(f32(self.g_lo[:, :, :]), 0.0).then_inc(self.zeroed.sem, 1)
        pool.iota(self.number_i[:, :], pattern=[[1, E]], base=0,
                  channel_multiplier=0).then_inc(self.numbered.sem, 1)

    def tensor_gate(self, pe):
        pe.wait_ge(self.loaded.sem, self.loaded.at(2))
        for k in range(KT):
            ins = pe.matmul(self.bank[:, k * E:(k + 1) * E], self.a_raw[:, k * P:(k + 1) * P], self.b_raw[:, :],
                            start=True, stop=True)
        ins.then_inc(self.delta_made.sem, 1)

    def vector_gate(self, dve):
        dve.wait_ge(self.loaded.sem, self.loaded.at(2))
        dve.wait_ge(self.delta_made.sem, self.delta_made.at(0))
        dve.scalar_tensor_tensor(self.g_full[:, :, :],
                                 self.bank[:, 0:KT * E].rearrange("p (k e) -> p k e", k=KT), 2.0,
                                 self.g_raw[:, :, :], ALU.mult, ALU.add).then_inc(self.gate_steps.sem, 1)
        dve.wait_ge(self.gate_steps.sem, self.gate_steps.at(0))
        dve.wait_ge(self.zeroed.sem, self.zeroed.at(1))
        dve.tensor_copy(self.g_hi[:, :, 0:E], self.g_full[:, :, :]).then_inc(self.gate_made.sem, 1)
        dve.wait_ge(self.gate_made.sem, self.gate_made.at(0))
        dve.tensor_tensor(self.g_lo[:, :, 0:E], self.g_full[:, :, :], f32(self.g_hi[:, :, 0:E]),
                          ALU.subtract).then_inc(self.gate_made.sem, 1)
        dve.wait_ge(self.numbered.sem, self.numbered.at(0))
        dve.tensor_copy(self.number[:, :], self.number_i[:, :]).then_inc(self.gate_steps.sem, 1)
        dve.wait_ge(self.gate_steps.sem, self.gate_steps.at(1))

    def tensor_logits(self, pe, norm, b):
        pe.wait_ge(self.gate_made.sem, self.gate_made.at(1))
        pe.wait_ge(norm.lo_made.sem, norm.lo_made.at(KT - 1, b))
        cols = slice(b * S, (b + 1) * S)
        for k in range(KT):
            ins = three_pass(pe, self.bank[:, :], self.g_hi[:, k, :], self.g_lo[:, k, :],
                             self.K.xt_hi[:, k, cols], self.K.xt_lo[:, k, cols], k == 0, k == KT - 1)
        ins.then_inc(self.logits_made.sem, 1)

    def scalar_logits(self, act, b):
        act.wait_ge(self.logits_made.sem, self.logits_made.at(b))
        act.activation(self.flat[:, :], self.bank[0:E, :], ACT.Copy).then_inc(self.logits_read.sem, 1)

    def tensor_turn(self, pe, b):
        pe.wait_ge(self.logits_read.sem, self.logits_read.at(b))
        for t in range(TT):
            ins = pe.transpose(self.bank[:, t * E:(t + 1) * E], self.flat[:, t * P:(t + 1) * P],
                               self.K.ident[0:E, 0:E])
        ins.then_inc(self.turned.sem, 1)

    def scalar_exp(self, act, b):
        act.wait_ge(self.shifted.sem, self.shifted.at(b))
        act.activation(self.prob[:, :, :], self.logit[:, :, :], ACT.Exp).then_inc(self.exp_made.sem, 1)

    def vector_route(self, dve, b):
        step = Count(self.steps, b)
        logit, prob, mask, other = (t[:, :, :] for t in (self.logit, self.prob, self.mask, self.other))
        most, total, inv = (t[:, :] for t in (self.most, self.total, self.inv))
        top, place = self.top[:, :, :], self.place[:, :, :]

        def over(ap):
            return ap.to_broadcast([P, TT, E])

        dve.wait_ge(self.turned.sem, self.turned.at(b))
        dve.tensor_copy(logit, self.bank[:, 0:TT * E].rearrange("p (t e) -> p t e",
                                                                t=TT)).then_inc(self.turned_read.sem, 1)
        dve.wait_ge(self.turned_read.sem, self.turned_read.at(b))
        dve.tensor_reduce(most, logit, AX.X, ALU.max).then_inc(step.sem, 1)
        dve.wait_ge(step.sem, step.next())
        dve.tensor_tensor(logit, logit, over(most.unsqueeze(2)), ALU.subtract).then_inc(self.shifted.sem, 1)
        dve.wait_ge(self.exp_made.sem, self.exp_made.at(b))
        dve.tensor_reduce(total, prob, AX.X, ALU.add).then_inc(step.sem, 1)
        dve.wait_ge(step.sem, step.next())
        dve.reciprocal(inv, total).then_inc(step.sem, 1)
        dve.wait_ge(step.sem, step.next())
        dve.tensor_tensor(prob, prob, over(inv.unsqueeze(2)), ALU.mult).then_inc(step.sem, 1)
        dve.wait_ge(step.sem, step.next())
        for t in range(TT):
            ins = dve.max(self.top[:, t, :], self.prob[:, t, :])
        ins.then_inc(step.sem, 1)
        dve.wait_ge(step.sem, step.next())
        for t in range(TT):
            ins = dve.max_index(self.index[:, t, :], self.top[:, t, :], self.prob[:, t, :])
        ins.then_inc(step.sem, 1)
        dve.wait_ge(step.sem, step.next())
        dve.tensor_copy(place, self.index[:, :, 0:2]).then_inc(step.sem, 1)
        dve.wait_ge(step.sem, step.next())
        every = self.number[:, :].unsqueeze(1).to_broadcast([P, TT, E])
        dve.tensor_tensor(mask, every, over(place[:, :, 0:1]), ALU.is_equal)
        dve.tensor_tensor(other, every, over(place[:, :, 1:2]), ALU.is_equal).then_inc(step.sem, 1)
        dve.wait_ge(step.sem, step.next())
        dve.tensor_tensor(mask, mask, other, ALU.add).then_inc(step.sem, 1)
        dve.wait_ge(step.sem, step.next())
        dve.tensor_tensor(total, top[:, :, 0], top[:, :, 1], ALU.add).then_inc(step.sem, 1)
        dve.wait_ge(step.sem, step.next())
        dve.reciprocal(inv, total).then_inc(step.sem, 1)
        dve.wait_ge(step.sem, step.next())
        dve.tensor_scalar(inv, inv, self.K.gates[:, 3:4], None, ALU.mult).then_inc(step.sem, 1)
        dve.wait_ge(step.sem, step.next())
        dve.tensor_tensor(mask, mask, prob, ALU.mult).then_inc(step.sem, 1)
        dve.wait_ge(step.sem, step.next())
        dve.tensor_tensor(self.K.route[:, b * TT:(b + 1) * TT, :], mask, over(inv.unsqueeze(2)),
                          ALU.mult).then_inc(step.sem, 1)
        dve.wait_ge(step.sem, step.next())
        assert step.n == self.steps.per


def stage_experts(K, gate_t, gate_a, gate_b_t, gup, down, gup_a, gup_b_t, down_a, down_b_t, out):
    with ExitStack() as ctx:
        sb, ps = K.scope(ctx)
        IT = I // P
        NC = KT + IT
        LR = 3 * 32
        w_raw = sb("e_w_raw", [P, NC, D])
        la_raw, lb_raw = sb("la_raw", [LR, D + I]), sb("lb_raw", [LR, 2 * D])
        la, lb = sb("la", [LR, D + I], F32R), sb("lb", [LR, 2 * D], F32R)
        w_hi, w_lo = sb("e_w_hi", [P, 2, NC, D], F32R), sb("e_w_lo", [P, 2, NC, D], F32R)
        silu = sb("e_silu", [P, IT, S])
        h_full = sb("e_h", [P, IT, S])
        h_hi, h_lo = sb("e_h_hi", [P, IT, S], F32R), sb("e_h_lo", [P, IT, S], F32R)
        p_h = [ps(f"e_h{n}") for n in range(3)]
        p_d = ps("e_d")
        p_y = [ps(f"e_y{t}") for t in range(TT)]
        H_BANK = [0, 1, 2, 0]
        norm = Norm(K, sb, "m", [p_d], first_banks=p_y)
        router = Router(K, sb, p_d)

        raw_in = Signal(K, "e_weights_in", per=14, unit=16)
        zeroed = Signal(K, "e_zeroed")
        lora_hi = Signal(K, "e_lora_hi", per=2, credit=2)
        lora_lo = Signal(K, "e_lora_lo", per=2)
        delta_made = Signal(K, "e_delta", per=NC, credit=NC)
        merged = Signal(K, "e_merged", per=NC, credit=1)
        hi_made = Signal(K, "e_weights_hi", per=NC)
        lo_made = Signal(K, "e_weights_lo", per=NC, credit=1)
        h_made = Signal(K, "e_h_product", per=4 * B)
        silu_made = Signal(K, "e_silu_made", per=IT * B, credit=IT)
        h_full_made = Signal(K, "e_h_made", per=IT * B, credit=IT)
        h_hi_made = Signal(K, "e_h_hi_made", per=IT * B)
        h_lo_made = Signal(K, "e_h_lo_made", per=IT * B, credit=IT)
        y_made = Signal(K, "e_product", per=TT * B, credit=TT)
        y_added = Signal(K, "e_added", per=TT * B, credit=TT)
        stored = Signal(K, "result_stored", unit=16)
        block = ctx.enter_context(K.nc.Block())
        chunks_at = [[0, 1], [2, 3], [4, 5], []]

        def experts(eng, run):
            run(1, 1, True)
            with eng.Fori(1, E // 2 - 1) as i:
                for u in range(2):
                    run(i * 2 + u, u, True)
            run(E - 2, 0, True)
            run(E - 1, 1, False)

        def delta_bank(e, c):
            return p_h[c % len(p_h)] if isinstance(e, int) and e == 0 else p_d

        def lora_rows(c):
            return slice(c * P, (c + 1) * P), slice(0, D) if c < KT else slice(D, 2 * D)

        @block.sync
        def _(sp):
            def load(e):
                at = slice(e, e + 1) if isinstance(e, int) else bass.ds(e, 1)
                sp.dma_start(w_raw[:, 0:KT, :],
                             gup[at].rearrange("a (k p) n -> p (a k) n", p=P)).then_inc(raw_in.sem, 16)
                sp.dma_start(w_raw[:, KT:NC, :],
                             down[at].rearrange("a (k p) n -> p (a k) n", p=P)).then_inc(raw_in.sem, 16)
                if isinstance(e, int):
                    sp.wait_ge(zeroed.sem, zeroed.at(1))
                for s in range(3):
                    rows = slice(32 * s, 32 * s + R)
                    for dst, src in ((la_raw[rows, 0:D], gup_a), (la_raw[rows, D:D + I], down_a),
                                     (lb_raw[rows, 0:D], gup_b_t), (lb_raw[rows, D:2 * D], down_b_t)):
                        sp.dma_start(dst, src[at].rearrange("a r n -> (a r) n")).then_inc(raw_in.sem, 16)

            router.sync_loads(sp, gate_t, gate_a, gate_b_t)
            load(0)
            with sp.Fori(1, E) as e:
                sp.wait_ge(lo_made.sem, lo_made.at(-1, e))
                sp.sem_inc(K.apart, 1)
                sp.wait_ge(delta_made.sem, delta_made.at(-1, e))
                sp.sem_inc(K.apart, 1)
                load(e)

            for b in range(B):
                sp.wait_ge(y_added.sem, y_added.at(TT * (b + 1) - 1, E - 1))
                sp.dma_start(out[b * S:(b + 1) * S, :].rearrange("(t p) d -> p t d", p=P),
                             K.x[:, b * TT:(b + 1) * TT, :]).then_inc(stored.sem, 16)
            sp.wait_ge(stored.sem, stored.at(B - 1))

        @block.gpsimd
        def _(pool):
            pool.memset(la_raw[:, :], 0.0).then_inc(zeroed.sem, 1)
            pool.memset(lb_raw[:, :], 0.0).then_inc(zeroed.sem, 1)
            router.pool_constants(pool)
            for b in range(B):
                norm.pool_rstd(pool, b)

        @block.scalar
        def _(act):
            act.sem_inc(silu_made.sem, silu_made.opening)
            act.sem_inc(lora_hi.sem, lora_hi.opening)

            def lora(e):
                act.wait_ge(raw_in.sem, raw_in.at(raw_in.per - 1, e))
                act.wait_ge(delta_made.sem, delta_made.at(-1, e))
                act.activation(la[:, :], la_raw[:, :], ACT.Copy).then_inc(lora_hi.sem, 1)
                act.activation(lb[:, :], lb_raw[:, :], ACT.Copy).then_inc(lora_hi.sem, 1)

            def chunk(e, u, c):
                act.wait_ge(merged.sem, merged.at(c, e))
                act.activation(w_hi[:, u, c, :], w_raw[:, c, :], ACT.Copy).then_inc(hi_made.sem, 1)

            def silu_of(e, b, n):
                act.wait_ge(h_made.sem, h_made.at(4 * b + 2 * n, e))
                act.wait_ge(h_full_made.sem, h_full_made.at(IT * (b - 1) + n, e))
                act.activation(silu[:, n, :], p_h[H_BANK[2 * n]][:, :], ACT.Silu).then_inc(silu_made.sem, 1)

            def split_h(e, b, n):
                act.wait_ge(h_full_made.sem, h_full_made.at(IT * b + n, e))
                if n == 0:
                    act.wait_ge(y_made.sem, y_made.at(TT * b - 1, e))
                act.activation(h_hi[:, n, :], h_full[:, n, :], ACT.Copy).then_inc(h_hi_made.sem, 1)

            def run_first():
                for b in range(B - 1):
                    silu_of(0, b, 0)
                    norm.scalar_hi(act, b + 1, b + 1, 0)
                    split_h(0, b, 0)
                    norm.scalar_hi(act, b + 1, b + 1, 1)
                    silu_of(0, b, 1)
                    norm.scalar_hi(act, b + 1, b + 1, 2)
                    split_h(0, b, 1)
                    norm.scalar_hi(act, b + 1, b + 1, 3)
                    router.scalar_logits(act, b + 1)
                    router.scalar_exp(act, b + 1)
                lora(1)
                silu_of(0, B - 1, 0)
                chunk(1, 1, 0)
                split_h(0, B - 1, 0)
                chunk(1, 1, 1)
                silu_of(0, B - 1, 1)
                chunk(1, 1, 2)
                split_h(0, B - 1, 1)
                for c in range(3, NC):
                    chunk(1, 1, c)

            def run(e, u, more):
                for b in range(B):
                    if more and b == 0:
                        lora(e + 1)
                    for n in range(IT):
                        silu_of(e, b, n)
                        split_h(e, b, n)
                    if more:
                        for c in chunks_at[b]:
                            chunk(e + 1, 1 - u, c)

            for k in range(KT):
                norm.scalar_hi(act, 0, 0, k)
            lora(0)
            router.scalar_logits(act, 0)
            for c in range(NC):
                chunk(0, 0, c)
            router.scalar_exp(act, 0)
            run_first()
            experts(act, run)

        @block.vector
        def _(dve):
            for s in (merged, lo_made, h_full_made, h_lo_made, y_added):
                dve.sem_inc(s.sem, s.opening)

            def lora(e):
                dve.wait_ge(lora_hi.sem, lora_hi.at(1, e))
                rows = slice(64, 64 + 32)
                dve.tensor_tensor(la[rows, :], la_raw[rows, :], f32(la[rows, :]),
                                  ALU.subtract).then_inc(lora_lo.sem, 1)
                rows = slice(32, 32 + 32)
                dve.tensor_tensor(lb[rows, :], lb_raw[rows, :], f32(lb[rows, :]),
                                  ALU.subtract).then_inc(lora_lo.sem, 1)

            def merge(e, c):
                dve.wait_ge(delta_made.sem, delta_made.at(c, e))
                dve.scalar_tensor_tensor(w_raw[:, c, :], delta_bank(e, c)[:, :], 2.0, w_raw[:, c, :],
                                         ALU.mult, ALU.add).then_inc(merged.sem, 1)

            def split(e, u, c):
                dve.wait_ge(hi_made.sem, hi_made.at(c, e))
                dve.tensor_tensor(w_lo[:, u, c, :], w_raw[:, c, :], f32(w_hi[:, u, c, :]),
                                  ALU.subtract).then_inc(lo_made.sem, 1)

            def gated(e, b, n):
                dve.wait_ge(h_made.sem, h_made.at(4 * b + 2 * n + 1, e))
                dve.wait_ge(silu_made.sem, silu_made.at(IT * b + n, e))
                dve.tensor_tensor(h_full[:, n, :], p_h[H_BANK[2 * n + 1]][:, :], silu[:, n, :],
                                  ALU.mult).then_inc(h_full_made.sem, 1)

            def split_h(e, b, n):
                dve.wait_ge(h_hi_made.sem, h_hi_made.at(IT * b + n, e))
                dve.tensor_tensor(h_lo[:, n, :], h_full[:, n, :], f32(h_hi[:, n, :]),
                                  ALU.subtract).then_inc(h_lo_made.sem, 1)

            def add(e, b, t):
                dve.wait_ge(y_made.sem, y_made.at(TT * b + t, e))
                route = K.route[:, b * TT + t, bass.ds(e, 1) if not isinstance(e, int) else slice(e, e + 1)]
                dve.scalar_tensor_tensor(K.x[:, b * TT + t, :], p_y[t][:, :], route, K.x[:, b * TT + t, :],
                                         ALU.mult, ALU.add).then_inc(y_added.sem, 1)

            def run_first():
                for b in range(B - 1):
                    norm.vector_lo(dve, b + 1, b + 1, 0)
                    gated(0, b, 0)
                    norm.vector_lo(dve, b + 1, b + 1, 1)
                    split_h(0, b, 0)
                    norm.vector_lo(dve, b + 1, b + 1, 2)
                    gated(0, b, 1)
                    norm.vector_lo(dve, b + 1, b + 1, 3)
                    split_h(0, b, 1)
                    if b + 2 < B:
                        norm.vector_stats(dve, b + 2, b + 2)
                    add(0, b, 0)
                    add(0, b, 1)
                    if b + 2 < B:
                        norm.vector_scale(dve, b + 2, b + 2)
                    add(0, b, 2)
                    add(0, b, 3)
                    router.vector_route(dve, b + 1)
                lora(1)
                merge(1, 0)
                gated(0, B - 1, 0)
                merge(1, 1)
                split_h(0, B - 1, 0)
                split(1, 1, 0)
                merge(1, 2)
                gated(0, B - 1, 1)
                split(1, 1, 1)
                merge(1, 3)
                split_h(0, B - 1, 1)
                split(1, 1, 2)
                merge(1, 4)
                split(1, 1, 3)
                for t in range(TT):
                    add(0, B - 1, t)
                merge(1, 5)
                split(1, 1, 4)
                split(1, 1, 5)

            def run(e, u, more):
                for b in range(B):
                    if more and b == 0:
                        lora(e + 1)
                    chunks = chunks_at[b] if more else []
                    for n in range(IT):
                        gated(e, b, n)
                        if n < len(chunks):
                            merge(e + 1, chunks[n])
                        split_h(e, b, n)
                    for t in range(TT):
                        add(e, b, t)
                        if t < len(chunks):
                            split(e + 1, 1 - u, chunks[t])

            dve.sem_inc(norm.normed.sem, norm.normed.opening)
            dve.sem_inc(norm.lo_made.sem, norm.lo_made.opening)
            norm.vector_stats(dve, 0, 0)
            router.vector_gate(dve)
            norm.vector_scale(dve, 0, 0)
            norm.vector_stats(dve, 1, 1)
            for k in range(KT):
                norm.vector_lo(dve, 0, 0, k)
            norm.vector_scale(dve, 1, 1)
            lora(0)
            for c in range(NC):
                merge(0, c)
                if c:
                    split(0, 0, c - 1)
            split(0, 0, NC - 1)
            router.vector_route(dve, 0)
            run_first()
            experts(dve, run)

        @block.tensor
        def _(pe):
            pe.sem_inc(delta_made.sem, delta_made.opening)
            pe.sem_inc(y_made.sem, y_made.opening)

            def delta(e, c):
                if c == 0:
                    pe.wait_ge(lora_lo.sem, lora_lo.at(1, e))
                if not (isinstance(e, int) and e == 0):
                    pe.wait_ge(merged.sem, merged.at(c - 1, e))
                elif c >= len(p_h):
                    pe.wait_ge(merged.sem, merged.at(c - len(p_h)))
                rows, cols = lora_rows(c)
                pe.matmul(delta_bank(e, c)[:, :], la[:, rows], lb[:, cols], start=True,
                          stop=True).then_inc(delta_made.sem, 1)

            def hidden(e, u, b, n, half):
                m = 2 * n + half
                if m == 0:
                    pe.wait_ge(h_full_made.sem, h_full_made.at(IT * b - 1, e))
                elif m == 3:
                    pe.wait_ge(silu_made.sem, silu_made.at(IT * b, e))
                elif m == 1:
                    pe.wait_ge(h_full_made.sem, h_full_made.at(IT * (b - 1), e))
                else:
                    pe.wait_ge(silu_made.sem, silu_made.at(IT * (b - 1) + 1, e))
                rows = slice(half * I + n * P, half * I + (n + 1) * P)
                cols = slice(b * S, (b + 1) * S)
                for k in range(KT):
                    ins = three_pass(pe, p_h[H_BANK[m]][:, :], w_hi[:, u, k, rows], w_lo[:, u, k, rows],
                                     K.xt_hi[:, k, cols], K.xt_lo[:, k, cols], k == 0, k == KT - 1)
                ins.then_inc(h_made.sem, 1)

            def output(e, u, b, n):
                pe.wait_ge(h_lo_made.sem, h_lo_made.at(IT * b + n, e))
                for t in range(TT):
                    if n == 0:
                        pe.wait_ge(y_added.sem, y_added.at(TT * (b - 1) + t, e))
                    rows = slice(t * P, (t + 1) * P)
                    ins = three_pass(pe, p_y[t][:, :], h_hi[:, n, rows], h_lo[:, n, rows],
                                     w_hi[:, u, KT + n, :], w_lo[:, u, KT + n, :], n == 0, n == IT - 1)
                    if n == IT - 1:
                        ins.then_inc(y_made.sem, 1)

            def run_first():
                for b in range(B - 1):
                    for n in range(IT):
                        for half in range(2):
                            hidden(0, 0, b, n, half)
                            if n + half == 0:
                                pe.wait_ge(router.turned_read.sem, router.turned_read.at(b))
                            norm.tensor_turn(pe, b + 1, 2 * n + half)
                    if b == 0:
                        pe.wait_ge(lo_made.sem, lo_made.at(NC - 1))
                    output(0, 0, b, 0)
                    router.tensor_logits(pe, norm, b + 1)
                    output(0, 0, b, 1)
                    router.tensor_turn(pe, b + 1)
                for n in range(IT):
                    for half in range(2):
                        hidden(0, 0, B - 1, n, half)
                        if n + half == 0:
                            pe.wait_ge(router.turned_read.sem, router.turned_read.at(B - 1))
                        delta(1, 2 * n + half)
                output(0, 0, B - 1, 0)
                delta(1, 4)
                output(0, 0, B - 1, 1)
                delta(1, 5)

            def run(e, u, more):
                pe.wait_ge(lo_made.sem, lo_made.at(NC - 1, e))
                for b in range(B):
                    chunks = chunks_at[b] if more else []
                    for n in range(IT):
                        for half in range(2):
                            hidden(e, u, b, n, half)
                        if n < len(chunks):
                            delta(e + 1, chunks[n])
                    for n in range(IT):
                        output(e, u, b, n)

            pe.sem_inc(norm.turned.sem, norm.turned.opening)
            router.tensor_gate(pe)
            pe.wait_ge(router.gate_steps.sem, router.gate_steps.at(0))
            for k in range(KT):
                norm.tensor_turn(pe, 0, k)
            router.tensor_logits(pe, norm, 0)
            for c in range(NC):
                delta(0, c)
            pe.wait_ge(merged.sem, merged.at(NC - 1))
            router.tensor_turn(pe, 0)
            pe.wait_ge(lo_made.sem, lo_made.at(KT - 1))
            run_first()
            experts(pe, run)


def flamingo_kernel(nc, a, out):
    keys = nc.dram_tensor("keys_split", (B, P, 2, G, S), F32, kind="Internal").ap()
    values = nc.dram_tensor("values_split", (B, P, TT, 2, G * DH), F32, kind="Internal").ap()
    with ExitStack() as ctx:
        K = Kernel(nc, ctx)
        sb, _ = K.scope(ctx)
        K.x = sb("x", [P, T, D])
        K.ident = sb("ident", [P, P])
        K.power = sb("power", [P, 16])
        K.gates_raw, K.gates = sb("gates_raw", [P, 4]), sb("gates", [P, 4])
        K.ln_eps = sb("ln_eps", [P, TT])
        K.gates_made = Signal(K, "gates_made")
        K.apart = ctx.enter_context(nc.semaphore("wait_stands_alone"))
        K.xt_hi, K.xt_lo = sb("xt_hi", [P, KT, B * S], F32R), sb("xt_lo", [P, KT, B * S], F32R)
        K.w1_in = [Signal(K, f"f_weight0_in{n}", unit=16) for n in range(2)]
        K.wq_in = Signal(K, "a_weights_in", per=2, unit=16)
        with ExitStack() as scope:
            K.wq_raw = K.scope(scope)[0]("a_w_raw", [P, KT, HG * DH])
            with ExitStack() as early:
                K.w_early = [K.wq_raw, K.scope(early)[0]("f_early", [P, KT, F // KT])]
                stage_context(K, a["x"], a["ctx_t"], a["L1_xattn_Wk"], a["L1_xattn_Wv"],
                              a["L1_xattn_k_norm_w"], a["g_xattn"], a["g_ffn"], a["w1_t"], keys, values)
                stage_ffn(K, a["w1_t"], a["w2_t"], a["b1_t"], a["L0_ffn_b2"], a["L1_xattn_Wq"])
            stage_attention(K, a["L1_xattn_Wq"], a["L1_xattn_Wo"], a["L1_xattn_q_norm_w"], keys, values)
        K.route = sb("route", [P, T, E])
        stage_experts(K, a["gate_t"], a["L1_ffn_gate_lora_A"], a["gate_b_t"],
                      a["L1_ffn_gate_up_proj"], a["L1_ffn_down_proj"], a["L1_ffn_gup_lora_A"],
                      a["gup_b_t"], a["L1_ffn_down_lora_A"], a["down_b_t"], out)


def kernel(**inputs):
    import numpy as np
    import concourse.bacc as bacc
    from concourse.bass_utils import run_bass_kernel_spmd

    given = {k: np.asarray(v) for k, v in inputs.items()}
    turned = {
        "x": given["x"].reshape(B * S, D),
        "ctx_t": given["ctx_2048"].transpose(0, 2, 1),
        "w1_t": given["L0_ffn_w1"].T,
        "w2_t": given["L0_ffn_w2"].T,
        "b1_t": given["L0_ffn_b1"].reshape(FT, P).T,
        "gate_t": given["L1_ffn_gate_weight"].T,
        "gate_b_t": given["L1_ffn_gate_lora_B"].T,
        "gup_b_t": given["L1_ffn_gup_lora_B"].transpose(0, 2, 1),
        "down_b_t": given["L1_ffn_down_lora_B"].transpose(0, 2, 1),
    }
    same = ["g_xattn", "g_ffn", "L0_ffn_b2", "L1_xattn_Wq", "L1_xattn_Wk", "L1_xattn_Wv",
            "L1_xattn_Wo", "L1_xattn_q_norm_w", "L1_xattn_k_norm_w", "L1_ffn_gate_lora_A",
            "L1_ffn_gate_up_proj", "L1_ffn_down_proj", "L1_ffn_gup_lora_A", "L1_ffn_down_lora_A"]
    nc = bacc.Bacc("TRN2", target_bir_lowering=False, num_devices=1)
    arrays, aps = {}, {}
    for name, a in [*turned.items(), *((n, given[n]) for n in same)]:
        arrays[f"in_{name}"] = np.ascontiguousarray(a)
        aps[name] = nc.dram_tensor(f"in_{name}", a.shape, mybir.dt.from_np(a.dtype), kind="ExternalInput").ap()
    out = nc.dram_tensor("out", (B * S, D), F32, kind="ExternalOutput").ap()
    flamingo_kernel(nc, aps, out)
    r = run_bass_kernel_spmd(nc, [arrays], core_ids=[0])
    return r.results[0]["out"].reshape(B, S, D)
```
